# Optimizing a Trainium2 kernel written in Bass

```python
import numpy as np
import jax
import jax.numpy as jnp

def _softmax(x, axis=-1):
    return jax.nn.softmax(x, axis=axis)

def _gelu(x):
    return jax.nn.gelu(x, approximate=True)

def _silu(x):
    return jax.nn.silu(x)

def _sigmoid(x):
    return jax.nn.sigmoid(x)

def _layernorm(x, axis=-1, eps=1e-05):
    m = jnp.mean(x, axis=axis, keepdims=True)
    v = jnp.var(x, axis=axis, keepdims=True)
    return (x - m) / jnp.sqrt(v + eps)

def _scatter_add(tgt, idx, src, axis=0):
    return tgt.at[idx].add(src)

def _segment_sum(src, seg, n):
    return jax.ops.segment_sum(src, seg, n)
kernel_name = 'mk_seq_preln_d2_jaxref_r8_fd8429'

def setup_inputs(seed: int=0):
    np.random.seed(seed)
    _w = jnp.asarray

    def _L0_attn_setup():
        import jax, jax.numpy as jnp
        import numpy as np
        DIM = 256
        H = 16
        KV = 4
        G = H // KV
        CQ = 128
        QN, QR = (96, 32)
        CKV = 128
        KN, KR = (64, 64)
        VD = 32
        THETA = 10000.0

        def _t5_layer_norm(x, gamma, eps=1e-05):
            mu = jnp.mean(x, axis=-1, keepdims=True)
            var = jnp.var(x, axis=-1, keepdims=True)
            return (x - mu) * jax.lax.rsqrt(var + eps) * gamma

        def _rope(x):
            S, D = (x.shape[-2], x.shape[-1])
            inv_freq = 1.0 / THETA ** (jnp.arange(0, D, 2, dtype=jnp.float32) / D)
            ang = jnp.arange(S, dtype=jnp.float32)[:, None] * inv_freq
            cos = jnp.cos(ang).astype(x.dtype)
            sin = jnp.sin(ang).astype(x.dtype)
            xe, xo = (x[..., ::2], x[..., 1::2])
            re = xe * cos - xo * sin
            ro = xe * sin + xo * cos
            return jnp.stack((re, ro), axis=-1).reshape(x.shape)
        key = jax.random.key(seed)
        ks = jax.random.split(key, 7)
        s = 0.02
        return {'x': jax.random.normal(ks[0], (2, 256, DIM), dtype=jnp.float32), 'w_dq': jax.random.normal(ks[1], (DIM, CQ), dtype=jnp.float32) * s, 'gamma_q': jnp.ones((CQ,), dtype=jnp.float32), 'w_uq': jax.random.normal(ks[2], (CQ, H * (QN + QR)), dtype=jnp.float32) * s, 'w_dkv': jax.random.normal(ks[3], (DIM, CKV + KR), dtype=jnp.float32) * s, 'gamma_kv': jnp.ones((CKV,), dtype=jnp.float32), 'w_ukv': jax.random.normal(ks[4], (CKV, KV * (KN + VD)), dtype=jnp.float32) * s, 'w_o': jax.random.normal(ks[5], (H * VD, DIM), dtype=jnp.float32) * s}
    _L0_attn_in = _L0_attn_setup()

    def _L0_ffn_setup():
        import jax, jax.numpy as jnp
        import numpy as np

        def _sparsify_2to4(h):
            B, S, I = h.shape
            g = h.reshape(B, S, I // 4, 4)
            a = jnp.abs(g)
            _, idx = jax.lax.top_k(a, 2)
            pos = jnp.arange(4)
            mask = (pos == idx[..., 0:1]) | (pos == idx[..., 1:2])
            return (g * mask.astype(g.dtype)).reshape(B, S, I)
        key = jax.random.key(seed)
        k1, k2, k3, k4 = jax.random.split(key, 4)
        B, S, H, I = (4, 256, 256, 1024)
        x = jax.random.normal(k1, (B, S, H), dtype=jnp.float32)
        w_gate = jax.random.normal(k2, (H, I), dtype=jnp.float32) / np.sqrt(H)
        w_up = jax.random.normal(k3, (H, I), dtype=jnp.float32) / np.sqrt(H)
        w_down = jax.random.normal(k4, (I, H), dtype=jnp.float32) / np.sqrt(I)
        return {'x': x, 'w_gate': w_gate, 'w_up': w_up, 'w_down': w_down}
    _L0_ffn_in = _L0_ffn_setup()

    def _L1_attn_setup():
        import jax, jax.numpy as jnp
        import numpy as np
        D_MODEL = 256
        NUM_HEADS = 16
        HEAD_DIM = D_MODEL // NUM_HEADS
        WINDOW = 64
        SINKS = 4
        BATCH = 2
        SEQ = 256

        def _sliding_window_banned(q_len, kv_len):
            i = jnp.arange(q_len)[:, None]
            j = jnp.arange(kv_len)[None, :]
            pos = kv_len - q_len + i
            return (j >= SINKS) & (j < pos - WINDOW)
        key = jax.random.key(seed)
        ks = jax.random.split(key, 9)
        s = 0.02
        return {'hidden_states': jax.random.normal(ks[0], (BATCH, SEQ, D_MODEL), jnp.float32), 'Wq': jax.random.normal(ks[1], (D_MODEL, D_MODEL), jnp.float32) * s, 'bq': jax.random.normal(ks[2], (D_MODEL,), jnp.float32) * s, 'Wk': jax.random.normal(ks[3], (D_MODEL, D_MODEL), jnp.float32) * s, 'bk': jax.random.normal(ks[4], (D_MODEL,), jnp.float32) * s, 'Wv': jax.random.normal(ks[5], (D_MODEL, D_MODEL), jnp.float32) * s, 'bv': jax.random.normal(ks[6], (D_MODEL,), jnp.float32) * s, 'Wo': jax.random.normal(ks[7], (D_MODEL, D_MODEL), jnp.float32) * s, 'bo': jax.random.normal(ks[8], (D_MODEL,), jnp.float32) * s}
    _L1_attn_in = _L1_attn_setup()

    def _L1_ffn_setup():
        import jax, jax.numpy as jnp
        import numpy as np
        from jax import lax
        DIM = 256
        INTER = 176
        N_EXPERTS = 32
        TOP_K = 6
        N_SHARED = 2
        CAPACITY = 256
        ROUTE_SCALE = 1.0

        def _gate(xf, gate_w):
            logits = xf @ gate_w.T
            scores = jax.nn.softmax(logits.astype(jnp.float32), axis=-1)
            top_w, top_i = lax.top_k(scores, TOP_K)
            return ((top_w * ROUTE_SCALE).astype(xf.dtype), top_i)

        def _moe(xf, gate_w, w1, w2, w3):
            T, D = xf.shape
            E, CAP = (N_EXPERTS, CAPACITY)
            top_w, top_i = _gate(xf, gate_w)
            e_flat = top_i.reshape(-1)
            t_flat = jnp.repeat(jnp.arange(T), TOP_K)
            w_flat = top_w.reshape(-1)
            order = jnp.argsort(e_flat)
            e_s, t_s, w_s = (e_flat[order], t_flat[order], w_flat[order])
            counts = jnp.zeros((E,), jnp.int32).at[e_s].add(1)
            starts = jnp.concatenate([jnp.zeros((1,), jnp.int32), jnp.cumsum(counts)[:-1]])
            pos = jnp.arange(T * TOP_K, dtype=jnp.int32) - starts[e_s]
            valid = pos < CAP
            buf_idx = jnp.where(valid, e_s * CAP + pos, E * CAP)
            xbuf = jnp.zeros((E * CAP + 1, D), xf.dtype).at[buf_idx].set(xf[t_s])
            xb = xbuf[:E * CAP].reshape(E, CAP, D)
            h = jax.nn.silu(jnp.einsum('ecd,edi->eci', xb, w1)) * jnp.einsum('ecd,edi->eci', xb, w3)
            ob = jnp.einsum('eci,eid->ecd', h, w2).reshape(E * CAP, D)
            ob = jnp.concatenate([ob, jnp.zeros((1, D), ob.dtype)], axis=0)
            y_pairs = ob[buf_idx] * w_s[:, None]
            y = jnp.zeros((T, D), xf.dtype).at[t_s].add(y_pairs)
            return y
        key = jax.random.key(seed)
        ks = jax.random.split(key, 9)
        B, S = (4, 256)
        si = INTER * N_SHARED
        inputs = {'x': jax.random.normal(ks[0], (B, S, DIM), jnp.float32), 'gate_w': jax.random.normal(ks[1], (N_EXPERTS, DIM), jnp.float32), 'w1': jax.random.normal(ks[2], (N_EXPERTS, DIM, INTER), jnp.float32) * DIM ** (-0.5), 'w2': jax.random.normal(ks[3], (N_EXPERTS, INTER, DIM), jnp.float32) * INTER ** (-0.5), 'w3': jax.random.normal(ks[4], (N_EXPERTS, DIM, INTER), jnp.float32) * DIM ** (-0.5), 'sw1': jax.random.normal(ks[5], (DIM, si), jnp.float32) * DIM ** (-0.5), 'sw2': jax.random.normal(ks[6], (si, DIM), jnp.float32) * si ** (-0.5), 'sw3': jax.random.normal(ks[7], (DIM, si), jnp.float32) * DIM ** (-0.5)}
        return inputs
    _L1_ffn_in = _L1_ffn_setup()
    _d = {'L0_attn_x': _L0_attn_in['x'], 'L0_attn_w_dq': _L0_attn_in['w_dq'], 'L0_attn_gamma_q': _L0_attn_in['gamma_q'], 'L0_attn_w_uq': _L0_attn_in['w_uq'], 'L0_attn_w_dkv': _L0_attn_in['w_dkv'], 'L0_attn_gamma_kv': _L0_attn_in['gamma_kv'], 'L0_attn_w_ukv': _L0_attn_in['w_ukv'], 'L0_attn_w_o': _L0_attn_in['w_o'], 'L0_ffn_w_gate': _L0_ffn_in['w_gate'], 'L0_ffn_w_up': _L0_ffn_in['w_up'], 'L0_ffn_w_down': _L0_ffn_in['w_down'], 'L1_attn_Wq': _L1_attn_in['Wq'], 'L1_attn_bq': _L1_attn_in['bq'], 'L1_attn_Wk': _L1_attn_in['Wk'], 'L1_attn_bk': _L1_attn_in['bk'], 'L1_attn_Wv': _L1_attn_in['Wv'], 'L1_attn_bv': _L1_attn_in['bv'], 'L1_attn_Wo': _L1_attn_in['Wo'], 'L1_attn_bo': _L1_attn_in['bo'], 'L1_ffn_gate_w': _L1_ffn_in['gate_w'], 'L1_ffn_w1': _L1_ffn_in['w1'], 'L1_ffn_w2': _L1_ffn_in['w2'], 'L1_ffn_w3': _L1_ffn_in['w3'], 'L1_ffn_sw1': _L1_ffn_in['sw1'], 'L1_ffn_sw2': _L1_ffn_in['sw2'], 'L1_ffn_sw3': _L1_ffn_in['sw3']}
    _x0 = _d['L0_attn_x']
    _d['L0_attn_x'] = jax.random.normal(jax.random.fold_in(jax.random.key(seed), 1), (4, 512, 256), dtype=_x0.dtype)
    del _x0
    return _d

def reference(L0_attn_x, L0_attn_w_dq, L0_attn_gamma_q, L0_attn_w_uq, L0_attn_w_dkv, L0_attn_gamma_kv, L0_attn_w_ukv, L0_attn_w_o, L0_ffn_w_gate, L0_ffn_w_up, L0_ffn_w_down, L1_attn_Wq, L1_attn_bq, L1_attn_Wk, L1_attn_bk, L1_attn_Wv, L1_attn_bv, L1_attn_Wo, L1_attn_bo, L1_ffn_gate_w, L1_ffn_w1, L1_ffn_w2, L1_ffn_w3, L1_ffn_sw1, L1_ffn_sw2, L1_ffn_sw3):

    def _L0_attn_ref(x, w_dq, gamma_q, w_uq, w_dkv, gamma_kv, w_ukv, w_o):
        import jax, jax.numpy as jnp
        import numpy as np
        DIM = 256
        H = 16
        KV = 4
        G = H // KV
        CQ = 128
        QN, QR = (96, 32)
        CKV = 128
        KN, KR = (64, 64)
        VD = 32
        THETA = 10000.0

        def _t5_layer_norm(x, gamma, eps=1e-05):
            mu = jnp.mean(x, axis=-1, keepdims=True)
            var = jnp.var(x, axis=-1, keepdims=True)
            return (x - mu) * jax.lax.rsqrt(var + eps) * gamma

        def _rope(x):
            S, D = (x.shape[-2], x.shape[-1])
            inv_freq = 1.0 / THETA ** (jnp.arange(0, D, 2, dtype=jnp.float32) / D)
            ang = jnp.arange(S, dtype=jnp.float32)[:, None] * inv_freq
            cos = jnp.cos(ang).astype(x.dtype)
            sin = jnp.sin(ang).astype(x.dtype)
            xe, xo = (x[..., ::2], x[..., 1::2])
            re = xe * cos - xo * sin
            ro = xe * sin + xo * cos
            return jnp.stack((re, ro), axis=-1).reshape(x.shape)
        B, S, _ = x.shape
        cq = _t5_layer_norm(x @ w_dq, gamma_q)
        q = cq @ w_uq
        q_nope = q[..., :H * QN].reshape(B, S, H, QN).transpose(0, 2, 1, 3)
        q_rope = q[..., H * QN:].reshape(B, S, H, QR).transpose(0, 2, 1, 3)
        q_rope = _rope(q_rope)
        q_states = jnp.concatenate((q_nope, q_rope), axis=-1)
        ckv_kr = x @ w_dkv
        ckv = _t5_layer_norm(ckv_kr[..., :CKV], gamma_kv)
        k_rope = _rope(ckv_kr[..., CKV:][:, None, :, :])
        kv = ckv @ w_ukv
        k_nope = kv[..., :KV * KN].reshape(B, S, KV, KN).transpose(0, 2, 1, 3)
        v_states = kv[..., KV * KN:].reshape(B, S, KV, VD).transpose(0, 2, 1, 3)
        k_states = jnp.concatenate((k_nope, jnp.broadcast_to(k_rope, (B, KV, S, KR))), axis=-1)
        dqk = QN + QR
        qg = q_states.reshape(B, KV, G, S, dqk)
        scores = jnp.einsum('bgrqd,bgkd->bgrqk', qg, k_states) / jnp.sqrt(jnp.asarray(dqk, dtype=x.dtype))
        causal = jnp.triu(jnp.ones((S, S), dtype=bool), k=1)
        scores = jnp.where(causal, -jnp.inf, scores)
        attn = jax.nn.softmax(scores, axis=-1)
        out = jnp.einsum('bgrqk,bgkv->bgrqv', attn, v_states)
        out = out.reshape(B, H, S, VD).transpose(0, 2, 1, 3).reshape(B, S, H * VD)
        return out @ w_o

    def _L0_ffn_ref(x, w_gate, w_up, w_down):
        import jax, jax.numpy as jnp
        import numpy as np

        def _sparsify_2to4(h):
            B, S, I = h.shape
            g = h.reshape(B, S, I // 4, 4)
            a = jnp.abs(g)
            _, idx = jax.lax.top_k(a, 2)
            pos = jnp.arange(4)
            mask = (pos == idx[..., 0:1]) | (pos == idx[..., 1:2])
            return (g * mask.astype(g.dtype)).reshape(B, S, I)
        h = jax.nn.silu(jnp.einsum('bsh,hi->bsi', x, w_gate)) * jnp.einsum('bsh,hi->bsi', x, w_up)
        h_sparse = _sparsify_2to4(h)
        return jnp.einsum('bsi,ih->bsh', h_sparse, w_down)

    def _L1_attn_ref(hidden_states, Wq, bq, Wk, bk, Wv, bv, Wo, bo):
        import jax, jax.numpy as jnp
        import numpy as np
        D_MODEL = 256
        NUM_HEADS = 16
        HEAD_DIM = D_MODEL // NUM_HEADS
        WINDOW = 64
        SINKS = 4
        BATCH = 2
        SEQ = 256

        def _sliding_window_banned(q_len, kv_len):
            i = jnp.arange(q_len)[:, None]
            j = jnp.arange(kv_len)[None, :]
            pos = kv_len - q_len + i
            return (j >= SINKS) & (j < pos - WINDOW)
        b, s, _ = hidden_states.shape
        q = hidden_states @ Wq.T + bq
        k = hidden_states @ Wk.T + bk
        v = hidden_states @ Wv.T + bv
        q = q.reshape(b, s, NUM_HEADS, HEAD_DIM).transpose(0, 2, 1, 3)
        k = k.reshape(b, s, NUM_HEADS, HEAD_DIM).transpose(0, 2, 1, 3)
        v = v.reshape(b, s, NUM_HEADS, HEAD_DIM).transpose(0, 2, 1, 3)
        scale = HEAD_DIM ** (-0.5)
        scores = jnp.einsum('bhqd,bhkd->bhqk', q, k) * scale
        kv_len = k.shape[2]
        if kv_len > WINDOW + SINKS:
            banned = _sliding_window_banned(s, kv_len)
            scores = jnp.where(banned[None, None], -jnp.inf, scores)
        probs = jax.nn.softmax(scores, axis=-1)
        out = jnp.einsum('bhqk,bhkd->bhqd', probs, v)
        out = out.transpose(0, 2, 1, 3).reshape(b, s, D_MODEL)
        return out @ Wo.T + bo

    def _L1_ffn_ref(x, gate_w, w1, w2, w3, sw1, sw2, sw3):
        import jax, jax.numpy as jnp
        import numpy as np
        from jax import lax
        DIM = 256
        INTER = 176
        N_EXPERTS = 32
        TOP_K = 6
        N_SHARED = 2
        CAPACITY = 256
        ROUTE_SCALE = 1.0

        def _gate(xf, gate_w):
            logits = xf @ gate_w.T
            scores = jax.nn.softmax(logits.astype(jnp.float32), axis=-1)
            top_w, top_i = lax.top_k(scores, TOP_K)
            return ((top_w * ROUTE_SCALE).astype(xf.dtype), top_i)

        def _moe(xf, gate_w, w1, w2, w3):
            T, D = xf.shape
            E, CAP = (N_EXPERTS, CAPACITY)
            top_w, top_i = _gate(xf, gate_w)
            e_flat = top_i.reshape(-1)
            t_flat = jnp.repeat(jnp.arange(T), TOP_K)
            w_flat = top_w.reshape(-1)
            order = jnp.argsort(e_flat)
            e_s, t_s, w_s = (e_flat[order], t_flat[order], w_flat[order])
            counts = jnp.zeros((E,), jnp.int32).at[e_s].add(1)
            starts = jnp.concatenate([jnp.zeros((1,), jnp.int32), jnp.cumsum(counts)[:-1]])
            pos = jnp.arange(T * TOP_K, dtype=jnp.int32) - starts[e_s]
            valid = pos < CAP
            buf_idx = jnp.where(valid, e_s * CAP + pos, E * CAP)
            xbuf = jnp.zeros((E * CAP + 1, D), xf.dtype).at[buf_idx].set(xf[t_s])
            xb = xbuf[:E * CAP].reshape(E, CAP, D)
            h = jax.nn.silu(jnp.einsum('ecd,edi->eci', xb, w1)) * jnp.einsum('ecd,edi->eci', xb, w3)
            ob = jnp.einsum('eci,eid->ecd', h, w2).reshape(E * CAP, D)
            ob = jnp.concatenate([ob, jnp.zeros((1, D), ob.dtype)], axis=0)
            y_pairs = ob[buf_idx] * w_s[:, None]
            y = jnp.zeros((T, D), xf.dtype).at[t_s].add(y_pairs)
            return y
        shape = x.shape
        xf = x.reshape(-1, DIM)
        y = _moe(xf, gate_w, w1, w2, w3)
        shared = jax.nn.silu(xf @ sw1) * (xf @ sw3) @ sw2
        return (y + shared).reshape(shape)
    x = L0_attn_x
    x = x + _L0_attn_ref(_layernorm(x, axis=-1), L0_attn_w_dq, L0_attn_gamma_q, L0_attn_w_uq, L0_attn_w_dkv, L0_attn_gamma_kv, L0_attn_w_ukv, L0_attn_w_o)
    x = x + _L0_ffn_ref(_layernorm(x, axis=-1), L0_ffn_w_gate, L0_ffn_w_up, L0_ffn_w_down)
    x = x + _L1_attn_ref(_layernorm(x, axis=-1), L1_attn_Wq, L1_attn_bq, L1_attn_Wk, L1_attn_bk, L1_attn_Wv, L1_attn_bv, L1_attn_Wo, L1_attn_bo)
    x = x + _L1_ffn_ref(_layernorm(x, axis=-1), L1_ffn_gate_w, L1_ffn_w1, L1_ffn_w2, L1_ffn_w3, L1_ffn_sw1, L1_ffn_sw2, L1_ffn_sw3)
    return x

_drawn_inputs = setup_inputs


def setup_inputs(seed=0):
    import zlib

    import numpy as np

    out = dict(_drawn_inputs(seed))
    spreads = {'L0_attn_gamma_q': (1.0, 0.6), 'L0_attn_gamma_kv': (1.0, 0.564)}
    factors = {'L0_attn_w_dq': 4.336,
     'L0_attn_w_uq': 3.624,
     'L1_attn_Wq': 8.0,
     'L1_attn_bq': 8.0,
     'L1_attn_Wk': 7.329,
     'L1_attn_bk': 8.0}
    for name, (base, spread) in spreads.items():
        noise = np.random.default_rng([zlib.crc32(name.encode()), seed]).standard_normal(out[name].shape)
        drawn = base * np.exp(spread * noise) if base else spread * noise
        out[name] = jnp.asarray(drawn.astype(out[name].dtype))
    for name, factor in factors.items():
        out[name] = (out[name] * factor).astype(out[name].dtype)
    return out
```

```python
from contextlib import ExitStack

import concourse.bass as bass
from concourse import mybir

F32 = mybir.dt.float32
F32R = mybir.dt.float32r
BF16 = mybir.dt.bfloat16
I32 = mybir.dt.int32
U32 = mybir.dt.uint32
ALU = mybir.AluOpType
ACT = mybir.ActivationFunctionType
AX = mybir.AxisListType

P = 128
B, S, D = 4, 512, 256
T = B * S
NT = S // P
KD = D // P
EPS = 1e-5
H0, G0, QN, QR, KN, KR, VD0 = 16, 4, 96, 32, 64, 64, 32
CQ = 128
HG = H0 // G0
FF = 1024
PLANES, HALVES = 4, 2
H1, HD1, WINDOW, SINKS = 16, 16, 64, 4
QK_ROWS = 96
E, TOPK, INTER, CAP = 32, 6, 176, 256
IC = 88
NI = INTER // IC
SI = 2 * INTER
NSI = SI // IC
ROW = D + E
DUMMY = T
YROWS = T + P
UNITS = H0 * NT
LAG = 3


def dense_units():
    u = [(("xT", 1, k), "A") for k in range(KD)]
    u += [(("proj", t), "V") for t in range(NT)]
    u += [(("cT", c), "A") for c in range(2)]
    u += [(("kr", r), "V") for r in range(2)]
    u += [(("v0",), "A")]
    u += [(("kn", g), "A") for g in range(G0)]
    for g in range(G0):
        u += [(("qr", g, r), "V") for r in range(2)]
        u += [(("qn", g, j), "A") for j in range(HG)]
    u += [(("o0", t), "V") for t in range(NT)]
    u += [(("xT", 2, k), "A") for k in range(KD)]
    for hf in range(HALVES):
        for i in range(PLANES):
            u += [(("gate", i, hf), "A"), (("up", i, hf), "V")]
    u += [(("down", t), "V") for t in range(NT)]
    u += [(("xT", 3, k), "A") for k in range(KD)]
    u += [(("qk", c), "V") for c in range(4)]
    u += [(("v1", t), "V") for t in range(NT)]
    u += [(("o1", t), "V") for t in range(NT)]
    u += [(("xT", 4, k), "A") for k in range(KD)]
    u += [(("logit",), "A")]
    for c in range(NSI):
        u += [(("sg", c), "A"), (("su", c), "V")]
    u += [(("sdown", t), "V") for t in range(NT)]
    return u


class DenseRing:

    def __init__(self, banks, filled, freed):
        units = dense_units()
        self.banks, self.filled, self.freed = banks, filled, freed
        self.n = {name: i for i, (name, _) in enumerate(units)}
        self.by = [who for _, who in units]
        self.total = len(units)
        assert self.total % 2 == 0
        self.reads = {w: self.by.count(w) for w in "AV"}

    def bank(self, *name):
        return self.banks[self.n[name] % 2]

    def wait_free(self, pe, b, *name):
        n = self.n[name]
        m = (n - 2) % self.total
        who = self.by[m]
        k = self.by[:m + 1].count(who)
        base = (b + 1) if n >= 2 else b
        pe.wait_ge(self.freed[who], base * self.reads[who] + k)

    def wait_read(self, eng, b, *name):
        n = self.n[name]
        who = self.by[n]
        eng.wait_ge(self.freed[who], (b + 1) * self.reads[who] + self.by[:n + 1].count(who))

    def wait_filled(self, eng, b, *name):
        eng.wait_ge(self.filled, b * self.total + self.n[name] + 1)


class Chain:

    def __init__(self, eng, sem, b=0, per_pass=0):
        self.eng, self.sem, self.b, self.per_pass, self.n = eng, sem, b, per_pass, 0

    def link(self, ins):
        self.n += 1
        ins.then_inc(self.sem, 1)
        self.eng.wait_ge(self.sem, self.b * self.per_pass + self.n)

    def done(self):
        assert self.n == self.per_pass, (self.n, self.per_pass)


def build(nc, x, w_proj, w_kr, gamma_q, gamma_kv, w_qn, w_qr, w_uk, w_uv, w_o0, w_gate, w_up, w_down,
          w_q1, w_k1, w_v1, w_o1, b_q1, b_k1, b_v1, b_o1, gate_w, w1, w2, w3, sw1, sw2, sw3,
          cos_q, sin_q, cos_k, sin_k, ident, identb, causal, window, tri, small, out):
    x_rows = x.rearrange("(b t p) d -> b p t d", b=B, p=P)
    xn_rows = nc.dram_tensor("xn_rows", (T, ROW), F32).ap()
    slot_tokens = nc.dram_tensor("slot_tokens", (2, E * CAP), I32).ap()
    y_sum = [nc.dram_tensor(f"y_sum{i}", (YROWS, D), F32).ap() for i in range(4)]

    ctx = ExitStack()
    with ctx:
        def sb(name, shape, dt=F32, stack=None):
            return (stack or ctx).enter_context(nc.sbuf_tensor(name, shape, dt))

        def sem(name):
            return ctx.enter_context(nc.semaphore(name))

        banks = [ctx.enter_context(nc.psum_tensor(f"bank{i}", [P, 512], F32)) for i in range(8)]
        score_banks, turn_banks, out_bank, dense_banks = banks[0:3], banks[3:5], banks[5], banks[6:8]

        identity = sb("identity", [P, P])
        identity_bf = sb("identity_bf", [P, P], BF16)
        tri_sb = sb("tri_sb", [P, P], BF16)
        small_sb = sb("small_sb", [P, 96])
        logits = sb("logits", [P, B * NT, E])
        zeros = sb("zeros", [P, D])

        seq = ExitStack()
        wproj_sb = sb("wproj_sb", [P, KD, 2 * CQ], F32, seq)
        wkr_sb = sb("wkr_sb", [P, 2, KD, P], F32, seq)
        gam_sb = sb("gam_sb", [P, 2], F32, seq)
        wqn_sb = sb("wqn_sb", [P, H0, QN], F32, seq)
        wqr_sb = sb("wqr_sb", [P, 2, G0, P], F32, seq)
        wuk_sb = sb("wuk_sb", [P, G0, KN], F32, seq)
        wuv_sb = sb("wuv_sb", [P, G0 * VD0], F32, seq)
        wo0_sb = sb("wo0_sb", [P, G0, D], F32, seq)
        wgate_sb = sb("wgate_sb", [P, KD, FF], F32, seq)
        wup_sb = sb("wup_sb", [P, KD, FF], F32, seq)
        wdown_sb = sb("wdown_sb", [P, 8, D], F32, seq)
        wqk1_sb = sb("wqk1_sb", [P, 2, KD, D], F32, seq)
        bqk1_sb = sb("bqk1_sb", [P, 2, KD], F32, seq)
        wv1_sb = sb("wv1_sb", [P, KD, 512], F32, seq)
        wo1_sb = sb("wo1_sb", [P, 4, D], F32, seq)
        bv1_sb = sb("bv1_sb", [P, 512], F32, seq)
        bo1_sb = sb("bo1_sb", [P, D], F32, seq)
        gatew_sb = sb("gatew_sb", [P, KD, E], F32, seq)
        sw13_sb = sb("sw13_sb", [P, 2, KD, SI], F32, seq)
        sw2_sb = sb("sw2_sb", [IC, NSI, D], F32, seq)
        rope_q = sb("rope_q", [P, 2, S], F32, seq)
        rope_k = sb("rope_k", [P, 2, S], F32, seq)
        causal_sb = sb("causal_sb", [P, P], BF16, seq)
        window_sb = sb("window_sb", [P, S], BF16, seq)
        mhalf = sb("mhalf", [P, 8], F32, seq)

        xb = sb("xb", [P, NT, D], F32, seq)
        xnT = sb("xnT", [P, KD, S], F32, seq)
        probs = sb("probs", [P, 3, S], F32, seq)
        probs_n = sb("probs_n", [P, 3, S], F32, seq)
        xn = probs[:, 0:2, :].rearrange("p a (c n) -> p (a c) n", c=2)
        cn = probs_n[:, 0:2, :].rearrange("p a (c n) -> p (a c) n", c=2)
        probsT = sb("probsT", [P, HG, NT, S], F32, seq)
        attnT = sb("attnT", [P, G0, S], F32, seq)
        stats = sb("stats", [P, 2 * NT, 6], F32, seq)
        mv = sb("mv", [P, 2 * NT, 2], F32, seq)
        vare = sb("vare", [P, 2 * NT], F32, seq)
        rstd = sb("rstd", [P, 2 * NT], F32, seq)
        nmax = sb("nmax", [P, 4], F32, seq)
        den = sb("den", [P, 4], F32, seq)
        rden = sb("rden", [P, 4], F32, seq)

        l0 = ExitStack()
        cT = sb("cT", [P, 2, S], F32, l0)
        qT = sb("qT", [P, 2, HG, S], F32, l0)
        kT = sb("kT", [P, G0, S], F32, l0)
        v0 = sb("v0_sb", [P, NT, G0 * VD0], F32, l0)
        rp = sb("rp", [P, 3, S], F32, l0)
        l0.close()
        ff = ExitStack()
        sg = sb("sg", [P, 2, S], F32, ff)
        hp = sb("hp", [P, PLANES, S], F32, ff)
        ha = sb("ha", [P, PLANES, S], F32, ff)
        wins = sb("wins", [P, 6, S], BF16, ff)
        wsum = sb("wsum", [P, 4, S], BF16, ff)
        hT = sb("hT", [P, 2 * PLANES, S], F32, ff)
        ff.close()
        l1 = ExitStack()
        qk32 = sb("qk32", [P, 2, S], F32, l1)
        qk_hi = sb("qk_hi", [P, 4, S], F32R, l1)
        qk_lo = sb("qk_lo", [P, 4, S], F32R, l1)
        q_st = sb("q_st", [QK_ROWS, 2, HG, S], F32R, l1)
        k_st = sb("k_st", [QK_ROWS, 2, HG, S], F32R, l1)
        v1 = sb("v1_sb", [P, NT, H1 * 32], F32, l1)
        l1.close()
        sh = ExitStack()
        ssg = sb("ssg", [IC, 2, S], F32, sh)
        shT = sb("shT", [IC, NSI, S], F32, sh)
        sh.close()
        seq.close()

        moe = ExitStack()
        sc = sb("sc", [P, B * NT, E], F32, moe)
        rsum = sb("rsum", [P, B * NT], F32, moe)
        rrec = sb("rrec", [P, B * NT], F32, moe)
        top = sb("top", [P, B * NT, 8], F32, moe)
        topi = sb("topi", [P, B * NT, 8], U32, moe)
        topf = sb("topf", [P, B * NT, 8], F32, moe)
        hit = sb("hit", [P, 2, B * NT, E], F32, moe)
        mask_b = sb("mask_b", [P, B * NT, E], BF16, moe)
        ones_b = sb("ones_b", [P, P], BF16, moe)
        posi = sb("posi", [P, 3, B * NT, E], I32, moe)
        posf = sb("posf", [P, 2, B * NT, E], F32, moe)
        onehot_a = sb("onehot_a", [P, B * NT, E * 16], BF16, moe)
        onehot_b = sb("onehot_b", [P, B * NT, E * 16], BF16, moe)
        val_b = sb("val_b", [P, 2, B * NT, E * 16], BF16, moe)
        blockm = sb("blockm", [P, 8], F32, moe)
        tabm = sb("tabm", [P, 4, 256], F32, moe)
        tab = sb("tab", [P, 4, 2, 16], F32, moe)
        tabs = sb("tabs", [P, 4, 3, 16], F32, moe)
        tab_i = sb("tab_i", [P, 2, 4, 16], I32, moe)
        slots = sb("slots", [P, 2, E * 2], I32, moe)
        slot_now = sb("slot_now", [P, 2, 2, 2], I32, moe)
        w13_sb = sb("w13_sb", [P, 2, 2, KD, INTER], F32, moe)
        w2_sb = sb("w2_sb", [IC, 2, NI, D], F32, moe)
        xg = sb("xg", [P, 2, 2, ROW], F32, moe)
        xgT = sb("xgT", [P, 2, KD, CAP], F32, moe)
        eg = sb("eg", [IC, 2, NI, CAP], F32, moe)
        eh = sb("eh", [IC, 2, NI, CAP], F32, moe)
        yo = sb("yo", [P, 2, 2, D], F32, moe)
        fin = sb("fin", [P, 2, 4, 4, D], F32, moe)
        moe.close()

        weights_in = sem("weights_in")
        x_in = sem("x_in")
        dense_filled = sem("dense_filled")
        freed_act = sem("dense_freed_act")
        freed_dve = sem("dense_freed_dve")
        consts_made = sem("consts_made")
        xn_ready = sem("xn_ready")
        var_ready = sem("var_ready")
        rstd_ready = sem("rstd_ready")
        kr_ready = sem("kr_ready")
        kr_copied = sem("kr_copied")
        rope_ready = sem("rope_ready")
        rope_moved = sem("rope_moved")
        scores_ready = sem("scores_ready")
        max_ready = sem("max_ready")
        probs_ready = sem("probs_ready")
        rden_ready = sem("rden_ready")
        probs_normed = sem("probs_normed")
        turned = sem("turned")
        turn_read_dve = sem("turn_read_dve")
        turn_read_act = sem("turn_read_act")
        heads_out = sem("heads_out")
        attn_ready = sem("attn_ready")
        res_ready = sem("res_ready")
        abs_ready = sem("abs_ready")
        hT_ready = sem("hT_ready")
        qk_hi_ready = sem("qk_hi_ready")
        qk_lo_ready = sem("qk_lo_ready")
        stack_zeroed = sem("stack_zeroed")
        stacks_in = [sem(f"stacks_in{i}") for i in range(2)]
        rows_out = sem("rows_out")
        y_out = sem("y_out")
        y_zeroed = sem("y_zeroed")
        dve_chain = sem("dve_chain")
        spare = sem("spare")
        pool_chain = sem("pool_chain")

        dense = DenseRing(dense_banks, dense_filled, {"A": freed_act, "V": freed_dve})
        NWEIGHTS = 35
        DVE_LINKS = 27

        m_exp = sem("m_exp")
        m_mask = sem("m_mask")
        m_pos = sem("m_pos")
        m_hots = sem("m_hots")
        m_tab = sem("m_tab")
        m_tab_i = sem("m_tab_i")
        m_tab_out = sem("m_tab_out")
        m_slots = sem("m_slots")
        m_w_out = sem("m_w_out")
        m_chain = sem("m_chain")
        ew_in = [sem(f"expert_w_in{i}") for i in range(2)]
        e_rows = [sem(f"expert_rows{i}") for i in range(2)]
        idx_ready = sem("idx_ready")
        e_turned = sem("expert_turned")
        e_xT = sem("expert_xT")
        e_up = sem("expert_up")
        e_gate = sem("expert_gate")
        e_h = sem("expert_h")
        e_down = sem("expert_down")
        e_y = sem("expert_y")
        e_added = [[sem(f"expert_added{i}{h}") for h in range(2)] for i in range(2)]
        f_in = [sem(f"f_in{i}") for i in range(2)]
        f_sum = sem("f_sum")
        f_out = [sem(f"f_out{i}") for i in range(2)]

        def unit_of(layer, s):
            h, t = divmod(s, NT)
            return h, t, ((t + 1) * P if layer == 0 else S)

        def q_group_units(g):
            return [("qr", g, 0), ("qr", g, 1)] + [("qn", g, j) for j in range(HG)]

        block = ctx.enter_context(nc.Block())

        @block.sync
        def _(sp):
            n = 0
            for dst, src in (
                (identity[:], ident), (identity_bf[:], identb), (wproj_sb[:], w_proj.rearrange("(k p) n -> p k n", p=P)),
                (wkr_sb[:, 0], w_kr.rearrange("(k p) n -> p k n", p=P)),
                (gam_sb[:, 0:1], gamma_q), (gam_sb[:, 1:2], gamma_kv),
                (wqr_sb[:, 0].rearrange("p g n -> p (g n)"), w_qr), (wqn_sb[:].rearrange("p h n -> p (h n)"), w_qn),
                (wuk_sb[:].rearrange("p g n -> p (g n)"), w_uk), (wuv_sb[:], w_uv),
                (rope_q[:, 0], cos_q), (rope_q[:, 1], sin_q), (rope_k[:, 0], cos_k), (rope_k[:, 1], sin_k),
                (causal_sb[:], causal), (window_sb[:], window),
                (wo0_sb[:], w_o0.rearrange("(k p) n -> p k n", p=P)),
                (wgate_sb[:], w_gate.rearrange("(k p) n -> p k n", p=P)), (wup_sb[:], w_up.rearrange("(k p) n -> p k n", p=P)),
                (wdown_sb[:], w_down.rearrange("(k p) n -> p k n", p=P)),
                (wqk1_sb[:, 0], w_q1.rearrange("(k p) n -> p k n", p=P)), (wqk1_sb[:, 1], w_k1.rearrange("(k p) n -> p k n", p=P)),
                (bqk1_sb[:, 0], b_q1), (bqk1_sb[:, 1], b_k1),
                (wv1_sb[:], w_v1.rearrange("(k p) n -> p k n", p=P)), (wo1_sb[:], w_o1.rearrange("(k p) n -> p k n", p=P)),
                (bv1_sb[:], b_v1.to_broadcast([P, 512])), (bo1_sb[:], b_o1.to_broadcast([P, D])),
                (gatew_sb[:], gate_w.rearrange("(k p) n -> p k n", p=P)),
                (sw13_sb[:, 0], sw1.rearrange("(k p) n -> p k n", p=P)), (sw13_sb[:, 1], sw3.rearrange("(k p) n -> p k n", p=P)),
                (sw2_sb[:], sw2.rearrange("(k p) n -> p k n", p=IC)),
                (tri_sb[:], tri), (small_sb[:], small),
            ):
                sp.dma_start(dst, src).then_inc(weights_in, 16)
                n += 1
            assert n == NWEIGHTS - 1, n
            def wait(signal, value):
                sp.wait_ge(signal, value)
                sp.sem_inc(spare, 1)

            with sp.Fori(0, B) as b:
                wait(y_out, b * 16)
                sp.dma_start(xb[:], x_rows[bass.ds(b, 1)].rearrange("o p t d -> p (o t) d")).then_inc(x_in, 16)
                for g in range(G0):
                    wait(rope_ready, b * G0 + g + 1)
                    if g >= 2:
                        wait(scores_ready, b * 2 * UNITS + 16 * (g - 1))
                    for j in range(HG):
                        sp.dma_start(qT[QN:P, g % 2, j, :], rp[32 * j:32 * j + 32, 0, :]).then_inc(rope_moved, 16)
                wait(stack_zeroed, b + 1)
                for g in range(G0):
                    c, r0 = divmod(g * HG * HD1, P)
                    wait(qk_hi_ready, b * 4 + 4)
                    wait(qk_lo_ready, b * 4 + 4)
                    if g >= 2:
                        wait(scores_ready, b * 2 * UNITS + UNITS + 16 * (g - 1))
                    for st, src0, order in ((q_st, 0, (0, 1, 0, 1)), (k_st, 2, (0, 0, 1, 1))):
                        for j in range(HG):
                            for blk, part in enumerate(order):
                                src = (qk_hi, qk_lo)[part]
                                r = r0 + HD1 * j
                                sp.dma_start(st[blk * 16:blk * 16 + 16, g % 2, j, :].bitcast(F32),
                                             src[r:r + HD1, src0 + c, :].bitcast(F32)).then_inc(stacks_in[g % 2], 16)
                wait(xn_ready, b * 5 * NT + 5 * NT)
                sp.dma_start(xn_rows.rearrange("(b t p) d -> b p t d", b=B, p=P)[bass.ds(b, 1), :, :, 0:D]
                             .rearrange("o p t d -> p (o t) d"), xn).then_inc(rows_out, 16)
                wait(res_ready, b * 4 + 4)
                sp.dma_start(y_sum[0][0:T, :].rearrange("(b t p) d -> b p t d", b=B, p=P)[bass.ds(b, 1)]
                             .rearrange("o p t d -> p (o t) d"), xb[:]).then_inc(y_out, 16)

            sp.wait_ge(rows_out, B * 16)
            sp.wait_ge(y_out, B * 16)
            sp.wait_ge(m_mask, 1)
            sp.dma_start(xn_rows.rearrange("(t p) d -> p t d", p=P)[:, :, D:ROW], sc[:]).then_inc(m_w_out, 16)
            sp.wait_ge(m_tab_i, 1)
            for k in range(2):
                sp.dma_start(slot_tokens[k].rearrange("(g p c) -> p g c", g=4, p=P), tab_i[:, k]).then_inc(m_tab_out, 16)
            sp.wait_ge(m_tab_out, 32)
            for k in range(2):
                sp.dma_start(slots[:, k, :], slot_tokens[k].rearrange("(c p) -> p c", p=P),
                             allow_slow_non_contiguous=True).then_inc(m_slots, 16)
            with sp.Fori(0, E // 2) as ep:
                for i in range(2):
                    sp.wait_ge(e_down, ep * 2 + i + 1)
                    sp.sem_inc(spare, 1)
                    e = ep * 2 + i
                    for m, w in enumerate((w1, w3)):
                        sp.dma_start(w13_sb[:, i, m], w.rearrange("e (k p) n -> e p k n", p=P)[bass.ds(e, 1)]
                                     .rearrange("o p k n -> p (o k) n")).then_inc(ew_in[i], 16)
                    sp.dma_start(w2_sb[:, i], w2.rearrange("e (k p) n -> e p k n", p=IC)[bass.ds(e, 1)]
                                 .rearrange("o p k n -> p (o k) n")).then_inc(ew_in[i], 16)
            for done in e_added[0] + e_added[1]:
                sp.wait_ge(done, 16 * E // 2)
            for q in range(4):
                if q >= 2:
                    sp.wait_ge(f_out[q % 2], 16)
                for i in range(4):
                    sp.dma_start(fin[:, q % 2, i], y_sum[i][q * 512:(q + 1) * 512, :].rearrange("(t p) d -> p t d", p=P))\
                        .then_inc(f_in[q % 2], 16)
                sp.wait_ge(f_sum, q + 1)
                sp.dma_start(out[q * 512:(q + 1) * 512, :].rearrange("(t p) d -> p t d", p=P), fin[:, q % 2, 0])\
                    .then_inc(f_out[q % 2], 16)
            for done in f_out:
                sp.wait_ge(done, 32)

        @block.tensor
        def _(pe):
            pe.wait_ge(weights_in, (NWEIGHTS - 1) * 16)
            pe.wait_ge(consts_made, 2)

            def transposes(b, layer):
                pe.wait_ge(xn_ready, b * 5 * NT + NT * (layer if layer == 1 else layer + 1))
                for k in range(KD):
                    dense.wait_free(pe, b, "xT", layer, k)
                    for t in range(NT):
                        mm = pe.transpose(dense.bank("xT", layer, k)[:, t * P:(t + 1) * P],
                                          xn[:, t, k * P:(k + 1) * P], identity[:])
                    mm.then_inc(dense_filled, 1)

            def product(b, name, out, pairs):
                dense.wait_free(pe, b, *name)
                bank = dense.bank(*name)
                for i, (lhsT, rhs) in enumerate(pairs):
                    mm = pe.matmul(out(bank), lhsT, rhs, start=(i == 0), stop=(i == len(pairs) - 1))
                mm.then_inc(dense_filled, 1)

            def q_unit(b, name):
                g, j = name[1], name[2]
                if name[0] == "qr":
                    product(b, name, lambda k: k[:, :], [(wqr_sb[:, j, g, :], cT[:, 0, :])])
                else:
                    product(b, name, lambda k: k[0:QN, :], [(wqn_sb[:, g * HG + j, :], cT[:, 0, :])])

            def scores(b, layer, s):
                h, t, n = unit_of(layer, s)
                u = layer * UNITS + s
                g, j = divmod(h, HG)
                bank = score_banks[u % 3]
                pe.wait_ge(probs_ready, b * 2 * UNITS + (u - 2 if u >= 3 else 0))
                if t == 0 and j == 0:
                    if layer == 0:
                        dense.wait_read(pe, b, "qn", g, HG - 1)
                        pe.wait_ge(rope_moved, b * H0 * 16 + 64 * (g + 1))
                        if g == 0:
                            pe.wait_ge(kr_copied, b + 1)
                    else:
                        pe.wait_ge(stacks_in[g % 2], (b * 2 + g // 2 + 1) * 32 * 16)
                q = (qT[:, g % 2, j] if layer == 0 else q_st[:, g % 2, j])[:, t * P:(t + 1) * P]
                k = kT[:, g, 0:n] if layer == 0 else k_st[:, g % 2, j]
                pe.matmul(bank[:, 0:n], q, k, start=True, stop=False)
                if layer == 0:
                    mm = pe.matmul(bank[:, t * P:n], identity_bf[:], causal_sb[:], start=False, stop=True)
                else:
                    m = t * P + P - WINDOW
                    mm = pe.matmul(bank[:, SINKS:m], identity_bf[:],
                                   window_sb[:, SINKS + P * (NT - 1 - t):m + P * (NT - 1 - t)], start=False, stop=True)
                mm.then_inc(scores_ready, 1)

            def turn(b, layer, s):
                h, t, n = unit_of(layer, s)
                u = layer * UNITS + s
                pe.wait_ge(probs_normed, b * 2 * UNITS + u + 1)
                who = (turn_read_dve, turn_read_act)[u % 2]
                pe.wait_ge(who, b * UNITS + u // 2)
                for c in range(n // P):
                    mm = pe.transpose(turn_banks[u % 2][:, c * P:(c + 1) * P],
                                      probs_n[:, u % 3, c * P:(c + 1) * P], identity[:])
                mm.then_inc(turned, 1)

            def heads(b, layer, g):
                base = b * UNITS + layer * (UNITS // 2) + 8 * (g + 1)
                pe.wait_ge(turn_read_dve, base)
                pe.wait_ge(turn_read_act, base)
                pe.wait_ge(attn_ready, b * 2 * G0 + layer * G0 + g)
                if g == 0:
                    dense.wait_read(pe, b, *(("v0",) if layer == 0 else ("v1", NT - 1)))
                for kt in range(NT):
                    q0 = kt * P if layer == 0 else 0
                    for j in range(HG):
                        c = g * VD0 if layer == 0 else (g * HG + j) * 32
                        v = (v0 if layer == 0 else v1)[:, kt, c:c + 32]
                        mm = pe.matmul(out_bank[32 * j:32 * j + 32, q0:S], v, probsT[:, j, kt, q0:S],
                                       start=(kt == 0), stop=(kt == NT - 1))
                mm.then_inc(heads_out, 1)

            def attention(b, layer):
                for s in range(UNITS + 21):
                    if s < UNITS:
                        scores(b, layer, s)
                    if 0 <= s - LAG < UNITS:
                        turn(b, layer, s - LAG)
                    g, r = divmod(s, 16)
                    if r == 4 and g >= 1 and g - 1 < G0:
                        heads(b, layer, g - 1)
                    if layer == 0 and g + 1 < G0 and r in (5, 7, 9, 11, 13, 15):
                        q_unit(b, q_group_units(g + 1)[(r - 5) // 2])

            with pe.Fori(0, B) as b:
                transposes(b, 1)
                dense.wait_read(pe, b, "xT", 1, KD - 1)
                for t in range(NT):
                    product(b, ("proj", t), lambda k: k[:, 0:2 * CQ],
                            [(xnT[:, k, t * P:(t + 1) * P], wproj_sb[:, k, :]) for k in range(KD)])
                pe.wait_ge(xn_ready, b * 5 * NT + 2 * NT)
                for c in range(2):
                    dense.wait_free(pe, b, "cT", c)
                    for t in range(NT):
                        mm = pe.transpose(dense.bank("cT", c)[:, t * P:(t + 1) * P], cn[:, t, c * P:(c + 1) * P], identity[:])
                    mm.then_inc(dense_filled, 1)
                for r in range(2):
                    product(b, ("kr", r), lambda k: k[:, :], [(wkr_sb[:, r, k, :], xnT[:, k, :]) for k in range(KD)])
                dense.wait_read(pe, b, "cT", 1)
                dense.wait_free(pe, b, "v0")
                for t in range(NT):
                    mm = pe.matmul(dense.bank("v0")[:, t * P:(t + 1) * P], cT[:, 1, t * P:(t + 1) * P], wuv_sb[:],
                                   start=True, stop=True)
                mm.then_inc(dense_filled, 1)
                for g in range(G0):
                    product(b, ("kn", g), lambda k: k[0:KN, :], [(wuk_sb[:, g, :], cT[:, 1, :])])
                for name in q_group_units(0):
                    q_unit(b, name)
                attention(b, 0)
                pe.wait_ge(attn_ready, b * 2 * G0 + G0)
                for t in range(NT):
                    product(b, ("o0", t), lambda k: k[:, 0:D],
                            [(attnT[:, g, t * P:(t + 1) * P], wo0_sb[:, g, :]) for g in range(G0)])
                transposes(b, 2)
                dense.wait_read(pe, b, "xT", 2, KD - 1)
                for hf in range(HALVES):
                    for i in range(PLANES):
                        c = i * 256 + hf * P
                        for name, w in (("gate", wgate_sb), ("up", wup_sb)):
                            product(b, (name, i, hf), lambda k: k[:, :],
                                    [(w[:, k, c:c + P], xnT[:, k, :]) for k in range(KD)])
                pe.wait_ge(hT_ready, b * HALVES + HALVES)
                for t in range(NT):
                    product(b, ("down", t), lambda k: k[:, 0:D],
                            [(hT[:, m, t * P:(t + 1) * P], wdown_sb[:, m, :]) for m in range(8)])
                transposes(b, 3)
                dense.wait_read(pe, b, "xT", 3, KD - 1)
                for c in range(4):
                    product(b, ("qk", c), lambda k: k[:, :],
                            [(wqk1_sb[:, c // 2, k, (c % 2) * P:(c % 2 + 1) * P], xnT[:, k, :]) for k in range(KD)])
                for t in range(NT):
                    product(b, ("v1", t), lambda k: k[:, :],
                            [(xnT[:, k, t * P:(t + 1) * P], wv1_sb[:, k, :]) for k in range(KD)])
                attention(b, 1)
                pe.wait_ge(attn_ready, b * 2 * G0 + 2 * G0)
                for t in range(NT):
                    product(b, ("o1", t), lambda k: k[:, 0:D],
                            [(attnT[:, g, t * P:(t + 1) * P], wo1_sb[:, g, :]) for g in range(4)])
                transposes(b, 4)
                dense.wait_read(pe, b, "xT", 4, KD - 1)
                dense.wait_free(pe, b, "logit")
                for t in range(NT):
                    for k in range(KD):
                        mm = pe.matmul(dense.bank("logit")[:, t * E:(t + 1) * E], xnT[:, k, t * P:(t + 1) * P],
                                       gatew_sb[:, k, :], start=(k == 0), stop=(k == KD - 1))
                mm.then_inc(dense_filled, 1)
                for c in range(NSI):
                    for m, name in enumerate(("sg", "su")):
                        product(b, (name, c), lambda k: k[0:IC, :],
                                [(sw13_sb[:, m, k, c * IC:(c + 1) * IC], xnT[:, k, :]) for k in range(KD)])
                dense.wait_read(pe, b, "su", NSI - 1)
                for t in range(NT):
                    product(b, ("sdown", t), lambda k: k[:, 0:D],
                            [(shT[:, c, t * P:(t + 1) * P], sw2_sb[:, c, :]) for c in range(NSI)])

            pe.wait_ge(freed_dve, (B + 1) * dense.reads["V"])
            pe.wait_ge(m_mask, 2)
            flat = lambda a: a.rearrange("p t e -> p (t e)")
            pe.matmul(banks[0][:], tri_sb[:], flat(mask_b[:]), start=True, stop=False)
            for t in range(B * NT - 1):
                rest = B * NT - 1 - t
                mm = pe.matmul(banks[0][:, (t + 1) * E:].rearrange("p (t e) -> p t e", e=E), ones_b[:],
                               mask_b[:, t:t + 1, :].to_broadcast([P, rest, E]), start=False, stop=(rest == 1))
            mm.then_inc(m_pos, 1)
            pe.wait_ge(m_hots, 1)
            for g in range(4):
                for v in range(2):
                    for t in range(B * NT):
                        mm = pe.matmul(banks[1 + g][:, v * P:(v + 1) * P], onehot_a[:, t, g * P:(g + 1) * P],
                                       val_b[:, v, t, g * P:(g + 1) * P], start=(t == 0), stop=(t == B * NT - 1))
            mm.then_inc(m_tab, 1)
            pe.sem_inc(e_down, 2)
            with pe.Fori(0, E // 2) as ep:
                for i in range(2):
                    turned_bank, g_bank, u_bank, y_bank = banks[4 * i:4 * i + 4]
                    pe.wait_ge(e_rows[i], (ep + 1) * 32)
                    pe.wait_ge(e_xT, ep * 2 + i)
                    for hf in range(2):
                        for k in range(KD):
                            mm = pe.transpose(turned_bank[:, k * CAP + hf * P:k * CAP + hf * P + P],
                                              xg[:, i, hf, k * P:(k + 1) * P], identity[:])
                    mm.then_inc(e_turned, 1)
                    pe.wait_ge(e_xT, ep * 2 + i + 1)
                    pe.wait_ge(ew_in[i], (ep + 1) * 48)
                    pe.wait_ge(e_h, ep * 2 + i)
                    for m, bank in ((0, g_bank), (1, u_bank)):
                        for c in range(NI):
                            for k in range(KD):
                                mm = pe.matmul(bank[0:IC, c * CAP:(c + 1) * CAP], w13_sb[:, i, m, k, c * IC:(c + 1) * IC],
                                               xgT[:, i, k, :], start=(k == 0), stop=(k == KD - 1))
                    mm.then_inc(e_up, 1)
                    pe.wait_ge(e_h, ep * 2 + i + 1)
                    pe.wait_ge(e_y, ep * 2 + i + 1)
                    for hf in range(2):
                        for c in range(NI):
                            mm = pe.matmul(y_bank[:, hf * D:(hf + 1) * D], eh[:, i, c, hf * P:(hf + 1) * P],
                                           w2_sb[:, i, c, :], start=(c == 0), stop=(c == NI - 1))
                    mm.then_inc(e_down, 1)

        @block.scalar
        def _(act):
            act.wait_ge(weights_in, (NWEIGHTS - 1) * 16)
            act.sem_inc(freed_act, dense.reads["A"])

            def xT_copy(b, layer):
                for k in range(KD):
                    dense.wait_filled(act, b, "xT", layer, k)
                    act.activation(xnT[:, k, :], dense.bank("xT", layer, k)[:], ACT.Copy).then_inc(freed_act, 1)

            def qn_copy(b, g, j):
                dense.wait_filled(act, b, "qn", g, j)
                if g >= 2 and j == 0:
                    act.wait_ge(scores_ready, b * 2 * UNITS + 16 * (g - 1))
                act.activation(qT[0:QN, g % 2, j, :], dense.bank("qn", g, j)[0:QN, :], ACT.Copy,
                               scale=float(QN + QR) ** -0.5).then_inc(freed_act, 1)

            def attention(b, layer):
                for s in range(UNITS + 22):
                    if s < UNITS:
                        h, t, n = unit_of(layer, s)
                        u = layer * UNITS + s
                        act.wait_ge(max_ready, b * 2 * UNITS + u + 1)
                        act.wait_ge(probs_normed, b * 2 * UNITS + (u - 2 if u >= 3 else 0))
                        act.activation(probs[:, u % 3, 0:n], score_banks[u % 3][:, 0:n], ACT.Exp,
                                       bias=nmax[:, u % 4:u % 4 + 1], accum_out=den[:, u % 4:u % 4 + 1])\
                            .then_inc(probs_ready, 1)
                    v = s - LAG - 1
                    if 0 <= v < UNITS and v % 2 == 1:
                        h, t, n = unit_of(layer, v)
                        u = layer * UNITS + v
                        act.wait_ge(turned, b * 2 * UNITS + u + 1)
                        if v % 16 == 1:
                            act.wait_ge(heads_out, b * 2 * G0 + layer * G0 + v // 16)
                        act.activation(probsT[:, h % HG, 0:n // P, t * P:(t + 1) * P],
                                       turn_banks[1][:, 0:n].rearrange("p (c q) -> p c q", q=P), ACT.Copy)\
                            .then_inc(turn_read_act, 1)
                    g, r = divmod(s, 16)
                    if r == 5 and g >= 1 and g - 1 < G0:
                        act.wait_ge(heads_out, b * 2 * G0 + layer * G0 + g)
                        if g == 1 and layer == 1:
                            dense.wait_filled(act, b, "o0", NT - 1)
                        act.activation(attnT[:, g - 1, :], out_bank[:], ACT.Copy).then_inc(attn_ready, 1)
                    if layer == 0 and g + 1 < G0 and r in (9, 11, 13, 15):
                        qn_copy(b, g + 1, (r - 9) // 2)

            with act.Fori(0, B) as b:
                xT_copy(b, 1)
                for c in range(2):
                    dense.wait_filled(act, b, "cT", c)
                    act.activation(cT[:, c, :], dense.bank("cT", c)[:], ACT.Copy, scale=gam_sb[:, c:c + 1]).then_inc(freed_act, 1)
                dense.wait_filled(act, b, "v0")
                act.activation(v0[:].rearrange("p t n -> p (t n)"), dense.bank("v0")[:], ACT.Copy).then_inc(freed_act, 1)
                for g in range(G0):
                    dense.wait_filled(act, b, "kn", g)
                    act.activation(kT[0:KN, g, :], dense.bank("kn", g)[0:KN, :], ACT.Copy).then_inc(freed_act, 1)
                for j in range(HG):
                    qn_copy(b, 0, j)
                attention(b, 0)
                xT_copy(b, 2)
                for hf in range(HALVES):
                    for i in range(PLANES):
                        dense.wait_filled(act, b, "gate", i, hf)
                        n = hf * PLANES + i
                        if n >= 2:
                            dense.wait_read(act, b, "up", (n - 2) % PLANES, (n - 2) // PLANES)
                        act.activation(sg[:, i % 2, :], dense.bank("gate", i, hf)[:], ACT.Silu).then_inc(freed_act, 1)
                        dense.wait_read(act, b, "up", i, hf)
                        act.activation(ha[:, i, :], hp[:, i, :], ACT.Abs).then_inc(abs_ready, 1)
                xT_copy(b, 3)
                for c in range(4):
                    dense.wait_read(act, b, "qk", c)
                    act.activation(qk_hi[:, c, :], qk32[:, c % 2, :], ACT.Copy).then_inc(qk_hi_ready, 1)
                attention(b, 1)
                xT_copy(b, 4)
                dense.wait_filled(act, b, "logit")
                act.activation(logits[:, bass.ds(b * NT, NT), :].rearrange("p t e -> p (t e)"),
                               dense.bank("logit")[:, 0:NT * E], ACT.Copy).then_inc(freed_act, 1)
                for c in range(NSI):
                    dense.wait_filled(act, b, "sg", c)
                    if c >= 2:
                        dense.wait_read(act, b, "su", c - 2)
                    act.activation(ssg[:, c % 2, :], dense.bank("sg", c)[0:IC, :], ACT.Silu).then_inc(freed_act, 1)

            act.wait_ge(y_out, B * 16)
            act.wait_ge(m_exp, 1)
            act.activation(sc[:], hit[:, 0], ACT.Exp).then_inc(m_exp, 1)
            with act.Fori(0, E // 2) as ep:
                for i in range(2):
                    turned_bank, g_bank, u_bank, y_bank = banks[4 * i:4 * i + 4]
                    act.wait_ge(e_turned, ep * 2 + i + 1)
                    act.activation(xgT[:, i].rearrange("p k n -> p (k n)"), turned_bank[:], ACT.Copy).then_inc(e_xT, 1)
                    act.wait_ge(e_up, ep * 2 + i + 1)
                    act.activation(eg[:, i].rearrange("p k n -> p (k n)"), g_bank[0:IC, :], ACT.Silu).then_inc(e_gate, 1)

        @block.vector
        def _(dve):
            dve.wait_ge(weights_in, (NWEIGHTS - 1) * 16)
            dve.sem_inc(freed_dve, dense.reads["V"])
            for w in (wkr_sb[:].rearrange("p r k n -> p r (k n)"), wqr_sb[:].rearrange("p r g n -> p r (g n)")):
                a, r = (w[:, i, :].rearrange("p (m two) -> p m two", two=2) for i in range(2))
                dve.tensor_scalar(r[:, :, 0], a[:, :, 1], -1.0, None, ALU.mult)
                last = dve.tensor_copy(r[:, :, 1], a[:, :, 0])
            last.then_inc(consts_made, 1)
            dve.tensor_scalar(bqk1_sb[:, 0, :], bqk1_sb[:, 0, :], float(HD1) ** -0.5, None, ALU.mult).then_inc(consts_made, 1)
            dve.wait_ge(consts_made, 2)

            def norm(b, n, ch, src, dst, count, width):
                for i in range(count):
                    if i == count - 1:
                        ch.link(dve.bn_stats(stats[:, i, :], src(i)))
                    else:
                        dve.bn_stats(stats[:, i, :], src(i))
                dve.sem_inc(spare, 1)
                for i in range(count):
                    if i == count - 1:
                        ch.link(dve.bn_aggr(mv[:, i, :], stats[:, i, :]))
                    else:
                        dve.bn_aggr(mv[:, i, :], stats[:, i, :])
                dve.tensor_scalar(vare[:, 0:count], mv[:, 0:count, 1], EPS, None, ALU.add).then_inc(var_ready, 1)
                dve.wait_ge(rstd_ready, b * 5 + n)
                for i in range(count):
                    ins = dve.tensor_scalar(dst(i), src(i), mv[:, i, 0:1], rstd[:, i:i + 1], ALU.subtract, ALU.mult)
                    if count == NT:
                        ins.then_inc(xn_ready, 1)
                return ins

            def q_rope(b, g, ch):
                for r in range(2):
                    dense.wait_filled(dve, b, "qr", g, r)
                    if r == 0:
                        dve.wait_ge(rope_moved, b * H0 * 16 + 64 * g)
                    dve.tensor_tensor(rp[:, 1 + r, :], dense.bank("qr", g, r)[:], rope_q[:, r, :], ALU.mult).then_inc(freed_dve, 1)
                ch.link(dve.drain())
                dve.tensor_tensor(rp[:, 0, :], rp[:, 1, :], rp[:, 2, :], ALU.add).then_inc(rope_ready, 1)

            def attention(b, layer, ch):
                for s in range(UNITS + 22):
                    if s < UNITS:
                        h, t, n = unit_of(layer, s)
                        u = layer * UNITS + s
                        dve.wait_ge(scores_ready, b * 2 * UNITS + u + 1)
                        dve.wait_ge(probs_ready, b * 2 * UNITS + (u - 3 if u >= 4 else 0))
                        dve.tensor_reduce(nmax[:, u % 4:u % 4 + 1], score_banks[u % 3][:, 0:n], AX.X, ALU.max, negate=True)\
                            .then_inc(max_ready, 1)
                    if 1 <= s <= UNITS:
                        u = layer * UNITS + s - 1
                        dve.wait_ge(probs_ready, b * 2 * UNITS + u + 1)
                        dve.wait_ge(probs_normed, b * 2 * UNITS + (u - 3 if u >= 4 else 0))
                        dve.reciprocal(rden[:, u % 4:u % 4 + 1], den[:, u % 4:u % 4 + 1]).then_inc(rden_ready, 1)
                    v = s - LAG - 1
                    if 0 <= v < UNITS and v % 2 == 0:
                        h, t, n = unit_of(layer, v)
                        u = layer * UNITS + v
                        dve.wait_ge(turned, b * 2 * UNITS + u + 1)
                        if v % 16 == 0:
                            dve.wait_ge(heads_out, b * 2 * G0 + layer * G0 + v // 16)
                        dve.tensor_copy(probsT[:, h % HG, 0:n // P, t * P:(t + 1) * P],
                                        turn_banks[0][:, 0:n].rearrange("p (c q) -> p c q", q=P)).then_inc(turn_read_dve, 1)
                    g, r = divmod(s, 16)
                    if layer == 0 and g + 1 < G0 and r == 7:
                        q_rope(b, g + 1, ch)

            def residual(b, name, ch, bias=None):
                for t in range(NT):
                    dense.wait_filled(dve, b, name, t)
                    ins = dve.tensor_tensor(xb[:, t, :], xb[:, t, :], dense.bank(name, t)[:, 0:D], ALU.add)
                    ins.then_inc(freed_dve, 1)
                ch.link(dve.drain())

            with dve.Fori(0, B) as b:
                ch = Chain(dve, dve_chain, b, DVE_LINKS)
                dve.wait_ge(x_in, (b + 1) * 16)
                dve.wait_ge(rows_out, b * 16)
                norm(b, 1, ch, lambda i: xb[:, i, :], lambda i: xn[:, i, :], NT, D)
                for t in range(NT):
                    dense.wait_filled(dve, b, "proj", t)
                    ins = dve.tensor_copy(probsT[:, 0, t, 0:2 * CQ], dense.bank("proj", t)[:, 0:2 * CQ])
                    ins.then_inc(freed_dve, 1)
                ch.link(dve.drain())
                lat = lambda i: probsT[:, 0, i // 2, (i % 2) * CQ:(i % 2 + 1) * CQ]
                norm(b, 2, ch, lat, lambda i: cn[:, i // 2, (i % 2) * CQ:(i % 2 + 1) * CQ], 2 * NT, CQ)
                dve.drain().then_inc(xn_ready, NT)
                for r in range(2):
                    dense.wait_filled(dve, b, "kr", r)
                    dve.tensor_tensor(rp[KN:P, 1 + r, :], dense.bank("kr", r)[KN:P, :], rope_k[KN:P, r, :], ALU.mult).then_inc(freed_dve, 1)
                ch.link(dve.drain())
                dve.tensor_tensor(kT[KN:P, 0, :], rp[KN:P, 1, :], rp[KN:P, 2, :], ALU.add).then_inc(kr_ready, 1)
                dve.wait_ge(kr_ready, b + 1)
                q_rope(b, 0, ch)
                attention(b, 0, ch)
                residual(b, "o0", ch)
                norm(b, 3, ch, lambda i: xb[:, i, :], lambda i: xn[:, i, :], NT, D)
                for hf in range(HALVES):
                    for i in range(PLANES):
                        dense.wait_filled(dve, b, "up", i, hf)
                        dense.wait_read(dve, b, "gate", i, hf)
                        if hf == 1:
                            dve.wait_ge(abs_ready, b * 8 + i + 1)
                        dve.tensor_tensor(hp[:, i, :], dense.bank("up", i, hf)[:], sg[:, i % 2, :], ALU.mult).then_inc(freed_dve, 1)
                    dve.wait_ge(abs_ready, b * 8 + (hf + 1) * PLANES)
                    flat = lambda a: a.rearrange("p a n -> p (a n)")
                    dve.tensor_tensor(flat(wins[:, 0:3, :]), flat(ha[:, 0:3, :]), flat(ha[:, 1:4, :]), ALU.is_ge)
                    dve.tensor_tensor(flat(wins[:, 3:5, :]), flat(ha[:, 0:2, :]), flat(ha[:, 2:4, :]), ALU.is_ge)
                    ch.link(dve.tensor_tensor(wins[:, 5, :], ha[:, 0, :], ha[:, 3, :], ALU.is_ge))
                    w01, w12, w23, w02, w13, w03 = (wins[:, n, :] for n in range(6))
                    dve.tensor_tensor(wsum[:, 0, :], w01, w02, ALU.add)
                    dve.tensor_tensor(wsum[:, 1, :], w12, w13, ALU.add)
                    dve.tensor_tensor(wsum[:, 2, :], w23, w02, ALU.subtract)
                    ch.link(dve.tensor_tensor(wsum[:, 3, :], w13, w23, ALU.add))
                    dve.tensor_tensor(wsum[:, 0, :], wsum[:, 0, :], w03, ALU.add)
                    dve.tensor_tensor(wsum[:, 1, :], wsum[:, 1, :], w01, ALU.subtract)
                    dve.tensor_tensor(wsum[:, 2, :], wsum[:, 2, :], w12, ALU.subtract)
                    ch.link(dve.tensor_tensor(wsum[:, 3, :], wsum[:, 3, :], w03, ALU.add))
                    for i, (bound, op) in enumerate(((2.0, ALU.is_ge), (1.0, ALU.is_ge), (0.0, ALU.is_ge), (1.0, ALU.is_le))):
                        ins = dve.scalar_tensor_tensor(hT[:, 2 * i + hf, :], wsum[:, i, :], bound, hp[:, i, :], op, ALU.mult)
                    ins.then_inc(hT_ready, 1)
                    dve.wait_ge(hT_ready, b * 2 + hf + 1)
                residual(b, "down", ch)
                norm(b, 4, ch, lambda i: xb[:, i, :], lambda i: xn[:, i, :], NT, D)
                for c in range(4):
                    dense.wait_filled(dve, b, "qk", c)
                    if c >= 2:
                        dve.wait_ge(qk_hi_ready, b * 4 + c - 1)
                    dve.tensor_scalar(qk32[:, c % 2, :], dense.bank("qk", c)[:], float(HD1) ** -0.5 if c < 2 else 1.0,
                                      bqk1_sb[:, c // 2, c % 2:c % 2 + 1], ALU.mult, ALU.add).then_inc(freed_dve, 1)
                    dve.wait_ge(qk_hi_ready, b * 4 + c + 1)
                    dve.tensor_tensor(qk_lo[:, c, :], qk32[:, c % 2, :], qk_hi[:, c, :].bitcast(F32), ALU.subtract).then_inc(qk_lo_ready, 1)
                for t in range(NT):
                    dense.wait_filled(dve, b, "v1", t)
                    dve.tensor_tensor(v1[:, t, :], dense.bank("v1", t)[:], bv1_sb[:], ALU.add).then_inc(freed_dve, 1)
                attention(b, 1, ch)
                for t in range(NT):
                    dve.tensor_tensor(xb[:, t, :], xb[:, t, :], bo1_sb[:], ALU.add)
                ch.link(dve.drain())
                residual(b, "o1", ch)
                norm(b, 5, ch, lambda i: xb[:, i, :], lambda i: xn[:, i, :], NT, D)
                for c in range(NSI):
                    dense.wait_filled(dve, b, "su", c)
                    dense.wait_read(dve, b, "sg", c)
                    dve.tensor_tensor(shT[:, c, :], dense.bank("su", c)[0:IC, :], ssg[:, c % 2, :], ALU.mult).then_inc(freed_dve, 1)
                residual(b, "sdown", ch)
                dve.drain().then_inc(res_ready, 4)
                ch.done()

            ch = Chain(dve, m_chain)
            dense.wait_read(dve, B - 1, "logit")
            dve.wait_ge(y_out, B * 16)
            NTT = B * NT
            wide = lambda a: a.unsqueeze(2).to_broadcast([P, NTT, E])
            ch.link(dve.tensor_reduce(rsum[:], logits[:], AX.X, ALU.max))
            dve.tensor_tensor(hit[:, 0], logits[:], wide(rsum[:]), ALU.subtract).then_inc(m_exp, 1)
            dve.wait_ge(m_exp, 2)
            ch.link(dve.tensor_reduce(rsum[:], sc[:], AX.X, ALU.add))
            ch.link(dve.reciprocal(rrec[:], rsum[:]))
            ch.link(dve.tensor_tensor(sc[:], sc[:], wide(rrec[:]), ALU.mult))
            for t in range(NTT):
                last = dve.max(top[:, t, :], sc[:, t, :])
            ch.link(last)
            for t in range(NTT):
                last = dve.max_index(topi[:, t, :], top[:, t, :], sc[:, t, :])
            ch.link(last)
            dve.drain().then_inc(m_mask, 1)
            ch.link(dve.tensor_copy(topf[:], topi[:]))
            iota_e = small_sb[:, 0:E].unsqueeze(1).to_broadcast([P, NTT, E])
            ch.link(dve.tensor_tensor(hit[:, 0], iota_e, topf[:, :, 0:1].to_broadcast([P, NTT, E]), ALU.is_equal))
            for k in range(1, TOPK):
                ch.link(dve.tensor_tensor(hit[:, 1], iota_e, topf[:, :, k:k + 1].to_broadcast([P, NTT, E]), ALU.is_equal))
                ch.link(dve.tensor_tensor(hit[:, 0], hit[:, 0], hit[:, 1], ALU.add))
            dve.memset(ones_b[:], 1.0)
            ch.link(dve.tensor_copy(mask_b[:], hit[:, 0]))
            dve.drain().then_inc(m_mask, 1)
            pos = banks[0][:].rearrange("p (t e) -> p t e", e=E)
            dve.wait_ge(m_pos, 1)
            ch.link(dve.tensor_copy(posi[:, 0], pos))
            dve.tensor_single_scalar(posi[:, 1], posi[:, 0], 4, ALU.arith_shift_right)
            ch.link(dve.tensor_single_scalar(posi[:, 2], posi[:, 0], 15, ALU.bitwise_and))
            dve.tensor_copy(posf[:, 0], posi[:, 1])
            ch.link(dve.tensor_copy(posf[:, 1], posi[:, 2]))
            ch.link(dve.scalar_tensor_tensor(posf[:, 0], hit[:, 0], -1000.0, posf[:, 0], ALU.mult, ALU.add))
            ch.link(dve.tensor_scalar(posf[:, 0], posf[:, 0], 1000.0, None, ALU.add))
            iota16 = small_sb[:, 32:48].unsqueeze(1).to_broadcast([P, NTT * E, 16])
            for half, hot in ((0, onehot_a), (1, onehot_b)):
                col = posf[:, half].rearrange("p t e -> p (t e)").unsqueeze(2).to_broadcast([P, NTT * E, 16])
                last = dve.tensor_tensor(hot[:].rearrange("p t (e s) -> p (t e) s", s=16), iota16, col, ALU.is_equal)
            ch.link(last)
            dve.tensor_scalar(val_b[:, 0].rearrange("p t n -> p (t n)"), onehot_b[:].rearrange("p t n -> p (t n)"),
                              small_sb[:, 80:81], None, ALU.mult)
            for t in range(NTT):
                last = dve.tensor_scalar(val_b[:, 1, t, :], onehot_b[:, t, :], float(t + 1), None, ALU.mult)
            last.then_inc(m_hots, 1)
            dve.wait_ge(m_tab, 1)
            for g in range(4):
                last = dve.tensor_tensor(tabm[:, g, :].rearrange("p (v e s) -> p v e s", v=2, s=16),
                                         banks[1 + g][:, 0:256].rearrange("p (v e s) -> p v e s", v=2, s=16),
                                         small_sb[:, 64:72].unsqueeze(1).unsqueeze(3).to_broadcast([P, 2, 8, 16]), ALU.mult)
            ch.link(last)
            ch.link(dve.tensor_reduce(tab[:].rearrange("p g v s -> p (g v) s"),
                                      tabm[:].rearrange("p g (v e s) -> p (g v) s e", v=2, s=16), AX.X, ALU.add))
            ch.link(dve.tensor_scalar(tabs[:, :, 0, :], tab[:, :, 1, :], float(P), float(-P), ALU.mult, ALU.add))
            ch.link(dve.tensor_tensor(tabs[:, :, 0, :], tabs[:, :, 0, :], tab[:, :, 0, :], ALU.add))
            ch.link(dve.tensor_scalar(tabs[:, :, 0, :], tabs[:, :, 0, :], 0.0, None, ALU.max))
            ch.link(dve.tensor_scalar(tabs[:, :, 1, :], tab[:, :, 1, :], 0.0, None, ALU.is_equal))
            ch.link(dve.tensor_tensor(tabs[:, :, 2, :], tabs[:, :, 1, :],
                                      small_sb[:, 48:64].unsqueeze(1).to_broadcast([P, 4, 16]), ALU.mult))
            ch.link(dve.tensor_tensor(tabs[:, :, 2, :], tabs[:, :, 2, :], tabs[:, :, 0, :], ALU.add))
            dve.tensor_copy(tab_i[:, 0], tabs[:, :, 0, :])
            ch.link(dve.tensor_copy(tab_i[:, 1], tabs[:, :, 2, :]))
            dve.drain().then_inc(m_tab_i, 1)
            dve.sem_inc(e_y, 2)
            with dve.Fori(0, E // 2) as ep:
                for i in range(2):
                    turned_bank, g_bank, u_bank, y_bank = banks[4 * i:4 * i + 4]
                    dve.wait_ge(e_gate, ep * 2 + i + 1)
                    dve.tensor_tensor(eh[:, i].rearrange("p k n -> p (k n)"), u_bank[0:IC, :],
                                      eg[:, i].rearrange("p k n -> p (k n)"), ALU.mult).then_inc(e_h, 1)
                    dve.wait_ge(e_down, ep * 2 + i + 3)
                    for hf in range(2):
                        dve.wait_ge(e_added[i][hf], ep * 16)
                    for hf in range(2):
                        last = dve.tensor_scalar(yo[:, i, hf, :], y_bank[:, hf * D:(hf + 1) * D],
                                                 xg[:, i, hf, bass.ds(ep * 2 + (D + i), 1)], None, ALU.mult)
                    last.then_inc(e_y, 1)
            for q in range(4):
                dve.wait_ge(f_in[q % 2], 64 * (q // 2 + 1))
                a = [fin[:, q % 2, i].rearrange("p t d -> p (t d)") for i in range(4)]
                dve.tensor_tensor(a[0], a[0], a[1], ALU.add)
                ch.link(dve.tensor_tensor(a[2], a[2], a[3], ALU.add))
                dve.tensor_tensor(a[0], a[0], a[2], ALU.add).then_inc(f_sum, 1)

        @block.gpsimd
        def _(pool):
            pool.memset(zeros[:], 0.0).then_inc(pool_chain, 1)
            pool.memset(mhalf[:], -0.5).then_inc(pool_chain, 1)
            pool.wait_ge(pool_chain, 2)
            wide = lambda n: zeros[:].unsqueeze(1).to_broadcast([P, n, D])
            pool.dma_start(y_sum[0][T:YROWS, :], zeros[:]).then_inc(y_zeroed, 16)
            for i in range(1, 4):
                pool.dma_start(y_sum[i].rearrange("(t p) d -> p t d", p=P), wide(YROWS // P)).then_inc(y_zeroed, 16)

            def rstd_of(b, n, count):
                pool.wait_ge(var_ready, b * 5 + n)
                pool.tensor_tensor(rstd[:, 0:count], vare[:, 0:count], mhalf[:, 0:count], ALU.pow).then_inc(rstd_ready, 1)

            def attention(b, layer):
                for s in range(UNITS):
                    h, t, n = unit_of(layer, s)
                    u = layer * UNITS + s
                    pool.wait_ge(rden_ready, b * 2 * UNITS + u + 1)
                    pool.wait_ge(turned, b * 2 * UNITS + (u - 2 if u >= 3 else 0))
                    pool.sem_inc(spare, 1)
                    pool.tensor_scalar(probs_n[:, u % 3, 0:n], probs[:, u % 3, 0:n], rden[:, u % 4:u % 4 + 1], None, ALU.mult)\
                        .then_inc(probs_normed, 1)

            with pool.Fori(0, B) as b:
                rstd_of(b, 1, NT)
                rstd_of(b, 2, 2 * NT)
                pool.wait_ge(kr_ready, b + 1)
                pool.sem_inc(spare, 1)
                for g in range(1, G0):
                    last = pool.tensor_copy(kT[KN:P, g, :], kT[KN:P, 0, :])
                last.then_inc(kr_copied, 1)
                attention(b, 0)
                rstd_of(b, 3, NT)
                rstd_of(b, 4, NT)
                dense.wait_filled(pool, b, "down", NT - 1)
                pool.wait_ge(rstd_ready, b * 5 + 4)
                pool.sem_inc(spare, 1)
                pool.memset(q_st[64:QK_ROWS].rearrange("p a j n -> p (a j n)").bitcast(F32), 0.0).then_inc(pool_chain, 1)
                pool.wait_ge(pool_chain, b + 3)
                pool.sem_inc(spare, 1)
                pool.memset(k_st[64:QK_ROWS].rearrange("p a j n -> p (a j n)").bitcast(F32), 0.0).then_inc(stack_zeroed, 1)
                attention(b, 1)
                rstd_of(b, 5, NT)

            pool.wait_ge(y_zeroed, 64)
            pool.wait_ge(m_w_out, 16)
            pool.wait_ge(m_slots, 32)

            def fetch(ep, i, kind, count):
                pool.tensor_copy(slot_now[:, i, kind, :], slots[:, kind, bass.ds(ep * 4 + 2 * i, 2)]).then_inc(idx_ready, 1)
                pool.wait_ge(idx_ready, count)
                pool.sem_inc(spare, 1)

            def gather(ep, i, count):
                fetch(ep, i, 0, count)
                for hf in range(2):
                    pool.indirect_dma_start(xg[:, i, hf, :], None, xn_rows,
                                            bass.IndirectOffsetOnAxis(ap=slot_now[:, i, 0, hf:hf + 1], axis=0),
                                            bounds_check=T - 1, oob_is_err=True).then_inc(e_rows[i], 16)

            def add_rows(ep, i, count):
                fetch(ep, i, 1, count)
                for hf in range(2):
                    pool.indirect_dma_start(y_sum[i * 2 + hf],
                                            bass.IndirectOffsetOnAxis(ap=slot_now[:, i, 1, hf:hf + 1], axis=0),
                                            yo[:, i, hf, :], None, bounds_check=YROWS - 1, oob_is_err=True,
                                            compute_op=ALU.add).then_inc(e_added[i][hf], 16)

            for i in range(2):
                gather(0, i, i + 1)
            with pool.Fori(0, E // 2 - 1) as ep:
                for i in range(2):
                    pool.wait_ge(e_y, ep * 2 + i + 3)
                    pool.sem_inc(spare, 1)
                    add_rows(ep, i, ep * 4 + 2 * i + 3)
                    gather(ep + 1, i, ep * 4 + 2 * i + 4)
            for i in range(2):
                pool.wait_ge(e_y, E - 2 + i + 3)
                add_rows(E // 2 - 1, i, 2 * E - 2 + i + 1)
            for done in e_added[0] + e_added[1]:
                pool.wait_ge(done, 16 * E // 2)


def kernel(**inputs):
    import ml_dtypes
    import numpy as np
    from concourse import bacc
    from concourse.bass_utils import run_bass_kernel_spmd

    i = {k: np.asarray(v) for k, v in inputs.items()}
    f = np.float32
    w_dkv = i["L0_attn_w_dkv"]
    w_ukv = i["L0_attn_w_ukv"]

    def planes(w):
        return w.reshape(w.shape[0], FF // 4, 4).transpose(0, 2, 1).reshape(w.shape[0], FF)

    def pad_heads(w):
        o = np.zeros((H1, 32) + w.shape[1:], w.dtype)
        o[:, :HD1] = w.reshape((H1, HD1) + w.shape[1:])
        return o.reshape((H1 * 32,) + w.shape[1:])

    def rope(dim, rows):
        inv = (1.0 / f(10000.0) ** (np.arange(0, dim, 2, dtype=f) / f(dim))).astype(f)
        ang = np.arange(S, dtype=f)[:, None] * inv
        c = np.repeat(np.cos(ang).astype(f).T, 2, axis=0), np.repeat(np.sin(ang).astype(f).T, 2, axis=0)
        return [np.tile(a, (rows // dim, 1)) for a in c]

    cos_q, sin_q = (a * f((QN + QR) ** -0.5) for a in rope(QR, P))
    cos_k, sin_k = rope(KR, P)
    bf = ml_dtypes.bfloat16
    r, c = np.arange(P)[:, None], np.arange(S)[None, :]
    small = np.zeros((P, 96), f)
    small[:, 0:32] = np.arange(32)
    small[:, 32:48] = np.arange(16)
    small[:, 48:64] = DUMMY + (r % 128 // 1 % 16 % 8) * 16 + np.arange(16)
    small[:, 64:72] = (r // 16 == np.arange(8))
    small[:, 80] = np.arange(P)
    arrays = {
        "x": i["L0_attn_x"].reshape(T, D),
        "w_proj": np.concatenate([i["L0_attn_w_dq"], w_dkv[:, :CQ]], axis=1),
        "w_kr": np.concatenate([np.zeros((D, KN), f), w_dkv[:, CQ:]], axis=1),
        "gamma_q": i["L0_attn_gamma_q"].reshape(CQ, 1), "gamma_kv": i["L0_attn_gamma_kv"].reshape(CQ, 1),
        "w_qn": i["L0_attn_w_uq"][:, :H0 * QN], "w_qr": i["L0_attn_w_uq"][:, H0 * QN:],
        "w_uk": w_ukv[:, :G0 * KN], "w_uv": w_ukv[:, G0 * KN:], "w_o0": i["L0_attn_w_o"],
        "w_gate": planes(i["L0_ffn_w_gate"]), "w_up": planes(i["L0_ffn_w_up"]), "w_down": planes(i["L0_ffn_w_down"].T).T,
        "w_q1": i["L1_attn_Wq"].T, "w_k1": i["L1_attn_Wk"].T,
        "w_v1": pad_heads(i["L1_attn_Wv"]).T, "w_o1": pad_heads(i["L1_attn_Wo"].T),
        "b_q1": i["L1_attn_bq"].reshape(KD, P).T, "b_k1": i["L1_attn_bk"].reshape(KD, P).T,
        "b_v1": pad_heads(i["L1_attn_bv"]).reshape(1, 512), "b_o1": i["L1_attn_bo"].reshape(1, D),
        "gate_w": i["L1_ffn_gate_w"].T, "w1": i["L1_ffn_w1"], "w2": i["L1_ffn_w2"], "w3": i["L1_ffn_w3"],
        "sw1": i["L1_ffn_sw1"], "sw2": i["L1_ffn_sw2"], "sw3": i["L1_ffn_sw3"],
        "cos_q": cos_q, "sin_q": sin_q, "cos_k": cos_k, "sin_k": sin_k,
        "ident": np.eye(P, dtype=f), "identb": np.eye(P, dtype=f).astype(bf),
        "causal": np.where(c[:, :P] > r, f(-1e30), f(0)).astype(bf),
        "window": np.where(c < r + S - P - WINDOW, f(-1e30), f(0)).astype(bf),
        "tri": (r < c[:, :P]).astype(bf), "small": small,
    }
    nc = bacc.Bacc("TRN2", target_bir_lowering=False, num_devices=1)
    args, ins = {}, {}
    for name, a in arrays.items():
        a = np.ascontiguousarray(a)
        ins[f"in_{name}"] = a
        args[name] = nc.dram_tensor(f"in_{name}", a.shape, mybir.dt.from_np(a.dtype), kind="ExternalInput").ap()
    args["out"] = nc.dram_tensor("out_0", (T, D), F32, kind="ExternalOutput").ap()
    build(nc, **args)
    res = run_bass_kernel_spmd(nc, [ins], core_ids=[0])
    return res.results[0]["out_0"].reshape(B, S, D)
```

```python
from contextlib import ExitStack

import concourse.bass as bass
from concourse import mybir

F32 = mybir.dt.float32
F32R = mybir.dt.float32r
BF16 = mybir.dt.bfloat16
I32 = mybir.dt.int32
U32 = mybir.dt.uint32
ALU = mybir.AluOpType
ACT = mybir.ActivationFunctionType
AX = mybir.AxisListType

P = 128
B, S, D = 4, 512, 256
T = B * S
NT = S // P
KD = D // P
EPS = 1e-5
H0, G0, QN, QR, KN, KR, VD0 = 16, 4, 96, 32, 64, 64, 32
CQ = 128
HG = H0 // G0
FF = 1024
PLANES, HALVES = 4, 2
H1, HD1, WINDOW, SINKS = 16, 16, 64, 4
QK_ROWS = 96
E, TOPK, INTER, CAP = 32, 6, 176, 256
IC = 88
NI = INTER // IC
SI = 2 * INTER
NSI = SI // IC
NBUF = 4
ROW = D + E
DUMMY = T
YROWS = T + P
WCOLS = 2 * P - 1 - WINDOW - SINKS
TILES = G0 * NT
UNITS = H0 * NT
DIVLAG = 2
LAG = 5
NPROB = 8


def shares(pattern, count):
    return [pattern[u % len(pattern)] for u in range(count)]


class Shared:

    def __init__(self, who, signals):
        self.who, self.signals = who, signals
        self.total = {w: who.count(w) for w in signals}

    def wait(self, eng, b, u):
        w = self.who[u]
        eng.wait_ge(self.signals[w], b * self.total[w] + self.who[:u + 1].count(w))

    def wait_up_to(self, eng, b, u):
        for w, signal in self.signals.items():
            eng.wait_ge(signal, b * self.total[w] + self.who[:u + 1].count(w))

    def done(self, ins, u):
        ins.then_inc(self.signals[self.who[u]], 1)


def dense_units():
    u = [(("xT", 1, k), "A") for k in range(KD)]
    u += [(("proj", t), "V") for t in range(NT)]
    u += [(("cT", c), "A") for c in range(2)]
    u += [(("kr", r), "V") for r in range(2)]
    u += [(("v0",), "A")]
    u += [(("kn", g), "A") for g in range(G0)]
    for g in range(G0):
        u += [(("qr", g, r), "V") for r in range(2)]
        u += [(("qn", g, j), "A") for j in range(HG)]
    u += [(("o0", t), "V") for t in range(NT)]
    u += [(("xT", 2, k), "A") for k in range(KD)]
    for hf in range(HALVES):
        for i in range(PLANES):
            u += [(("gate", i, hf), "A"), (("up", i, hf), "V")]
    u += [(("down", t), "V") for t in range(NT)]
    u += [(("xT", 3, k), "A") for k in range(KD)]
    u += [(("qk", c), "V") for c in range(4)]
    u += [(("v1", t), "V") for t in range(NT)]
    u += [(("o1", t), "V") for t in range(NT)]
    u += [(("xT", 4, k), "A") for k in range(KD)]
    u += [(("logit",), "A")]
    for c in range(NSI):
        u += [(("sg", c), "A"), (("su", c), "V")]
    u += [(("sdown", t), "V") for t in range(NT)]
    return u


class DenseRing:

    def __init__(self, banks, filled, freed):
        units = dense_units()
        self.banks, self.filled, self.freed = banks, filled, freed
        self.n = {name: i for i, (name, _) in enumerate(units)}
        self.by = [who for _, who in units]
        self.total = len(units)
        assert self.total % 2 == 0
        self.reads = {w: self.by.count(w) for w in "AV"}

    def bank(self, *name):
        return self.banks[self.n[name] % 2]

    def wait_free(self, pe, b, *name):
        n = self.n[name]
        m = (n - 2) % self.total
        who = self.by[m]
        k = self.by[:m + 1].count(who)
        base = (b + 1) if n >= 2 else b
        pe.wait_ge(self.freed[who], base * self.reads[who] + k)

    def wait_read(self, eng, b, *name):
        n = self.n[name]
        who = self.by[n]
        eng.wait_ge(self.freed[who], (b + 1) * self.reads[who] + self.by[:n + 1].count(who))

    def wait_filled(self, eng, b, *name):
        eng.wait_ge(self.filled, b * self.total + self.n[name] + 1)


class Chain:

    def __init__(self, eng, sem, b=0, per_pass=0):
        self.eng, self.sem, self.b, self.per_pass, self.n = eng, sem, b, per_pass, 0

    def link(self, ins):
        self.n += 1
        ins.then_inc(self.sem, 1)
        self.eng.wait_ge(self.sem, self.b * self.per_pass + self.n)

    def done(self):
        assert self.n == self.per_pass, (self.n, self.per_pass)


def build(nc, x, w_proj, w_kr, gamma_q, gamma_kv, w_qn, w_qr, w_uk, w_uv, w_o0, w_gate, w_up, w_down,
          w_q1, w_k1, w_v1, w_o1, b_q1, b_k1, b_v1, b_o1, gate_w, w1, w2, w3, sw1, sw2, sw3,
          cos_q, sin_q, cos_k, sin_k, ident, identb, causal, window, tri, small, out):
    x_rows = x.rearrange("(b t p) d -> b p t d", b=B, p=P)
    xn_rows = nc.dram_tensor("xn_rows", (T, ROW), F32).ap()
    q_parts = nc.dram_tensor("q_parts", (KD, P // HD1, 2, HD1, S), F32).ap()
    k_parts = nc.dram_tensor("k_parts", (KD, P // HD1, 4, HD1, S), F32).ap()
    slot_tokens = nc.dram_tensor("slot_tokens", (2, E * CAP), I32).ap()
    y_sum = [nc.dram_tensor(f"y_sum{i}", (YROWS, D), F32).ap() for i in range(4)]

    ctx = ExitStack()
    with ctx:
        def sb(name, shape, dt=F32, stack=None):
            return (stack or ctx).enter_context(nc.sbuf_tensor(name, shape, dt))

        def sem(name):
            return ctx.enter_context(nc.semaphore(name))

        banks = [ctx.enter_context(nc.psum_tensor(f"bank{i}", [P, 512], F32)) for i in range(8)]
        score_banks, turn_banks, out_bank, dense_banks = banks[0:3], banks[3:5], banks[5], banks[6:8]

        identity = sb("identity", [P, P])
        identity_bf = sb("identity_bf", [P, P], BF16)
        tri_sb = sb("tri_sb", [P, P], BF16)
        small_sb = sb("small_sb", [P, 96])
        logits = sb("logits", [P, B * NT, E])
        zeros = sb("zeros", [P, D])

        seq = ExitStack()
        wproj_sb = sb("wproj_sb", [P, KD, 2 * CQ], F32, seq)
        wkr_sb = sb("wkr_sb", [P, 2, KD, P], F32, seq)
        gam_sb = sb("gam_sb", [P, 2], F32, seq)
        wqn_sb = sb("wqn_sb", [P, H0, QN], F32, seq)
        wqr_sb = sb("wqr_sb", [P, 2, G0, P], F32, seq)
        wuk_sb = sb("wuk_sb", [P, G0, KN], F32, seq)
        wuv_sb = sb("wuv_sb", [P, G0 * VD0], F32, seq)
        wo0_sb = sb("wo0_sb", [P, G0, D], F32, seq)
        wgate_sb = sb("wgate_sb", [P, KD, FF], F32, seq)
        wup_sb = sb("wup_sb", [P, KD, FF], F32, seq)
        wdown_sb = sb("wdown_sb", [P, 8, D], F32, seq)
        wqk1_sb = sb("wqk1_sb", [P, 2, KD, D], F32, seq)
        bqk1_sb = sb("bqk1_sb", [P, 2, KD], F32, seq)
        wv1_sb = sb("wv1_sb", [P, KD, 512], F32, seq)
        wo1_sb = sb("wo1_sb", [P, 4, D], F32, seq)
        bv1_sb = sb("bv1_sb", [P, 512], F32, seq)
        bo1_sb = sb("bo1_sb", [P, D], F32, seq)
        gatew_sb = sb("gatew_sb", [P, KD, E], F32, seq)
        sw13_sb = sb("sw13_sb", [P, 2, KD, SI], F32, seq)
        sw2_sb = sb("sw2_sb", [IC, NSI, D], F32, seq)
        rope_q = sb("rope_q", [P, 2, S], F32, seq)
        rope_k = sb("rope_k", [P, 2, S], F32, seq)
        causal_sb = sb("causal_sb", [P, P], BF16, seq)
        window_sb = sb("window_sb", [P, WCOLS], BF16, seq)
        mhalf = sb("mhalf", [P, 8], F32, seq)

        xb = sb("xb", [P, NT, D], F32, seq)
        xnT = sb("xnT", [P, KD, S + SINKS], F32, seq)
        probs = sb("probs", [P, NPROB, S], F32, seq)
        xn = probs[:, 0:2, :].rearrange("p a (c n) -> p (a c) n", c=2)
        cn = probs[:, 2:4, :].rearrange("p a (c n) -> p (a c) n", c=2)
        probsT = sb("probsT", [P, 2, HG, NT, P], F32, seq)
        lat = probsT[:, 0, 0:2].rearrange("p a k (u q) -> p (a k u) q", u=1).rearrange("p (t k) q -> p t (k q)", t=NT)
        attnT = sb("attnT", [P, G0, S], F32, seq)
        stats = sb("stats", [P, 2 * NT, 6], F32, seq)
        mv = sb("mv", [P, 2 * NT, 2], F32, seq)
        vare = sb("vare", [P, 2 * NT], F32, seq)
        rstd = sb("rstd", [P, 2 * NT], F32, seq)
        nmax = sb("nmax", [P, 4], F32, seq)
        den = sb("den", [P, NPROB], F32, seq)
        rden = sb("rden", [P, NPROB], F32, seq)

        l0 = ExitStack()
        cT = sb("cT", [P, 2, S], F32, l0)
        qT = sb("qT", [P, 2, HG, S], F32, l0)
        kT = sb("kT", [P, G0, S], F32, l0)
        v0 = sb("v0_sb", [P, NT, G0 * VD0], F32, l0)
        rp = sb("rp", [P, 3, S], F32, l0)
        l0.close()
        ff = ExitStack()
        sg = sb("sg", [P, 2, S], F32, ff)
        hp = sb("hp", [P, PLANES, S], F32, ff)
        ha = sb("ha", [P, PLANES, S], F32, ff)
        wins = sb("wins", [P, 6, S], BF16, ff)
        wsum = sb("wsum", [P, 4, S], BF16, ff)
        hT = sb("hT", [P, 2 * PLANES, S], F32, ff)
        ff.close()
        l1 = ExitStack()
        qk32 = sb("qk32", [P, 2, S], F32, l1)
        qk_split = sb("qk_split", [P, 4, 2, S], F32R, l1)
        q_st = sb("q_st", [QK_ROWS, 2, HG, S], F32R, l1)
        k_st = sb("k_st", [QK_ROWS, 2, HG, S], F32R, l1)
        v1 = sb("v1_sb", [P, NT, H1 * 32], F32, l1)
        l1.close()
        sh = ExitStack()
        ssg = sb("ssg", [IC, 2, S], F32, sh)
        shT = sb("shT", [IC, NSI, S], F32, sh)
        sh.close()
        seq.close()

        moe = ExitStack()
        sc = sb("sc", [P, B * NT, E], F32, moe)
        rsum = sb("rsum", [P, B * NT], F32, moe)
        rrec = sb("rrec", [P, B * NT], F32, moe)
        top = sb("top", [P, B * NT, 8], F32, moe)
        topi = sb("topi", [P, B * NT, 8], U32, moe)
        topf = sb("topf", [P, B * NT, 8], F32, moe)
        hit = sb("hit", [P, 2, B * NT, E], F32, moe)
        mask_b = sb("mask_b", [P, B * NT, E], BF16, moe)
        ones_b = sb("ones_b", [P, P], BF16, moe)
        posi = sb("posi", [P, 3, B * NT, E], I32, moe)
        posf = sb("posf", [P, 2, B * NT, E], F32, moe)
        onehot_a = sb("onehot_a", [P, B * NT, E * 16], BF16, moe)
        onehot_b = sb("onehot_b", [P, B * NT, E * 16], BF16, moe)
        val_b = sb("val_b", [P, 2, B * NT, E * 16], BF16, moe)
        blockm = sb("blockm", [P, 8], F32, moe)
        tabm = sb("tabm", [P, 4, 256], F32, moe)
        tab = sb("tab", [P, 4, 2, 16], F32, moe)
        tabs = sb("tabs", [P, 4, 3, 16], F32, moe)
        tab_i = sb("tab_i", [P, 2, 4, 16], I32, moe)
        slots = sb("slots", [P, E + NBUF, 2, 2], I32, moe)
        slot_now = sb("slot_now", [P, NBUF, 2, 2], I32, moe)
        w13_sb = sb("w13_sb", [P, NBUF, 2, KD, INTER], F32, moe)
        w2_sb = sb("w2_sb", [IC, NBUF, NI, D], F32, moe)
        xg = sb("xg", [P, NBUF, 2, ROW], F32, moe)
        xgT = sb("xgT", [P, 2, KD, CAP], F32, moe)
        eg = sb("eg", [IC, 2, NI, CAP], F32, moe)
        eh = sb("eh", [IC, 2, NI, CAP], F32, moe)
        yo = sb("yo", [P, NBUF, 2, D], F32, moe)
        fin = sb("fin", [P, 2, 4, 4, D], F32, moe)
        moe.close()

        weights_in = sem("weights_in")
        x_in = sem("x_in")
        dense_filled = sem("dense_filled")
        freed_act = sem("dense_freed_act")
        freed_dve = sem("dense_freed_dve")
        consts_made = sem("consts_made")
        xn_ready = sem("xn_ready")
        var_ready = sem("var_ready")
        rstd_ready = sem("rstd_ready")
        kr_ready = sem("kr_ready")
        kr_copied = sem("kr_copied")
        rope_ready = sem("rope_ready")
        rope_moved = sem("rope_moved")
        scores_ready = sem("scores_ready")
        max_ready = sem("max_ready")
        probs_ready = sem("probs_ready")
        rden_ready = sem("rden_ready")
        turned = sem("turned")
        normed = Shared(shares("VPV", 2 * UNITS), {"P": sem("normed_pool"), "V": sem("normed_dve")})
        turn_read = Shared(shares("AVA", 2 * UNITS), {"A": sem("turn_read_act"), "V": sem("turn_read_dve")})
        heads_out = sem("heads_out")
        attn_ready = sem("attn_ready")
        res_ready = sem("res_ready")
        abs_ready = sem("abs_ready")
        hT_ready = sem("hT_ready")
        qk_hi_ready = sem("qk_hi_ready")
        qk_lo_ready = sem("qk_lo_ready")
        qk_out = sem("qk_out")
        stack_zeroed = sem("stack_zeroed")
        stacks_in = [sem(f"stacks_in{i}") for i in range(2)]
        rows_out = sem("rows_out")
        y_out = sem("y_out")
        y_zeroed = sem("y_zeroed")
        dve_chain = sem("dve_chain")
        spare = sem("spare")
        pool_chain = sem("pool_chain")

        dense = DenseRing(dense_banks, dense_filled, {"A": freed_act, "V": freed_dve})
        NWEIGHTS = 35
        DVE_LINKS = 27

        m_exp = sem("m_exp")
        m_mask = sem("m_mask")
        m_pos = sem("m_pos")
        m_hots = sem("m_hots")
        m_tab = sem("m_tab")
        m_tab_i = sem("m_tab_i")
        m_tab_out = sem("m_tab_out")
        m_slots = sem("m_slots")
        m_w_out = sem("m_w_out")
        m_chain = sem("m_chain")
        ew_in = [sem(f"expert_w_in{i}") for i in range(NBUF)]
        e_rows = [sem(f"expert_rows{i}") for i in range(NBUF)]
        idx_ready = sem("idx_ready")
        e_turned = sem("expert_turned")
        e_xT = sem("expert_xT")
        e_up = sem("expert_up")
        e_gate = sem("expert_gate")
        e_h = sem("expert_h")
        e_down = sem("expert_down")
        e_y = sem("expert_y")
        e_added = [sem(f"expert_added{i}") for i in range(NBUF)]
        e_settled = sem("expert_settled")
        f_in = [sem(f"f_in{i}") for i in range(2)]
        f_sum = sem("f_sum")
        f_out = [sem(f"f_out{i}") for i in range(2)]

        def unit_of(layer, s):
            g, t, j = s // 16, s // HG % NT, s % HG
            h = g * HG + j
            lo, hi = (0, (t + 1) * P) if layer == 0 else (max(t - 1, 0) * P, S)
            return h, t, lo, hi

        def q_group_units(g):
            return [("qr", g, 0), ("qr", g, 1)] + [("qn", g, j) for j in range(HG)]

        def copy_turned(eng, who, b, layer, s):
            u = layer * UNITS + s
            if not 0 <= s < UNITS or turn_read.who[u] != who:
                return
            h, t, lo, hi = unit_of(layer, s)
            eng.wait_ge(turned, b * 2 * UNITS + u + 1)
            if u >= 2 * HG and turn_read.who[u - s % HG:u].count(who) == 0:
                eng.wait_ge(heads_out, b * 2 * TILES + u // HG - 1)
            dst = probsT[:, t % 2, h % HG, lo // P:hi // P, :]
            src = turn_banks[u % 2][:, lo:hi].rearrange("p (c q) -> p c q", q=P)
            turn_read.done(eng.activation(dst, src, ACT.Copy) if who == "A" else eng.tensor_copy(dst, src), u)

        def normalise(eng, b, layer, s):
            h, t, lo, hi = unit_of(layer, s)
            u = layer * UNITS + s
            row = probs[:, u % NPROB, lo:hi]
            normed.done(eng.tensor_scalar(row, row, rden[:, u % NPROB:u % NPROB + 1], None, ALU.mult), u)

        row_banks, gate_banks, up_banks, y_banks = (banks[2 * n:2 * n + 2] for n in range(4))

        block = ctx.enter_context(nc.Block())

        @block.sync
        def _(sp):
            n = 0
            for dst, src in (
                (identity[:], ident), (identity_bf[:], identb), (wproj_sb[:], w_proj.rearrange("(k p) n -> p k n", p=P)),
                (wkr_sb[:, 0], w_kr.rearrange("(k p) n -> p k n", p=P)),
                (gam_sb[:, 0:1], gamma_q), (gam_sb[:, 1:2], gamma_kv),
                (wqr_sb[:, 0].rearrange("p g n -> p (g n)"), w_qr), (wqn_sb[:].rearrange("p h n -> p (h n)"), w_qn),
                (wuk_sb[:].rearrange("p g n -> p (g n)"), w_uk), (wuv_sb[:], w_uv),
                (rope_q[:, 0], cos_q), (rope_q[:, 1], sin_q), (rope_k[:, 0], cos_k), (rope_k[:, 1], sin_k),
                (causal_sb[:], causal), (window_sb[:], window),
                (wo0_sb[:], w_o0.rearrange("(k p) n -> p k n", p=P)),
                (wgate_sb[:], w_gate.rearrange("(k p) n -> p k n", p=P)), (wup_sb[:], w_up.rearrange("(k p) n -> p k n", p=P)),
                (wdown_sb[:], w_down.rearrange("(k p) n -> p k n", p=P)),
                (wqk1_sb[:, 0], w_q1.rearrange("(k p) n -> p k n", p=P)), (wqk1_sb[:, 1], w_k1.rearrange("(k p) n -> p k n", p=P)),
                (bqk1_sb[:, 0], b_q1), (bqk1_sb[:, 1], b_k1),
                (wv1_sb[:], w_v1.rearrange("(k p) n -> p k n", p=P)), (wo1_sb[:], w_o1.rearrange("(k p) n -> p k n", p=P)),
                (bv1_sb[:], b_v1.to_broadcast([P, 512])), (bo1_sb[:], b_o1.to_broadcast([P, D])),
                (gatew_sb[:], gate_w.rearrange("(k p) n -> p k n", p=P)),
                (sw13_sb[:, 0], sw1.rearrange("(k p) n -> p k n", p=P)), (sw13_sb[:, 1], sw3.rearrange("(k p) n -> p k n", p=P)),
                (sw2_sb[:], sw2.rearrange("(k p) n -> p k n", p=IC)),
                (tri_sb[:], tri), (small_sb[:], small),
            ):
                sp.dma_start(dst, src).then_inc(weights_in, 16)
                n += 1
            assert n == NWEIGHTS - 1, n
            def wait(signal, value):
                sp.wait_ge(signal, value)
                sp.sem_inc(spare, 1)

            sp.sem_inc(y_out, 16)
            sp.sem_inc(rows_out, 16)
            with sp.Fori(0, B) as b:
                wait(y_out, (b + 1) * 16)
                sp.dma_start(xb[:], x_rows[bass.ds(b, 1)].rearrange("o p t d -> p (o t) d")).then_inc(x_in, 16)
                for g in range(G0):
                    wait(rope_ready, b * G0 + g + 1)
                    if g >= 2:
                        wait(scores_ready, b * 2 * UNITS + 16 * (g - 1))
                    for j in range(HG):
                        sp.dma_start(qT[QN:P, g % 2, j, :], rp[32 * j:32 * j + 32, 0, :]).then_inc(rope_moved, 16)
                wait(stack_zeroed, b + 1)
                wait(qk_hi_ready, b * 4 + 4)
                for c in range(4):
                    wait(qk_lo_ready, b * 4 + c + 1)
                    for blk, part in enumerate((0, 1) if c < 2 else (0, 0, 1, 1)):
                        dst = q_parts[c, :, blk] if c < 2 else k_parts[c - 2, :, blk]
                        sp.dma_start(dst, qk_split[:, c, part, :].bitcast(F32)).then_inc(qk_out, 16)
                wait(stack_zeroed, b + 1)
                wait(qk_out, (b + 1) * 12 * 16)
                for g in range(G0):
                    if g >= 2:
                        wait(scores_ready, b * 2 * UNITS + UNITS + 16 * (g - 1))
                    c, h0 = divmod(g * HG, P // HD1)
                    heads_of = lambda parts: parts[c, h0:h0 + HG].rearrange("h a r n -> (a r) h n")
                    for half in range(2):
                        sp.dma_start(q_st[32 * half:32 * half + 32, g % 2].bitcast(F32), heads_of(q_parts)).then_inc(stacks_in[g % 2], 16)
                    sp.dma_start(k_st[0:64, g % 2].bitcast(F32), heads_of(k_parts)).then_inc(stacks_in[g % 2], 16)
                for done in stacks_in:
                    wait(done, (b + 1) * 2 * 48)
                wait(xn_ready, b * 5 * NT + 5 * NT)
                sp.dma_start(xn_rows.rearrange("(b t p) d -> b p t d", b=B, p=P)[bass.ds(b, 1), :, :, 0:D]
                             .rearrange("o p t d -> p (o t) d"), xn).then_inc(rows_out, 16)
                wait(res_ready, b * 4 + 4)
                sp.dma_start(y_sum[0][0:T, :].rearrange("(b t p) d -> b p t d", b=B, p=P)[bass.ds(b, 1)]
                             .rearrange("o p t d -> p (o t) d"), xb[:]).then_inc(y_out, 16)

            sp.wait_ge(rows_out, (B + 1) * 16)
            sp.wait_ge(y_out, (B + 1) * 16)
            def load_expert(e, i):
                at = (lambda w: w[e:e + 1]) if isinstance(e, int) else (lambda w: w[bass.ds(e, 1)])
                for m, w in enumerate((w1, w3)):
                    sp.dma_start(w13_sb[:, i, m], at(w.rearrange("e (k p) n -> e p k n", p=P))
                                 .rearrange("o p k n -> p (o k) n")).then_inc(ew_in[i], 16)
                sp.dma_start(w2_sb[:, i], at(w2.rearrange("e (k p) n -> e p k n", p=IC))
                             .rearrange("o p k n -> p (o k) n")).then_inc(ew_in[i], 16)

            for i in range(NBUF):
                load_expert(i, i)
            sp.wait_ge(m_mask, 1)
            sp.dma_start(xn_rows.rearrange("(t p) d -> p t d", p=P)[:, :, D:ROW], sc[:]).then_inc(m_w_out, 16)
            sp.wait_ge(m_tab_i, 1)
            for k in range(2):
                sp.dma_start(slot_tokens[k].rearrange("(g p c) -> p g c", g=4, p=P), tab_i[:, k]).then_inc(m_tab_out, 16)
            sp.wait_ge(m_tab_out, 32)
            for k in range(2):
                for hf in range(2):
                    sp.dma_start(slots[:, k * NBUF:k * NBUF + E, k, hf],
                                 slot_tokens[k].rearrange("(e h p) -> h p e", p=P, h=2)[hf],
                                 allow_slow_non_contiguous=True).then_inc(m_slots, 16)

            def settle(ep, i):
                sp.wait_ge(e_added[i], (ep + 1) * 32)
                sp.sem_inc(e_settled, 1)

            with sp.Fori(0, E // NBUF - 1) as ep:
                for i in range(NBUF):
                    wait(e_down, ep * NBUF + i + 1)
                    load_expert(ep * NBUF + (NBUF + i), i)
                    settle(ep, i)
            for i in range(NBUF):
                settle(E // NBUF - 1, i)
            for q in range(4):
                if q >= 2:
                    sp.wait_ge(f_out[q % 2], 16)
                for i in range(4):
                    sp.dma_start(fin[:, q % 2, i], y_sum[i][q * 512:(q + 1) * 512, :].rearrange("(t p) d -> p t d", p=P))\
                        .then_inc(f_in[q % 2], 16)
                sp.wait_ge(f_sum, q + 1)
                sp.dma_start(out[q * 512:(q + 1) * 512, :].rearrange("(t p) d -> p t d", p=P), fin[:, q % 2, 0])\
                    .then_inc(f_out[q % 2], 16)
            for done in f_out:
                sp.wait_ge(done, 32)

        @block.tensor
        def _(pe):
            pe.wait_ge(weights_in, (NWEIGHTS - 1) * 16)
            pe.wait_ge(consts_made, 2)

            def transposes(b, layer):
                pe.wait_ge(xn_ready, b * 5 * NT + NT * (layer if layer == 1 else layer + 1))
                for k in range(KD):
                    dense.wait_free(pe, b, "xT", layer, k)
                    for t in range(NT):
                        mm = pe.transpose(dense.bank("xT", layer, k)[:, t * P:(t + 1) * P],
                                          xn[:, t, k * P:(k + 1) * P], identity[:])
                    mm.then_inc(dense_filled, 1)

            def product(b, name, out, pairs):
                dense.wait_free(pe, b, *name)
                bank = dense.bank(*name)
                for i, (lhsT, rhs) in enumerate(pairs):
                    mm = pe.matmul(out(bank), lhsT, rhs, start=(i == 0), stop=(i == len(pairs) - 1))
                mm.then_inc(dense_filled, 1)

            def q_unit(b, name):
                g, j = name[1], name[2]
                if name[0] == "qr":
                    product(b, name, lambda k: k[:, :], [(wqr_sb[:, j, g, :], cT[:, 0, :])])
                else:
                    product(b, name, lambda k: k[0:QN, :], [(wqn_sb[:, g * HG + j, :], cT[:, 0, :])])

            def scores(b, layer, s):
                h, t, lo, hi = unit_of(layer, s)
                u = layer * UNITS + s
                g, j = divmod(h, HG)
                bank = score_banks[u % 3]
                if u >= 3:
                    pe.wait_ge(probs_ready, b * 2 * UNITS + u - 2)
                if s % 16 == 0:
                    if layer == 0:
                        dense.wait_read(pe, b, "qn", g, HG - 1)
                        pe.wait_ge(rope_moved, b * H0 * 16 + 64 * (g + 1))
                        if g == 0:
                            pe.wait_ge(kr_copied, b + 1)
                    else:
                        pe.wait_ge(stacks_in[g % 2], (b * 2 + g // 2 + 1) * 48)
                q = (qT[:, g % 2, j] if layer == 0 else q_st[:, g % 2, j])[:, t * P:(t + 1) * P]
                k = kT[:, g, lo:hi] if layer == 0 else k_st[:, g % 2, j, lo:hi]
                pe.matmul(bank[:, lo:hi], q, k, start=True, stop=False)
                if layer == 0:
                    mm = pe.matmul(bank[:, t * P:hi], identity_bf[:], causal_sb[:], start=False, stop=True)
                else:
                    first = P if t == 0 else 0
                    mm = pe.matmul(bank[:, lo:lo + WCOLS - first], identity_bf[:], window_sb[:, first:WCOLS],
                                   start=False, stop=True)
                mm.then_inc(scores_ready, 1)

            def turn(b, layer, s):
                h, t, lo, hi = unit_of(layer, s)
                u = layer * UNITS + s
                normed.wait(pe, b, u)
                if u >= 2:
                    turn_read.wait(pe, b, u - 2)
                for c in range(lo, hi, P):
                    mm = pe.transpose(turn_banks[u % 2][:, c:c + P], probs[:, u % NPROB, c:c + P], identity[:])
                mm.then_inc(turned, 1)

            def heads(b, layer, n):
                g, t = divmod(n, NT)
                turn_read.wait_up_to(pe, b, layer * UNITS + HG * (n + 1) - 1)
                if t == 0 and (layer or g):
                    pe.wait_ge(attn_ready, b * 2 * G0 + layer * G0 + g)
                if n == 0:
                    dense.wait_read(pe, b, *(("v0",) if layer == 0 else ("v1", NT - 1)))
                kts = range(t + 1) if layer == 0 else range(max(t - 1, 0), NT)
                for kt in kts:
                    for j in range(HG):
                        c = g * VD0 if layer == 0 else (g * HG + j) * 32
                        v = (v0 if layer == 0 else v1)[:, kt, c:c + 32]
                        mm = pe.matmul(out_bank[32 * j:32 * j + 32, t * P:(t + 1) * P], v, probsT[:, t % 2, j, kt, :],
                                       start=(kt == kts[0]), stop=(kt == kts[-1]))
                mm.then_inc(heads_out, 1)

            def attention(b, layer):
                for s in range(UNITS + LAG + 2):
                    if s < UNITS:
                        scores(b, layer, s)
                    if 0 <= s - LAG < UNITS:
                        turn(b, layer, s - LAG)
                    g, r = divmod(s, 16)
                    n, r4 = divmod(s - LAG - 1, HG)
                    if r4 == 0 and n >= 1:
                        heads(b, layer, n - 1)
                    if layer == 0 and g + 1 < G0 and r in (5, 7, 9, 11, 13, 15):
                        q_unit(b, q_group_units(g + 1)[(r - 5) // 2])

            with pe.Fori(0, B) as b:
                transposes(b, 1)
                dense.wait_read(pe, b, "xT", 1, KD - 1)
                for t in range(NT):
                    product(b, ("proj", t), lambda k: k[:, 0:2 * CQ],
                            [(xnT[:, k, t * P:(t + 1) * P], wproj_sb[:, k, :]) for k in range(KD)])
                pe.wait_ge(xn_ready, b * 5 * NT + 2 * NT)
                for c in range(2):
                    dense.wait_free(pe, b, "cT", c)
                    for t in range(NT):
                        mm = pe.transpose(dense.bank("cT", c)[:, t * P:(t + 1) * P], cn[:, t, c * P:(c + 1) * P], identity[:])
                    mm.then_inc(dense_filled, 1)
                for r in range(2):
                    product(b, ("kr", r), lambda k: k[:, :], [(wkr_sb[:, r, k, :], xnT[:, k, 0:S]) for k in range(KD)])
                dense.wait_read(pe, b, "cT", 1)
                dense.wait_free(pe, b, "v0")
                for t in range(NT):
                    mm = pe.matmul(dense.bank("v0")[:, t * P:(t + 1) * P], cT[:, 1, t * P:(t + 1) * P], wuv_sb[:],
                                   start=True, stop=True)
                mm.then_inc(dense_filled, 1)
                for g in range(G0):
                    product(b, ("kn", g), lambda k: k[0:KN, :], [(wuk_sb[:, g, :], cT[:, 1, :])])
                for name in q_group_units(0):
                    q_unit(b, name)
                attention(b, 0)
                pe.wait_ge(attn_ready, b * 2 * G0 + G0)
                for t in range(NT):
                    product(b, ("o0", t), lambda k: k[:, 0:D],
                            [(attnT[:, g, t * P:(t + 1) * P], wo0_sb[:, g, :]) for g in range(G0)])
                transposes(b, 2)
                dense.wait_read(pe, b, "xT", 2, KD - 1)
                for hf in range(HALVES):
                    for i in range(PLANES):
                        c = i * 256 + hf * P
                        for name, w in (("gate", wgate_sb), ("up", wup_sb)):
                            product(b, (name, i, hf), lambda k: k[:, :],
                                    [(w[:, k, c:c + P], xnT[:, k, 0:S]) for k in range(KD)])
                pe.wait_ge(hT_ready, b * HALVES + HALVES)
                for t in range(NT):
                    product(b, ("down", t), lambda k: k[:, 0:D],
                            [(hT[:, m, t * P:(t + 1) * P], wdown_sb[:, m, :]) for m in range(8)])
                transposes(b, 3)
                dense.wait_read(pe, b, "xT", 3, KD - 1)
                for c in range(4):
                    product(b, ("qk", c), lambda k: k[:, :],
                            [(wqk1_sb[:, c // 2, k, (c % 2) * P:(c % 2 + 1) * P],
                              xnT[:, k, 0:S] if c < 2 else xnT[:, k, SINKS:]) for k in range(KD)])
                for t in range(NT):
                    product(b, ("v1", t), lambda k: k[:, :],
                            [(xnT[:, k, SINKS + t * P:SINKS + (t + 1) * P], wv1_sb[:, k, :]) for k in range(KD)])
                attention(b, 1)
                pe.wait_ge(attn_ready, b * 2 * G0 + 2 * G0)
                for t in range(NT):
                    product(b, ("o1", t), lambda k: k[:, 0:D],
                            [(attnT[:, g, t * P:(t + 1) * P], wo1_sb[:, g, :]) for g in range(4)])
                transposes(b, 4)
                dense.wait_read(pe, b, "xT", 4, KD - 1)
                dense.wait_free(pe, b, "logit")
                for t in range(NT):
                    for k in range(KD):
                        mm = pe.matmul(dense.bank("logit")[:, t * E:(t + 1) * E], xnT[:, k, t * P:(t + 1) * P],
                                       gatew_sb[:, k, :], start=(k == 0), stop=(k == KD - 1))
                mm.then_inc(dense_filled, 1)
                for c in range(NSI):
                    for m, name in enumerate(("sg", "su")):
                        product(b, (name, c), lambda k: k[0:IC, :],
                                [(sw13_sb[:, m, k, c * IC:(c + 1) * IC], xnT[:, k, 0:S]) for k in range(KD)])
                dense.wait_read(pe, b, "su", NSI - 1)
                for t in range(NT):
                    product(b, ("sdown", t), lambda k: k[:, 0:D],
                            [(shT[:, c, t * P:(t + 1) * P], sw2_sb[:, c, :]) for c in range(NSI)])

            pe.wait_ge(freed_dve, (B + 1) * dense.reads["V"])
            pe.wait_ge(m_mask, 2)
            flat = lambda a: a.rearrange("p t e -> p (t e)")
            pe.matmul(banks[0][:], tri_sb[:], flat(mask_b[:]), start=True, stop=False)
            for t in range(B * NT - 1):
                rest = B * NT - 1 - t
                mm = pe.matmul(banks[0][:, (t + 1) * E:].rearrange("p (t e) -> p t e", e=E), ones_b[:],
                               mask_b[:, t:t + 1, :].to_broadcast([P, rest, E]), start=False, stop=(rest == 1))
            mm.then_inc(m_pos, 1)
            pe.wait_ge(m_hots, 1)
            for g in range(4):
                for v in range(2):
                    for t in range(B * NT):
                        mm = pe.matmul(banks[1 + g][:, v * P:(v + 1) * P], onehot_a[:, t, g * P:(g + 1) * P],
                                       val_b[:, v, t, g * P:(g + 1) * P], start=(t == 0), stop=(t == B * NT - 1))
            mm.then_inc(m_tab, 1)
            def turn_rows(ep, i):
                e, i, ep = ep * NBUF + i, i % NBUF, ep + i // NBUF
                pe.wait_ge(e_rows[i], (ep + 1) * 32)
                pe.wait_ge(e_xT, e + 1)
                for hf in range(2):
                    for k in range(KD):
                        mm = pe.transpose(row_banks[i % 2][:, k * CAP + hf * P:k * CAP + hf * P + P],
                                          xg[:, i, hf, k * P:(k + 1) * P], identity[:])
                mm.then_inc(e_turned, 1)

            def gate_up(ep, i):
                e, i, ep = ep * NBUF + i, i % NBUF, ep + i // NBUF
                pe.wait_ge(e_xT, e + 3)
                pe.wait_ge(ew_in[i], (ep + 1) * 48)
                pe.wait_ge(e_h, e + 1)
                for m, bank in enumerate((gate_banks[i % 2], up_banks[i % 2])):
                    for c in range(NI):
                        for k in range(KD):
                            mm = pe.matmul(bank[0:IC, c * CAP:(c + 1) * CAP], w13_sb[:, i, m, k, c * IC:(c + 1) * IC],
                                           xgT[:, i % 2, k, :], start=(k == 0), stop=(k == KD - 1))
                mm.then_inc(e_up, 1)

            def expert_out(ep, i):
                e = ep * NBUF + i
                pe.wait_ge(e_h, e + 3)
                pe.wait_ge(e_y, e + 1)
                for hf in range(2):
                    for c in range(NI):
                        mm = pe.matmul(y_banks[i % 2][:, hf * D:(hf + 1) * D], eh[:, i % 2, c, hf * P:(hf + 1) * P],
                                       w2_sb[:, i, c, :], start=(c == 0), stop=(c == NI - 1))
                mm.then_inc(e_down, 1)

            turn_rows(0, 0)
            gate_up(0, 0)
            turn_rows(0, 1)
            with pe.Fori(0, E // NBUF - 1) as ep:
                for i in range(NBUF):
                    gate_up(ep, i + 1)
                    expert_out(ep, i)
                    turn_rows(ep, i + 2)
            last = E // NBUF - 1
            for i in range(NBUF):
                if i + 1 < NBUF:
                    gate_up(last, i + 1)
                expert_out(last, i)
                if i + 2 < NBUF:
                    turn_rows(last, i + 2)

        @block.scalar
        def _(act):
            act.wait_ge(weights_in, (NWEIGHTS - 1) * 16)
            act.sem_inc(freed_act, dense.reads["A"])

            def xT_copy(b, layer):
                for k in range(KD):
                    dense.wait_filled(act, b, "xT", layer, k)
                    if layer == 3:
                        act.activation(xnT[:, k, S:], dense.bank("xT", layer, k)[:, 0:SINKS], ACT.Copy)
                    act.activation(xnT[:, k, 0:S], dense.bank("xT", layer, k)[:], ACT.Copy).then_inc(freed_act, 1)

            def qn_copy(b, g, j):
                dense.wait_filled(act, b, "qn", g, j)
                if g >= 2 and j == 0:
                    act.wait_ge(scores_ready, b * 2 * UNITS + 16 * (g - 1))
                act.activation(qT[0:QN, g % 2, j, :], dense.bank("qn", g, j)[0:QN, :], ACT.Copy,
                               scale=float(QN + QR) ** -0.5).then_inc(freed_act, 1)

            def attention(b, layer):
                for s in range(UNITS + LAG + 3):
                    copy_turned(act, "A", b, layer, s - LAG - 1)
                    if s < UNITS:
                        h, t, lo, hi = unit_of(layer, s)
                        u = layer * UNITS + s
                        act.wait_ge(max_ready, b * 2 * UNITS + u + 1)
                        if u >= NPROB:
                            act.wait_ge(turned, b * 2 * UNITS + u - NPROB + 1)
                        act.activation(probs[:, u % NPROB, lo:hi], score_banks[u % 3][:, lo:hi], ACT.Exp,
                                       bias=nmax[:, u % 4:u % 4 + 1], accum_out=den[:, u % NPROB:u % NPROB + 1])\
                            .then_inc(probs_ready, 1)
                    g, r = divmod(s, 16)
                    if r == LAG + 2 and g >= 1:
                        act.wait_ge(heads_out, b * 2 * TILES + layer * TILES + NT * g)
                        if g == 1 and layer == 1:
                            dense.wait_filled(act, b, "o0", NT - 1)
                        act.activation(attnT[:, g - 1, :], out_bank[:], ACT.Copy).then_inc(attn_ready, 1)
                    if layer == 0 and g + 1 < G0 and r in (9, 11, 13, 15):
                        qn_copy(b, g + 1, (r - 9) // 2)

            with act.Fori(0, B) as b:
                xT_copy(b, 1)
                for c in range(2):
                    dense.wait_filled(act, b, "cT", c)
                    act.activation(cT[:, c, :], dense.bank("cT", c)[:], ACT.Copy, scale=gam_sb[:, c:c + 1]).then_inc(freed_act, 1)
                dense.wait_filled(act, b, "v0")
                act.activation(v0[:].rearrange("p t n -> p (t n)"), dense.bank("v0")[:], ACT.Copy).then_inc(freed_act, 1)
                for g in range(G0):
                    dense.wait_filled(act, b, "kn", g)
                    act.activation(kT[0:KN, g, :], dense.bank("kn", g)[0:KN, :], ACT.Copy).then_inc(freed_act, 1)
                for j in range(HG):
                    qn_copy(b, 0, j)
                attention(b, 0)
                xT_copy(b, 2)
                for hf in range(HALVES):
                    for i in range(PLANES):
                        dense.wait_filled(act, b, "gate", i, hf)
                        n = hf * PLANES + i
                        if n >= 2:
                            dense.wait_read(act, b, "up", (n - 2) % PLANES, (n - 2) // PLANES)
                        act.activation(sg[:, i % 2, :], dense.bank("gate", i, hf)[:], ACT.Silu).then_inc(freed_act, 1)
                        dense.wait_read(act, b, "up", i, hf)
                        act.activation(ha[:, i, :], hp[:, i, :], ACT.Abs).then_inc(abs_ready, 1)
                xT_copy(b, 3)
                for c in range(4):
                    dense.wait_read(act, b, "qk", c)
                    act.activation(qk_split[:, c, 0, :], qk32[:, c % 2, :], ACT.Copy).then_inc(qk_hi_ready, 1)
                attention(b, 1)
                xT_copy(b, 4)
                dense.wait_filled(act, b, "logit")
                act.activation(logits[:, bass.ds(b * NT, NT), :].rearrange("p t e -> p (t e)"),
                               dense.bank("logit")[:, 0:NT * E], ACT.Copy).then_inc(freed_act, 1)
                for c in range(NSI):
                    dense.wait_filled(act, b, "sg", c)
                    if c >= 2:
                        dense.wait_read(act, b, "su", c - 2)
                    act.activation(ssg[:, c % 2, :], dense.bank("sg", c)[0:IC, :], ACT.Silu).then_inc(freed_act, 1)

            act.wait_ge(y_out, (B + 1) * 16)
            act.wait_ge(m_exp, 1)
            act.activation(sc[:], hit[:, 0], ACT.Exp).then_inc(m_exp, 1)
            act.sem_inc(e_xT, 2)

            def copy_rows(ep, i):
                act.wait_ge(e_turned, ep * NBUF + i + 1)
                act.activation(xgT[:, i % 2].rearrange("p k n -> p (k n)"), row_banks[i % 2][:], ACT.Copy).then_inc(e_xT, 1)

            def gate(ep, i):
                act.wait_ge(e_up, ep * NBUF + i + 1)
                act.activation(eg[:, i % 2].rearrange("p k n -> p (k n)"), gate_banks[i % 2][0:IC, :], ACT.Silu).then_inc(e_gate, 1)

            copy_rows(0, 0)
            with act.Fori(0, E // NBUF - 1) as ep:
                for i in range(NBUF):
                    gate(ep, i)
                    copy_rows(ep, i + 1)
            for i in range(NBUF):
                gate(E // NBUF - 1, i)
                if i + 1 < NBUF:
                    copy_rows(E // NBUF - 1, i + 1)

        @block.vector
        def _(dve):
            dve.wait_ge(weights_in, (NWEIGHTS - 1) * 16)
            dve.sem_inc(freed_dve, dense.reads["V"])
            for w in (wkr_sb[:].rearrange("p r k n -> p r (k n)"), wqr_sb[:].rearrange("p r g n -> p r (g n)")):
                a, r = (w[:, i, :].rearrange("p (m two) -> p m two", two=2) for i in range(2))
                dve.tensor_scalar(r[:, :, 0], a[:, :, 1], -1.0, None, ALU.mult)
                last = dve.tensor_copy(r[:, :, 1], a[:, :, 0])
            last.then_inc(consts_made, 1)
            dve.tensor_scalar(bqk1_sb[:, 0, :], bqk1_sb[:, 0, :], float(HD1) ** -0.5, None, ALU.mult).then_inc(consts_made, 1)
            dve.wait_ge(consts_made, 2)

            def norm(b, n, ch, src, dst, count, width):
                for i in range(count):
                    if i == count - 1:
                        ch.link(dve.bn_stats(stats[:, i, :], src(i)))
                    else:
                        dve.bn_stats(stats[:, i, :], src(i))
                dve.sem_inc(spare, 1)
                for i in range(count):
                    if i == count - 1:
                        ch.link(dve.bn_aggr(mv[:, i, :], stats[:, i, :]))
                    else:
                        dve.bn_aggr(mv[:, i, :], stats[:, i, :])
                dve.tensor_scalar(vare[:, 0:count], mv[:, 0:count, 1], EPS, None, ALU.add).then_inc(var_ready, 1)
                dve.wait_ge(rstd_ready, b * 5 + n)
                for i in range(count):
                    ins = dve.tensor_scalar(dst(i), src(i), mv[:, i, 0:1], rstd[:, i:i + 1], ALU.subtract, ALU.mult)
                    if count == NT:
                        ins.then_inc(xn_ready, 1)
                return ins

            def q_rope(b, g, ch):
                for r in range(2):
                    dense.wait_filled(dve, b, "qr", g, r)
                    if r == 0 and g >= 1:
                        dve.wait_ge(rope_moved, b * H0 * 16 + 64 * g)
                    dve.tensor_tensor(rp[:, 1 + r, :], dense.bank("qr", g, r)[:], rope_q[:, r, :], ALU.mult).then_inc(freed_dve, 1)
                ch.link(dve.drain())
                dve.tensor_tensor(rp[:, 0, :], rp[:, 1, :], rp[:, 2, :], ALU.add).then_inc(rope_ready, 1)

            def attention(b, layer, ch):
                for s in range(UNITS + LAG + 2):
                    if s < UNITS:
                        h, t, lo, hi = unit_of(layer, s)
                        u = layer * UNITS + s
                        dve.wait_ge(scores_ready, b * 2 * UNITS + u + 1)
                        if u >= 4:
                            dve.wait_ge(probs_ready, b * 2 * UNITS + u - 3)
                        dve.tensor_reduce(nmax[:, u % 4:u % 4 + 1], score_banks[u % 3][:, lo:hi], AX.X, ALU.max, negate=True)\
                            .then_inc(max_ready, 1)
                    d = s - DIVLAG
                    u = layer * UNITS + d
                    if 0 <= d < UNITS:
                        dve.wait_ge(probs_ready, b * 2 * UNITS + u + 1)
                        if u >= NPROB:
                            normed.wait(dve, b, u - NPROB)
                        dve.reciprocal(rden[:, u % NPROB:u % NPROB + 1], den[:, u % NPROB:u % NPROB + 1]).then_inc(rden_ready, 1)
                    copy_turned(dve, "V", b, layer, s - LAG - 1)
                    if 0 <= d < UNITS and normed.who[u] == "V":
                        dve.wait_ge(rden_ready, b * 2 * UNITS + u + 1)
                        normalise(dve, b, layer, d)
                    g, r = divmod(s, 16)
                    if layer == 0 and g + 1 < G0 and r == 7:
                        q_rope(b, g + 1, ch)

            def residual(b, name, ch, bias=None):
                for t in range(NT):
                    dense.wait_filled(dve, b, name, t)
                    ins = dve.tensor_tensor(xb[:, t, :], xb[:, t, :], dense.bank(name, t)[:, 0:D], ALU.add)
                    ins.then_inc(freed_dve, 1)
                ch.link(dve.drain())

            with dve.Fori(0, B) as b:
                ch = Chain(dve, dve_chain, b, DVE_LINKS)
                dve.wait_ge(x_in, (b + 1) * 16)
                dve.wait_ge(rows_out, (b + 1) * 16)
                norm(b, 1, ch, lambda i: xb[:, i, :], lambda i: xn[:, i, :], NT, D)
                for t in range(NT):
                    dense.wait_filled(dve, b, "proj", t)
                    ins = dve.tensor_copy(lat[:, t, :], dense.bank("proj", t)[:, 0:2 * CQ])
                    ins.then_inc(freed_dve, 1)
                ch.link(dve.drain())
                norm(b, 2, ch, lambda i: lat[:, i // 2, (i % 2) * CQ:(i % 2 + 1) * CQ], lambda i: cn[:, i // 2, (i % 2) * CQ:(i % 2 + 1) * CQ], 2 * NT, CQ)
                dve.drain().then_inc(xn_ready, NT)
                for r in range(2):
                    dense.wait_filled(dve, b, "kr", r)
                    dve.tensor_tensor(rp[KN:P, 1 + r, :], dense.bank("kr", r)[KN:P, :], rope_k[KN:P, r, :], ALU.mult).then_inc(freed_dve, 1)
                ch.link(dve.drain())
                dve.tensor_tensor(kT[KN:P, 0, :], rp[KN:P, 1, :], rp[KN:P, 2, :], ALU.add).then_inc(kr_ready, 1)
                dve.wait_ge(kr_ready, b + 1)
                q_rope(b, 0, ch)
                attention(b, 0, ch)
                residual(b, "o0", ch)
                norm(b, 3, ch, lambda i: xb[:, i, :], lambda i: xn[:, i, :], NT, D)
                for hf in range(HALVES):
                    for i in range(PLANES):
                        dense.wait_filled(dve, b, "up", i, hf)
                        dense.wait_read(dve, b, "gate", i, hf)
                        if hf == 1:
                            dve.wait_ge(abs_ready, b * 8 + i + 1)
                        dve.tensor_tensor(hp[:, i, :], dense.bank("up", i, hf)[:], sg[:, i % 2, :], ALU.mult).then_inc(freed_dve, 1)
                    dve.wait_ge(abs_ready, b * 8 + (hf + 1) * PLANES)
                    flat = lambda a: a.rearrange("p a n -> p (a n)")
                    dve.tensor_tensor(flat(wins[:, 0:3, :]), flat(ha[:, 0:3, :]), flat(ha[:, 1:4, :]), ALU.is_ge)
                    dve.tensor_tensor(flat(wins[:, 3:5, :]), flat(ha[:, 0:2, :]), flat(ha[:, 2:4, :]), ALU.is_ge)
                    ch.link(dve.tensor_tensor(wins[:, 5, :], ha[:, 0, :], ha[:, 3, :], ALU.is_ge))
                    w01, w12, w23, w02, w13, w03 = (wins[:, n, :] for n in range(6))
                    dve.tensor_tensor(wsum[:, 0, :], w01, w02, ALU.add)
                    dve.tensor_tensor(wsum[:, 1, :], w12, w13, ALU.add)
                    dve.tensor_tensor(wsum[:, 2, :], w23, w02, ALU.subtract)
                    ch.link(dve.tensor_tensor(wsum[:, 3, :], w13, w23, ALU.add))
                    dve.tensor_tensor(wsum[:, 0, :], wsum[:, 0, :], w03, ALU.add)
                    dve.tensor_tensor(wsum[:, 1, :], wsum[:, 1, :], w01, ALU.subtract)
                    dve.tensor_tensor(wsum[:, 2, :], wsum[:, 2, :], w12, ALU.subtract)
                    ch.link(dve.tensor_tensor(wsum[:, 3, :], wsum[:, 3, :], w03, ALU.add))
                    for i, (bound, op) in enumerate(((2.0, ALU.is_ge), (1.0, ALU.is_ge), (0.0, ALU.is_ge), (1.0, ALU.is_le))):
                        ins = dve.scalar_tensor_tensor(hT[:, 2 * i + hf, :], wsum[:, i, :], bound, hp[:, i, :], op, ALU.mult)
                    ins.then_inc(hT_ready, 1)
                    dve.wait_ge(hT_ready, b * 2 + hf + 1)
                residual(b, "down", ch)
                norm(b, 4, ch, lambda i: xb[:, i, :], lambda i: xn[:, i, :], NT, D)
                for c in range(4):
                    dense.wait_filled(dve, b, "qk", c)
                    if c >= 2:
                        dve.wait_ge(qk_hi_ready, b * 4 + c - 1)
                    dve.tensor_scalar(qk32[:, c % 2, :], dense.bank("qk", c)[:], float(HD1) ** -0.5 if c < 2 else 1.0,
                                      bqk1_sb[:, c // 2, c % 2:c % 2 + 1], ALU.mult, ALU.add).then_inc(freed_dve, 1)
                    dve.wait_ge(qk_hi_ready, b * 4 + c + 1)
                    dve.tensor_tensor(qk_split[:, c, 1, :], qk32[:, c % 2, :], qk_split[:, c, 0, :].bitcast(F32), ALU.subtract).then_inc(qk_lo_ready, 1)
                for t in range(NT):
                    dense.wait_filled(dve, b, "v1", t)
                    dve.tensor_tensor(v1[:, t, :], dense.bank("v1", t)[:], bv1_sb[:], ALU.add).then_inc(freed_dve, 1)
                attention(b, 1, ch)
                for t in range(NT):
                    dve.tensor_tensor(xb[:, t, :], xb[:, t, :], bo1_sb[:], ALU.add)
                ch.link(dve.drain())
                residual(b, "o1", ch)
                norm(b, 5, ch, lambda i: xb[:, i, :], lambda i: xn[:, i, :], NT, D)
                for c in range(NSI):
                    dense.wait_filled(dve, b, "su", c)
                    dense.wait_read(dve, b, "sg", c)
                    dve.tensor_tensor(shT[:, c, :], dense.bank("su", c)[0:IC, :], ssg[:, c % 2, :], ALU.mult).then_inc(freed_dve, 1)
                residual(b, "sdown", ch)
                dve.drain().then_inc(res_ready, 4)
                ch.done()

            ch = Chain(dve, m_chain)
            dense.wait_read(dve, B - 1, "logit")
            dve.wait_ge(y_out, (B + 1) * 16)
            NTT = B * NT
            wide = lambda a: a.unsqueeze(2).to_broadcast([P, NTT, E])
            ch.link(dve.tensor_reduce(rsum[:], logits[:], AX.X, ALU.max))
            dve.tensor_tensor(hit[:, 0], logits[:], wide(rsum[:]), ALU.subtract).then_inc(m_exp, 1)
            dve.wait_ge(m_exp, 2)
            ch.link(dve.tensor_reduce(rsum[:], sc[:], AX.X, ALU.add))
            ch.link(dve.reciprocal(rrec[:], rsum[:]))
            ch.link(dve.tensor_tensor(sc[:], sc[:], wide(rrec[:]), ALU.mult))
            for t in range(NTT):
                last = dve.max(top[:, t, :], sc[:, t, :])
            ch.link(last)
            for t in range(NTT):
                last = dve.max_index(topi[:, t, :], top[:, t, :], sc[:, t, :])
            ch.link(last)
            dve.drain().then_inc(m_mask, 1)
            ch.link(dve.tensor_copy(topf[:], topi[:]))
            iota_e = small_sb[:, 0:E].unsqueeze(1).to_broadcast([P, NTT, E])
            ch.link(dve.tensor_tensor(hit[:, 0], iota_e, topf[:, :, 0:1].to_broadcast([P, NTT, E]), ALU.is_equal))
            for k in range(1, TOPK):
                ch.link(dve.tensor_tensor(hit[:, 1], iota_e, topf[:, :, k:k + 1].to_broadcast([P, NTT, E]), ALU.is_equal))
                ch.link(dve.tensor_tensor(hit[:, 0], hit[:, 0], hit[:, 1], ALU.add))
            dve.memset(ones_b[:], 1.0)
            ch.link(dve.tensor_copy(mask_b[:], hit[:, 0]))
            dve.drain().then_inc(m_mask, 1)
            pos = banks[0][:].rearrange("p (t e) -> p t e", e=E)
            dve.wait_ge(m_pos, 1)
            ch.link(dve.tensor_copy(posi[:, 0], pos))
            dve.tensor_single_scalar(posi[:, 1], posi[:, 0], 4, ALU.arith_shift_right)
            ch.link(dve.tensor_single_scalar(posi[:, 2], posi[:, 0], 15, ALU.bitwise_and))
            dve.tensor_copy(posf[:, 0], posi[:, 1])
            ch.link(dve.tensor_copy(posf[:, 1], posi[:, 2]))
            ch.link(dve.scalar_tensor_tensor(posf[:, 0], hit[:, 0], -1000.0, posf[:, 0], ALU.mult, ALU.add))
            ch.link(dve.tensor_scalar(posf[:, 0], posf[:, 0], 1000.0, None, ALU.add))
            iota16 = small_sb[:, 32:48].unsqueeze(1).to_broadcast([P, NTT * E, 16])
            for half, hot in ((0, onehot_a), (1, onehot_b)):
                col = posf[:, half].rearrange("p t e -> p (t e)").unsqueeze(2).to_broadcast([P, NTT * E, 16])
                last = dve.tensor_tensor(hot[:].rearrange("p t (e s) -> p (t e) s", s=16), iota16, col, ALU.is_equal)
            ch.link(last)
            dve.tensor_scalar(val_b[:, 0].rearrange("p t n -> p (t n)"), onehot_b[:].rearrange("p t n -> p (t n)"),
                              small_sb[:, 80:81], None, ALU.mult)
            for t in range(NTT):
                last = dve.tensor_scalar(val_b[:, 1, t, :], onehot_b[:, t, :], float(t + 1), None, ALU.mult)
            last.then_inc(m_hots, 1)
            dve.wait_ge(m_tab, 1)
            for g in range(4):
                last = dve.tensor_tensor(tabm[:, g, :].rearrange("p (v e s) -> p v e s", v=2, s=16),
                                         banks[1 + g][:, 0:256].rearrange("p (v e s) -> p v e s", v=2, s=16),
                                         small_sb[:, 64:72].unsqueeze(1).unsqueeze(3).to_broadcast([P, 2, 8, 16]), ALU.mult)
            ch.link(last)
            ch.link(dve.tensor_reduce(tab[:].rearrange("p g v s -> p (g v) s"),
                                      tabm[:].rearrange("p g (v e s) -> p (g v) s e", v=2, s=16), AX.X, ALU.add))
            ch.link(dve.tensor_scalar(tabs[:, :, 0, :], tab[:, :, 1, :], float(P), float(-P), ALU.mult, ALU.add))
            ch.link(dve.tensor_tensor(tabs[:, :, 0, :], tabs[:, :, 0, :], tab[:, :, 0, :], ALU.add))
            ch.link(dve.tensor_scalar(tabs[:, :, 0, :], tabs[:, :, 0, :], 0.0, None, ALU.max))
            ch.link(dve.tensor_scalar(tabs[:, :, 1, :], tab[:, :, 1, :], 0.0, None, ALU.is_equal))
            ch.link(dve.tensor_tensor(tabs[:, :, 2, :], tabs[:, :, 1, :],
                                      small_sb[:, 48:64].unsqueeze(1).to_broadcast([P, 4, 16]), ALU.mult))
            ch.link(dve.tensor_tensor(tabs[:, :, 2, :], tabs[:, :, 2, :], tabs[:, :, 0, :], ALU.add))
            dve.tensor_copy(tab_i[:, 0], tabs[:, :, 0, :])
            ch.link(dve.tensor_copy(tab_i[:, 1], tabs[:, :, 2, :]))
            dve.drain().then_inc(m_tab_i, 1)
            dve.sem_inc(e_y, 2)
            dve.sem_inc(e_h, 2)

            def up_gate(ep, i):
                dve.wait_ge(e_gate, ep * NBUF + i + 1)
                dve.tensor_tensor(eh[:, i % 2].rearrange("p k n -> p (k n)"), up_banks[i % 2][0:IC, :],
                                  eg[:, i % 2].rearrange("p k n -> p (k n)"), ALU.mult).then_inc(e_h, 1)

            def weigh(ep, i):
                e = ep * NBUF + i
                dve.wait_ge(e_down, e + 1)
                dve.wait_ge(e_settled, e + 1)
                dve.sem_inc(spare, 1)
                score = slice(D + e, D + e + 1) if isinstance(e, int) else bass.ds(ep * NBUF + (D + i), 1)
                for hf in range(2):
                    last = dve.tensor_scalar(yo[:, i, hf, :], y_banks[i % 2][:, hf * D:(hf + 1) * D],
                                             xg[:, i, hf, score], None, ALU.mult)
                last.then_inc(e_y, 1)

            up_gate(0, 0)
            with dve.Fori(0, E // NBUF - 1) as ep:
                for i in range(NBUF):
                    up_gate(ep, i + 1)
                    weigh(ep, i)
            for i in range(NBUF):
                if i + 1 < NBUF:
                    up_gate(E // NBUF - 1, i + 1)
                weigh(E // NBUF - 1, i)
            for q in range(4):
                dve.wait_ge(f_in[q % 2], 64 * (q // 2 + 1))
                a = [fin[:, q % 2, i].rearrange("p t d -> p (t d)") for i in range(4)]
                dve.tensor_tensor(a[0], a[0], a[1], ALU.add)
                ch.link(dve.tensor_tensor(a[2], a[2], a[3], ALU.add))
                dve.tensor_tensor(a[0], a[0], a[2], ALU.add).then_inc(f_sum, 1)

        @block.gpsimd
        def _(pool):
            pool.memset(zeros[:], 0.0).then_inc(pool_chain, 1)
            pool.memset(mhalf[:], -0.5).then_inc(pool_chain, 1)
            pool.wait_ge(pool_chain, 2)
            wide = lambda n: zeros[:].unsqueeze(1).to_broadcast([P, n, D])
            pool.dma_start(y_sum[0][T:YROWS, :], zeros[:]).then_inc(y_zeroed, 16)
            for i in range(1, 4):
                pool.dma_start(y_sum[i].rearrange("(t p) d -> p t d", p=P), wide(YROWS // P)).then_inc(y_zeroed, 16)

            def rstd_of(b, n, count):
                pool.wait_ge(var_ready, b * 5 + n)
                pool.tensor_tensor(rstd[:, 0:count], vare[:, 0:count], mhalf[:, 0:count], ALU.pow).then_inc(rstd_ready, 1)

            def attention(b, layer):
                for s in range(UNITS):
                    u = layer * UNITS + s
                    if normed.who[u] == "P":
                        pool.wait_ge(rden_ready, b * 2 * UNITS + u + 1)
                        pool.sem_inc(spare, 1)
                        normalise(pool, b, layer, s)

            with pool.Fori(0, B) as b:
                rstd_of(b, 1, NT)
                rstd_of(b, 2, 2 * NT)
                pool.wait_ge(kr_ready, b + 1)
                pool.sem_inc(spare, 1)
                for g in range(1, G0):
                    last = pool.tensor_copy(kT[KN:P, g, :], kT[KN:P, 0, :])
                last.then_inc(kr_copied, 1)
                attention(b, 0)
                rstd_of(b, 3, NT)
                rstd_of(b, 4, NT)
                dense.wait_filled(pool, b, "down", NT - 1)
                pool.wait_ge(rstd_ready, b * 5 + 4)
                pool.sem_inc(spare, 1)
                pool.memset(q_st[64:QK_ROWS].rearrange("p a j n -> p (a j n)").bitcast(F32), 0.0).then_inc(pool_chain, 1)
                pool.wait_ge(pool_chain, b + 3)
                pool.sem_inc(spare, 1)
                pool.memset(k_st[64:QK_ROWS].rearrange("p a j n -> p (a j n)").bitcast(F32), 0.0).then_inc(stack_zeroed, 1)
                attention(b, 1)
                rstd_of(b, 5, NT)

            pool.wait_ge(y_zeroed, 64)
            pool.wait_ge(m_w_out, 16)
            pool.wait_ge(m_slots, 64)

            def gather(i):
                for hf in range(2):
                    pool.indirect_dma_start(xg[:, i, hf, :], None, xn_rows,
                                            bass.IndirectOffsetOnAxis(ap=slot_now[:, i, 0, hf:hf + 1], axis=0),
                                            bounds_check=T - 1, oob_is_err=True).then_inc(e_rows[i], 16)

            def add_rows(ep, i, more):
                e = ep * NBUF + i
                pool.wait_ge(e_y, e + 3)
                pool.wait_ge(e_settled, e + 3)
                pool.sem_inc(spare, 1)
                at = slice(e + NBUF, e + NBUF + 1) if isinstance(e, int) else bass.ds(ep * NBUF + (NBUF + i), 1)
                kinds = slice(0 if more else 1, 2)
                pool.tensor_copy(slot_now[:, i, kinds], slots[:, at, kinds].rearrange("p o k h -> p (o k) h")).then_inc(idx_ready, 1)
                pool.wait_ge(idx_ready, e + 2)
                pool.sem_inc(spare, 1)
                for hf in range(2):
                    pool.indirect_dma_start(y_sum[i % 2 * 2 + hf],
                                            bass.IndirectOffsetOnAxis(ap=slot_now[:, i, 1, hf:hf + 1], axis=0),
                                            yo[:, i, hf, :], None, bounds_check=YROWS - 1, oob_is_err=True,
                                            compute_op=ALU.add).then_inc(e_added[i], 16)
                if more:
                    gather(i)

            pool.sem_inc(e_settled, NBUF)
            pool.tensor_copy(slot_now[:, :, 0, :], slots[:, 0:NBUF, 0, :]).then_inc(idx_ready, 1)
            pool.wait_ge(idx_ready, 1)
            for i in range(NBUF):
                gather(i)
            with pool.Fori(0, E // NBUF - 1) as ep:
                for i in range(NBUF):
                    add_rows(ep, i, True)
            for i in range(NBUF):
                add_rows(E // NBUF - 1, i, False)
            for done in e_added:
                pool.wait_ge(done, 32 * E // NBUF)


def kernel(**inputs):
    import ml_dtypes
    import numpy as np
    from concourse import bacc
    from concourse.bass_utils import run_bass_kernel_spmd

    i = {k: np.asarray(v) for k, v in inputs.items()}
    f = np.float32
    w_dkv = i["L0_attn_w_dkv"]
    w_ukv = i["L0_attn_w_ukv"]

    def planes(w):
        return w.reshape(w.shape[0], FF // 4, 4).transpose(0, 2, 1).reshape(w.shape[0], FF)

    def pad_heads(w):
        o = np.zeros((H1, 32) + w.shape[1:], w.dtype)
        o[:, :HD1] = w.reshape((H1, HD1) + w.shape[1:])
        return o.reshape((H1 * 32,) + w.shape[1:])

    def rope(dim, rows):
        inv = (1.0 / f(10000.0) ** (np.arange(0, dim, 2, dtype=f) / f(dim))).astype(f)
        ang = np.arange(S, dtype=f)[:, None] * inv
        c = np.repeat(np.cos(ang).astype(f).T, 2, axis=0), np.repeat(np.sin(ang).astype(f).T, 2, axis=0)
        return [np.tile(a, (rows // dim, 1)) for a in c]

    cos_q, sin_q = (a * f((QN + QR) ** -0.5) for a in rope(QR, P))
    cos_k, sin_k = rope(KR, P)
    bf = ml_dtypes.bfloat16
    r, c = np.arange(P)[:, None], np.arange(S)[None, :]
    small = np.zeros((P, 96), f)
    small[:, 0:32] = np.arange(32)
    small[:, 32:48] = np.arange(16)
    small[:, 48:64] = DUMMY + (r % 8) * 16 + np.arange(16)
    small[:, 64:72] = (r // 16 == np.arange(8))
    small[:, 80] = np.arange(P)
    arrays = {
        "x": i["L0_attn_x"].reshape(T, D),
        "w_proj": np.concatenate([i["L0_attn_w_dq"], w_dkv[:, :CQ]], axis=1),
        "w_kr": np.concatenate([np.zeros((D, KN), f), w_dkv[:, CQ:]], axis=1),
        "gamma_q": i["L0_attn_gamma_q"].reshape(CQ, 1), "gamma_kv": i["L0_attn_gamma_kv"].reshape(CQ, 1),
        "w_qn": i["L0_attn_w_uq"][:, :H0 * QN], "w_qr": i["L0_attn_w_uq"][:, H0 * QN:],
        "w_uk": w_ukv[:, :G0 * KN], "w_uv": w_ukv[:, G0 * KN:], "w_o0": i["L0_attn_w_o"],
        "w_gate": planes(i["L0_ffn_w_gate"]), "w_up": planes(i["L0_ffn_w_up"]), "w_down": planes(i["L0_ffn_w_down"].T).T,
        "w_q1": i["L1_attn_Wq"].T, "w_k1": i["L1_attn_Wk"].T,
        "w_v1": pad_heads(i["L1_attn_Wv"]).T, "w_o1": pad_heads(i["L1_attn_Wo"].T),
        "b_q1": i["L1_attn_bq"].reshape(KD, P).T, "b_k1": i["L1_attn_bk"].reshape(KD, P).T,
        "b_v1": pad_heads(i["L1_attn_bv"]).reshape(1, 512), "b_o1": i["L1_attn_bo"].reshape(1, D),
        "gate_w": i["L1_ffn_gate_w"].T, "w1": i["L1_ffn_w1"], "w2": i["L1_ffn_w2"], "w3": i["L1_ffn_w3"],
        "sw1": i["L1_ffn_sw1"], "sw2": i["L1_ffn_sw2"], "sw3": i["L1_ffn_sw3"],
        "cos_q": cos_q, "sin_q": sin_q, "cos_k": cos_k, "sin_k": sin_k,
        "ident": np.eye(P, dtype=f), "identb": np.eye(P, dtype=f).astype(bf),
        "causal": np.where(c[:, :P] > r, f(-1e30), f(0)).astype(bf),
        "window": np.where(c[:, :WCOLS] < r + P - WINDOW - SINKS, f(-1e30), f(0)).astype(bf),
        "tri": (r < c[:, :P]).astype(bf), "small": small,
    }
    nc = bacc.Bacc("TRN2", target_bir_lowering=False, num_devices=1)
    args, ins = {}, {}
    for name, a in arrays.items():
        a = np.ascontiguousarray(a)
        ins[f"in_{name}"] = a
        args[name] = nc.dram_tensor(f"in_{name}", a.shape, mybir.dt.from_np(a.dtype), kind="ExternalInput").ap()
    args["out"] = nc.dram_tensor("out_0", (T, D), F32, kind="ExternalOutput").ap()
    build(nc, **args)
    res = run_bass_kernel_spmd(nc, [ins], core_ids=[0])
    return res.results[0]["out_0"].reshape(B, S, D)
```

```python
from contextlib import ExitStack

import concourse.bass as bass
from concourse import mybir

F32 = mybir.dt.float32
F32R = mybir.dt.float32r
BF16 = mybir.dt.bfloat16
I32 = mybir.dt.int32
U32 = mybir.dt.uint32
ALU = mybir.AluOpType
ACT = mybir.ActivationFunctionType
AX = mybir.AxisListType

P = 128
B, S, D = 4, 512, 256
T = B * S
NT = S // P
KD = D // P
EPS = 1e-5
H0, G0, QN, QR, KN, KR, VD0 = 16, 4, 96, 32, 64, 64, 32
CQ = 128
HG = H0 // G0
FF = 1024
PLANES, HALVES = 4, 2
H1, HD1, WINDOW, SINKS = 16, 16, 64, 4
QK_ROWS = 96
E, TOPK, INTER, CAP = 32, 6, 176, 256
IC = 88
NI = INTER // IC
SI = 2 * INTER
NSI = SI // IC
SMALL = 112
NBUF = 4
ROW = D + E
DUMMY = T
YROWS = T + P
WCOLS = 2 * P - 1 - WINDOW - SINKS
TILES = G0 * NT
QK_ORDER = (0, 2, 1, 3)
UNITS = H0 * NT
DIVLAG = 2
LAG = 6
PVLAG = LAG + 1
NPROB = 8


def shares(*patterns):
    return [p[u % len(p)] for p in patterns for u in range(UNITS)]


class Shared:

    def __init__(self, who, signals):
        self.who, self.signals = who, signals
        self.total = {w: who.count(w) for w in signals}

    def wait(self, eng, b, u):
        w = self.who[u]
        eng.wait_ge(self.signals[w], b * self.total[w] + self.who[:u + 1].count(w))

    def wait_up_to(self, eng, b, u):
        for w, signal in self.signals.items():
            eng.wait_ge(signal, b * self.total[w] + self.who[:u + 1].count(w))

    def done(self, ins, u):
        ins.then_inc(self.signals[self.who[u]], 1)


def dense_units():
    u = [(("xT", 1, k), "AV"[k]) for k in range(KD)]
    u += [(("proj", t), "V") for t in range(NT)]
    u += [(("kr", r), "V") for r in range(2)]
    u += [(("cT", c), "A") for c in range(2)]
    u += [(("qr", 0, r), "V") for r in range(2)]
    u += [(("v0",), "A")]
    u += [(("kn", g), "A") for g in range(G0)]
    for g in range(G0):
        if g:
            u += [(("qr", g, r), "V") for r in range(2)]
        u += [(("qn", g, j), "A") for j in range(HG)]
    u += [(("o0", t), "V") for t in range(NT)]
    u += [(("xT", 2, k), "AV"[k]) for k in range(KD)]
    for hf in range(HALVES):
        for i in range(PLANES):
            u += [(("gate", i, hf), "A"), (("up", i, hf), "V")]
    u += [(("down", t), "V") for t in range(NT)]
    u += [(("xT", 3, k), "AV"[k]) for k in range(KD)]
    u += [(("qk", c), "V") for c in QK_ORDER]
    u += [(("v1", t), "V") for t in range(NT)]
    u += [(("o1", t), "V") for t in range(NT)]
    u += [(("xT", 4, k), "AV"[k]) for k in range(KD)]
    u += [(("logit",), "A")]
    for c in range(NSI):
        u += [(("sg", c), "A"), (("su", c), "V")]
    u += [(("pos",), "V"), (("count",), "V")]
    u += [(("sdown", t), "V") for t in range(NT)]
    u += [(("table", n), "V") for n in range(2)]
    return u


class DenseRing:

    def __init__(self, banks, filled, freed):
        units = dense_units()
        self.filled, self.freed = filled, freed
        self.n = {name: i for i, (name, _) in enumerate(units)}
        self.by = [who for _, who in units]
        self.total = len(units)
        self.reads = {w: self.by.count(w) for w in "AV"}
        self.banks, turn = [], [0, 0]
        for name, _ in units:
            beside = name[0] in ("qr", "qn") and name[1] > 0
            ring = banks[6:8] if beside else banks[6:8] + banks[0:6]
            self.banks.append(ring[turn[beside] % len(ring)])
            turn[beside] += 1

    def bank(self, *name):
        return self.banks[self.n[name]]

    def wait_free(self, pe, b, *name):
        n = self.n[name]
        m = next(m for m in range(n - 1, n - 1 - self.total, -1) if self.banks[m % self.total] is self.banks[n])
        base = b + 1 if m >= 0 else b
        m %= self.total
        who = self.by[m]
        pe.wait_ge(self.freed[who], base * self.reads[who] + self.by[:m + 1].count(who))

    def wait_read(self, eng, b, *name):
        n = self.n[name]
        who = self.by[n]
        eng.wait_ge(self.freed[who], (b + 1) * self.reads[who] + self.by[:n + 1].count(who))

    def wait_filled(self, eng, b, *name):
        eng.wait_ge(self.filled, b * self.total + self.n[name] + 1)


class Chain:

    def __init__(self, eng, sem, b=0, per_pass=0, before=0):
        self.eng, self.sem, self.b, self.per_pass, self.before, self.n = eng, sem, b, per_pass, before, 0

    def link(self, ins):
        self.n += 1
        ins.then_inc(self.sem, 1)
        self.eng.wait_ge(self.sem, self.b * self.per_pass + (self.before + self.n))

    def done(self):
        assert self.n == self.per_pass, (self.n, self.per_pass)


def build(nc, x, w_proj, w_kr, gamma_q, gamma_kv, w_qn, w_qr, w_uk, w_uv, w_o0, w_gate, w_up, w_down,
          w_q1, w_k1, w_v1, w_o1, b_q1, b_k1, b_v1, b_o1, gate_w, w1, w2, w3, sw1, sw2, sw3,
          cos_q, sin_q, cos_k, sin_k, ident, identb, causal, window, tri, small, out):
    x_rows = x.rearrange("(b t p) d -> b p t d", b=B + 1, p=P)
    xn_rows = nc.dram_tensor("xn_rows", (T, ROW), F32).ap()
    q_parts = nc.dram_tensor("q_parts", (KD, P // HD1, 2, HD1, S), F32).ap()
    k_parts = nc.dram_tensor("k_parts", (KD, P // HD1, 4, HD1, S), F32).ap()

    ctx = ExitStack()
    with ctx:
        def sb(name, shape, dt=F32, stack=None):
            return (stack or ctx).enter_context(nc.sbuf_tensor(name, shape, dt))

        def sem(name):
            return ctx.enter_context(nc.semaphore(name))

        banks = [ctx.enter_context(nc.psum_tensor(f"bank{i}", [P, 512], F32)) for i in range(8)]
        score_banks, turn_banks, out_bank = banks[0:3], banks[3:5], banks[5]

        identity = sb("identity", [P, P])
        identity_bf = sb("identity_bf", [P, P], BF16)
        tri_sb = sb("tri_sb", [P, P], BF16)
        small_sb = sb("small_sb", [P, SMALL])
        ones_b = sb("ones_b", [P, P], BF16)
        seen = sb("seen", [P, E])
        table = sb("table", [P, 4, 2 * P])
        zeros = sb("zeros", [P, D])

        seq = ExitStack()
        wproj_sb = sb("wproj_sb", [P, KD, 2 * CQ], F32, seq)
        wkr_sb = sb("wkr_sb", [P, 2, KD, P], F32, seq)
        gam_sb = sb("gam_sb", [P, 2], F32, seq)
        wqn_sb = sb("wqn_sb", [P, H0, QN], F32, seq)
        wqr_sb = sb("wqr_sb", [P, 2, G0, P], F32, seq)
        wuk_sb = sb("wuk_sb", [P, G0, KN], F32, seq)
        wuv_sb = sb("wuv_sb", [P, G0 * VD0], F32, seq)
        wo0_sb = sb("wo0_sb", [P, G0, D], F32, seq)
        wgate_sb = sb("wgate_sb", [P, KD, FF], F32, seq)
        wup_sb = sb("wup_sb", [P, KD, FF], F32, seq)
        wdown_sb = sb("wdown_sb", [P, 8, D], F32, seq)
        wqk1_sb = sb("wqk1_sb", [P, 2, KD, D], F32, seq)
        bqk1_sb = sb("bqk1_sb", [P, 2, KD], F32, seq)
        wv1_sb = sb("wv1_sb", [P, KD, 512], F32, seq)
        wo1_sb = sb("wo1_sb", [P, 4, D], F32, seq)
        bv1_sb = sb("bv1_sb", [P, 512], F32, seq)
        bo1_sb = sb("bo1_sb", [P, D], F32, seq)
        gatew_sb = sb("gatew_sb", [P, KD, E], F32, seq)
        sw13_sb = sb("sw13_sb", [P, 2, KD, SI], F32, seq)
        sw2_sb = sb("sw2_sb", [IC, NSI, D], F32, seq)
        rope_q = sb("rope_q", [P, 2, S], F32, seq)
        rope_k = sb("rope_k", [P, 2, S], F32, seq)
        causal_sb = sb("causal_sb", [P, P], BF16, seq)
        window_sb = sb("window_sb", [P, WCOLS], BF16, seq)
        mhalf = sb("mhalf", [P, 8], F32, seq)

        xb = sb("xb", [P, NT, D], F32, seq)
        xnT = sb("xnT", [P, KD, S + SINKS], F32, seq)
        probs = sb("probs", [P, NPROB, S], F32, seq)
        xn = probs[:, 0:2, :].rearrange("p a (c n) -> p (a c) n", c=2)
        cn = probs[:, 2:4, :].rearrange("p a (c n) -> p (a c) n", c=2)
        probsT = sb("probsT", [P, 2, HG, NT, P], F32, seq)
        x_next = probs[:, 6:8, :].rearrange("p a (c n) -> p (a c) n", c=2)
        xn_next = probs[:, 4:6, :].rearrange("p a (c n) -> p (a c) n", c=2)
        sc = sb("sc", [P, NT, E], F32, seq)
        attnT = sb("attnT", [P, G0, S], F32, seq)
        stats = sb("stats", [P, 2 * NT, 6], F32, seq)
        mv = sb("mv", [P, 2 * NT, 2], F32, seq)
        vare = sb("vare", [P, 2 * NT], F32, seq)
        rstd = sb("rstd", [P, 2 * NT], F32, seq)
        nmax = sb("nmax", [P, 4], F32, seq)
        den = sb("den", [P, NPROB], F32, seq)
        rden = sb("rden", [P, NPROB], F32, seq)

        l0 = ExitStack()
        cT = sb("cT", [P, 2, S], F32, l0)
        qT = sb("qT", [P, 2, HG, S], F32, l0)
        kT = sb("kT", [P, G0, S], F32, l0)
        v0 = sb("v0_sb", [P, NT, G0 * VD0], F32, l0)
        rp = sb("rp", [P, 3, S], F32, l0)
        l0.close()
        ff = ExitStack()
        sg = sb("sg", [P, 2, S], F32, ff)
        hp = sb("hp", [P, PLANES, S], F32, ff)
        ha = sb("ha", [P, PLANES, S], F32, ff)
        wins = sb("wins", [P, 6, S], BF16, ff)
        wsum = sb("wsum", [P, 4, S], BF16, ff)
        hT = sb("hT", [P, 2 * PLANES, S], F32, ff)
        ff.close()
        l1 = ExitStack()
        qk32 = sb("qk32", [P, 2, S], F32, l1)
        qk_split = sb("qk_split", [P, 4, 2, S], F32R, l1)
        q_st = sb("q_st", [QK_ROWS, 2, HG, S], F32R, l1)
        k_st = sb("k_st", [QK_ROWS, 2, HG, S], F32R, l1)
        v1 = sb("v1_sb", [P, NT, H1 * 32], F32, l1)
        l1.close()
        sh = ExitStack()
        ssg = sb("ssg", [IC, 2, S], F32, sh)
        shT = sb("shT", [IC, NSI, S], F32, sh)
        onehot_a = sb("onehot_a", [P, NT, E * 16], BF16, sh)
        onehot_b = sb("onehot_b", [P, NT, E * 16], BF16, sh)
        val_b = sb("val_b", [P, 2, NT, E * 16], BF16, sh)
        rmax = sb("rmax", [P, NT], F32, sh)
        rsum = sb("rsum", [P, NT], F32, sh)
        rrec = sb("rrec", [P, NT], F32, sh)
        logits = sb("logits", [P, NT, E], F32, sh)
        shifted = sb("shifted", [P, NT, E], F32, sh)
        top = sb("top", [P, NT, 8], F32, sh)
        topi = sb("topi", [P, NT, 8], U32, sh)
        topf = sb("topf", [P, NT, 8], F32, sh)
        hits = sb("hits", [P, NT, TOPK, E], F32, sh)
        hit = sb("hit", [P, NT, E], F32, sh)
        mask_b = sb("mask_b", [P, NT, E], BF16, sh)
        posi = sb("posi", [P, 3, NT, E], I32, sh)
        posf = sb("posf", [P, 3, NT, E], F32, sh)
        sh.close()
        seq.close()

        moe = ExitStack()
        tabm = sb("tabm", [P, 4, 2 * P], F32, moe)
        tab = sb("tab", [P, 4, 2, 16], F32, moe)
        tabs = sb("tabs", [P, 4, 3, 16], F32, moe)
        spread = sb("spread", [P, 2, 4, 8, 16], F32, moe)
        slots = sb("slots", [P, E + NBUF, 2, 2], I32, moe)
        slot_now = sb("slot_now", [P, NBUF, 2, 2], I32, moe)
        w13_sb = sb("w13_sb", [P, NBUF, 2, KD, INTER], F32, moe)
        w2_sb = sb("w2_sb", [IC, NBUF, NI, D], F32, moe)
        xg = sb("xg", [P, NBUF, 2, ROW], F32, moe)
        w13_part = sb("w13_part", [P, 2, 2, 2, KD, INTER], F32R, moe)
        xgT_part = sb("xgT_part", [P, 2, 2, KD, CAP], F32R, moe)
        eg = sb("eg", [IC, 2, NI, CAP], F32, moe)
        eh = sb("eh", [IC, 2, NI, CAP], F32, moe)
        yo = sb("yo", [P, NBUF, 2, D], F32, moe)
        moe.close()

        proj_w_in = sem("proj_w_in")
        attn_w_in = sem("attn_w_in")
        weights_in = sem("weights_in")
        x_in = sem("x_in")
        res_in = sem("res_in")
        dense_filled = sem("dense_filled")
        freed_act = sem("dense_freed_act")
        freed_dve = sem("dense_freed_dve")
        consts_made = sem("consts_made")
        xn_ready = sem("xn_ready")
        var_ready = sem("var_ready")
        rstd_ready = sem("rstd_ready")
        kr_ready = sem("kr_ready")
        kr_copied = sem("kr_copied")
        rope_ready = sem("rope_ready")
        rope_moved = sem("rope_moved")
        scores_ready = sem("scores_ready")
        max_ready = sem("max_ready")
        probs_ready = sem("probs_ready")
        rden_ready = sem("rden_ready")
        turned = sem("turned")
        normed = Shared(shares("VPV", "VPV"), {"P": sem("normed_pool"), "V": sem("normed_dve")})
        turn_read = Shared(shares("A", "AAAV"), {"A": sem("turn_read_act"), "V": sem("turn_read_dve")})
        heads_out = sem("heads_out")
        attn_ready = sem("attn_ready")
        res_ready = sem("res_ready")
        abs_ready = sem("abs_ready")
        hT_ready = sem("hT_ready")
        qk_hi_ready = sem("qk_hi_ready")
        qk_lo_ready = sem("qk_lo_ready")
        qk_out = [sem(f"qk_out{c}") for c in range(KD)]
        stack_zeroed = sem("stack_zeroed")
        stacks_in = [sem(f"stacks_in{i}") for i in range(2)]
        rows_out = sem("rows_out")
        y_out = sem("y_out")
        spare_rows_zeroed = sem("spare_rows_zeroed")
        dve_chain = sem("dve_chain")
        table_chain = sem("table_chain")
        spare = sem("spare")
        pool_chain = sem("pool_chain")

        dense = DenseRing(banks, dense_filled, {"A": freed_act, "V": freed_dve})
        NPROJ_W, NATTN_W, NWEIGHTS = 4, 13, 17
        DVE_LINKS = 54
        RSTDS = 2 + 3 * NT
        FIRST_LINKS = 2

        logits_shifted = sem("logits_shifted")
        exp_ready = sem("exp_ready")
        sc_ready = sem("sc_ready")
        mask_ready = sem("mask_ready")
        low_hots_ready = sem("low_hots_ready")
        low_values_ready = sem("low_values_ready")
        hots_ready = sem("hots_ready")
        spread_ready = sem("spread_ready")
        slots_turned = sem("slots_turned")
        slots_ready = sem("slots_ready")
        ew_in = [sem(f"expert_w_in{i}") for i in range(NBUF)]
        e_rows = [sem(f"expert_rows{i}") for i in range(NBUF)]
        idx_ready = sem("idx_ready")
        e_turned = sem("expert_turned")
        e_x_hi = sem("expert_x_hi")
        e_x_lo = sem("expert_x_lo")
        e_w_hi = sem("expert_w_hi")
        e_w_lo = sem("expert_w_lo")
        e_up = sem("expert_up")
        e_gate = sem("expert_gate")
        e_h = sem("expert_h")
        e_down = sem("expert_down")
        e_y = sem("expert_y")
        e_added = [sem(f"expert_added{i}") for i in range(NBUF)]
        e_settled = sem("expert_settled")

        def unit_of(layer, s):
            g, t, j = s // 16, s // HG % NT, s % HG
            h = g * HG + j
            lo, hi = (0, (t + 1) * P) if layer == 0 else (max(t - 1, 0) * P, S)
            return h, t, lo, hi

        def q_group_units(g):
            return [("qr", g, 0), ("qr", g, 1)] + [("qn", g, j) for j in range(HG)]

        def copy_xT(eng, b, layer, k):
            freed = (freed_act, freed_dve)[k]

            def copy(dst, src):
                return eng.activation(dst, src, ACT.Copy) if k == 0 else eng.tensor_copy(dst, src)

            dense.wait_filled(eng, b, "xT", layer, k)
            bank = dense.bank("xT", layer, k)
            if layer == 3:
                copy(xnT[:, k, S:], bank[:, 0:SINKS])
            copy(xnT[:, k, 0:S], bank[:]).then_inc(freed, 1)

        def copy_turned(eng, who, b, layer, s):
            u = layer * UNITS + s
            if not 0 <= s < UNITS or turn_read.who[u] != who:
                return
            h, t, lo, hi = unit_of(layer, s)
            eng.wait_ge(turned, b * 2 * UNITS + u + 1)
            if u >= 2 * HG and turn_read.who[u - s % HG:u].count(who) == 0:
                eng.wait_ge(heads_out, b * 2 * TILES + u // HG - 1)
            dst = probsT[:, t % 2, h % HG, lo // P:hi // P, :]
            src = turn_banks[u % 2][:, lo:hi].rearrange("p (c q) -> p c q", q=P)
            turn_read.done(eng.activation(dst, src, ACT.Copy) if who == "A" else eng.tensor_copy(dst, src), u)

        def normalise(eng, b, layer, s):
            h, t, lo, hi = unit_of(layer, s)
            u = layer * UNITS + s
            row = probs[:, u % NPROB, lo:hi]
            normed.done(eng.tensor_scalar(row, row, rden[:, u % NPROB:u % NPROB + 1], None, ALU.mult), u)

        row_banks, gate_banks, up_banks, y_banks = (banks[2 * n:2 * n + 2] for n in range(4))

        block = ctx.enter_context(nc.Block())

        @block.sync
        def _(sp):
            sp.dma_start(x_next, x_rows[0:1].rearrange("o p t d -> p (o t) d")).then_inc(x_in, 16)

            def load(signal, count, pairs):
                for dst, src in pairs:
                    sp.dma_start(dst, src).then_inc(signal, 16)
                assert len(pairs) == count, len(pairs)

            by_rows = lambda w: w.rearrange("(k p) n -> p k n", p=P)
            load(proj_w_in, NPROJ_W, (
                (identity[:], ident), (wproj_sb[:], by_rows(w_proj)), (gam_sb[:, 0:1], gamma_q), (gam_sb[:, 1:2], gamma_kv)))
            load(attn_w_in, NATTN_W, (
                (wkr_sb[:, 0], by_rows(w_kr)), (wqr_sb[:, 0].rearrange("p g n -> p (g n)"), w_qr),
                (bqk1_sb[:, 0], b_q1), (bqk1_sb[:, 1], b_k1),
                (rope_k[:, 0], cos_k), (rope_k[:, 1], sin_k), (wuv_sb[:], w_uv), (wuk_sb[:].rearrange("p g n -> p (g n)"), w_uk),
                (rope_q[:, 0], cos_q), (rope_q[:, 1], sin_q), (wqn_sb[:].rearrange("p h n -> p (h n)"), w_qn),
                (identity_bf[:], identb), (causal_sb[:], causal)))
            load(weights_in, NWEIGHTS, (
                (wo0_sb[:], by_rows(w_o0)), (wgate_sb[:], by_rows(w_gate)), (wup_sb[:], by_rows(w_up)),
                (wdown_sb[:], by_rows(w_down)), (wqk1_sb[:, 0], by_rows(w_q1)), (wqk1_sb[:, 1], by_rows(w_k1)),
                (wv1_sb[:], by_rows(w_v1)), (wo1_sb[:], by_rows(w_o1)), (window_sb[:], window),
                (bv1_sb[:], b_v1.to_broadcast([P, 512])), (bo1_sb[:], b_o1.to_broadcast([P, D])),
                (gatew_sb[:], by_rows(gate_w)), (sw13_sb[:, 0], by_rows(sw1)), (sw13_sb[:, 1], by_rows(sw3)),
                (sw2_sb[:], sw2.rearrange("(k p) n -> p k n", p=IC)), (tri_sb[:], tri), (small_sb[:], small)))

            def wait(signal, value):
                sp.wait_ge(signal, value)
                sp.sem_inc(spare, 1)

            sp.sem_inc(y_out, 16)
            sp.sem_inc(rows_out, 32)
            with sp.Fori(0, B) as b:
                wait(y_out, (b + 1) * 16)
                sp.dma_start(xb[:], x_rows[bass.ds(b, 1)].rearrange("o p t d -> p (o t) d")).then_inc(res_in, 16)
                for g in range(G0):
                    wait(rope_ready, b * G0 + g + 1)
                    if g >= 2:
                        wait(scores_ready, b * 2 * UNITS + 16 * (g - 1))
                    for j in range(HG):
                        sp.dma_start(qT[QN:P, g % 2, j, :], rp[32 * j:32 * j + 32, 0, :]).then_inc(rope_moved, 16)
                for c in range(KD):
                    wait(qk_hi_ready, b * 4 + (2 * c + 2))
                    wait(qk_lo_ready, b * 4 + (2 * c + 2))
                    for chunk, parts, order in ((c, q_parts, (0, 1)), (KD + c, k_parts, (0, 0, 1, 1))):
                        for blk, part in enumerate(order):
                            sp.dma_start(parts[c, :, blk], qk_split[:, chunk, part, :].bitcast(F32)).then_inc(qk_out[c], 16)
                    if c == 0:
                        wait(stack_zeroed, b + 1)
                    wait(qk_out[c], (b + 1) * 6 * 16)
                    for g in (2 * c, 2 * c + 1):
                        if g >= 2:
                            wait(scores_ready, b * 2 * UNITS + UNITS + 16 * (g - 1))
                        h0 = g * HG % (P // HD1)
                        heads_of = lambda parts: parts[c, h0:h0 + HG].rearrange("h a r n -> (a r) h n")
                        for half in range(2):
                            sp.dma_start(q_st[32 * half:32 * half + 32, g % 2].bitcast(F32), heads_of(q_parts))\
                                .then_inc(stacks_in[g % 2], 16)
                        sp.dma_start(k_st[0:64, g % 2].bitcast(F32), heads_of(k_parts)).then_inc(stacks_in[g % 2], 16)
                for done in stacks_in:
                    wait(done, (b + 1) * 2 * 48)
                wait(attn_ready, b * 2 * G0 + 2 * G0)
                sp.dma_start(x_next, x_rows[bass.ds(b + 1, 1)].rearrange("o p t d -> p (o t) d")).then_inc(x_in, 16)
                wait(xn_ready, b * 5 * NT + 5 * NT)
                sp.dma_start(xn_rows.rearrange("(b t p) d -> b p t d", b=B, p=P)[bass.ds(b, 1), :, :, 0:D]
                             .rearrange("o p t d -> p (o t) d"), xn).then_inc(rows_out, 16)
                wait(sc_ready, b + 1)
                sp.dma_start(xn_rows.rearrange("(b t p) d -> b p t d", b=B, p=P)[bass.ds(b, 1), :, :, D:ROW]
                             .rearrange("o p t d -> p (o t) d"), sc[:]).then_inc(rows_out, 16)
                wait(res_ready, b + 1)
                sp.dma_start(out[0:T, :].rearrange("(b t p) d -> b p t d", b=B, p=P)[bass.ds(b, 1)]
                             .rearrange("o p t d -> p (o t) d"), xb[:]).then_inc(y_out, 16)

            sp.wait_ge(rows_out, (B + 1) * 32)
            sp.wait_ge(x_in, (B + 1) * 16)
            sp.wait_ge(y_out, (B + 1) * 16)

            def load_expert(e, i):
                at = (lambda w: w[e:e + 1]) if isinstance(e, int) else (lambda w: w[bass.ds(e, 1)])
                for m, w in enumerate((w1, w3)):
                    sp.dma_start(w13_sb[:, i, m], at(w.rearrange("e (k p) n -> e p k n", p=P))
                                 .rearrange("o p k n -> p (o k) n")).then_inc(ew_in[i], 16)
                sp.dma_start(w2_sb[:, i], at(w2.rearrange("e (k p) n -> e p k n", p=IC))
                             .rearrange("o p k n -> p (o k) n")).then_inc(ew_in[i], 16)

            for i in range(NBUF):
                load_expert(i, i)

            def settle(ep, i):
                sp.wait_ge(e_added[i], (ep + 1) * 32)
                sp.sem_inc(e_settled, 1)

            with sp.Fori(0, E // NBUF - 1) as ep:
                for i in range(NBUF):
                    wait(e_down, ep * NBUF + i + 1)
                    load_expert(ep * NBUF + (NBUF + i), i)
                    settle(ep, i)
            for i in range(NBUF):
                settle(E // NBUF - 1, i)

        @block.tensor
        def _(pe):
            pe.wait_ge(proj_w_in, NPROJ_W * 16)

            def turn_tile(b, layer, t):
                pe.wait_ge(xn_ready, b * 5 * NT + (NT * (0 if layer == 1 else layer) + t + 1))
                for k in range(KD):
                    if t == 0:
                        dense.wait_free(pe, b, "xT", layer, k)
                    mm = pe.transpose(dense.bank("xT", layer, k)[:, t * P:(t + 1) * P],
                                      (xn_next if layer == 1 else xn)[:, t, k * P:(k + 1) * P], identity[:])
                    if t == NT - 1:
                        mm.then_inc(dense_filled, 1)

            def product_and_turn(b, name, layer, factors):
                for t in range(NT):
                    product(b, (name, t), lambda k: k[:, 0:D], factors(t))
                    if t >= 2:
                        turn_tile(b, layer, t - 2)
                for t in (NT - 2, NT - 1):
                    turn_tile(b, layer, t)

            def product(b, name, out, pairs, fresh=0):
                dense.wait_free(pe, b, *name)
                bank = dense.bank(*name)
                for i, (lhsT, rhs) in enumerate(pairs):
                    if fresh:
                        dense.wait_read(pe, b, "xT", fresh, i)
                    mm = pe.matmul(out(bank), lhsT, rhs, start=(i == 0), stop=(i == len(pairs) - 1))
                mm.then_inc(dense_filled, 1)

            def q_unit(b, name):
                g, j = name[1], name[2]
                if name[0] == "qr":
                    product(b, name, lambda k: k[:, :], [(wqr_sb[:, j, g, :], cT[:, 0, :])])
                else:
                    product(b, name, lambda k: k[0:QN, :], [(wqn_sb[:, g * HG + j, :], cT[:, 0, :])])

            def scores(b, layer, s):
                h, t, lo, hi = unit_of(layer, s)
                u = layer * UNITS + s
                g, j = divmod(h, HG)
                bank = score_banks[u % 3]
                if u >= 3:
                    pe.wait_ge(probs_ready, b * 2 * UNITS + u - 2)
                if s % 16 == 0:
                    if layer == 0:
                        dense.wait_read(pe, b, "qn", g, HG - 1)
                        pe.wait_ge(rope_moved, b * H0 * 16 + 64 * (g + 1))
                        if g == 0:
                            pe.wait_ge(kr_copied, b + 1)
                    else:
                        pe.wait_ge(stacks_in[g % 2], (b * 2 + g // 2 + 1) * 48)
                q = (qT[:, g % 2, j] if layer == 0 else q_st[:, g % 2, j])[:, t * P:(t + 1) * P]
                k = kT[:, g, lo:hi] if layer == 0 else k_st[:, g % 2, j, lo:hi]
                pe.matmul(bank[:, lo:hi], q, k, start=True, stop=False)
                if layer == 0:
                    mm = pe.matmul(bank[:, t * P:hi], identity_bf[:], causal_sb[:], start=False, stop=True)
                else:
                    first = P if t == 0 else 0
                    mm = pe.matmul(bank[:, lo:lo + WCOLS - first], identity_bf[:], window_sb[:, first:WCOLS],
                                   start=False, stop=True)
                mm.then_inc(scores_ready, 1)

            def turn(b, layer, s):
                h, t, lo, hi = unit_of(layer, s)
                u = layer * UNITS + s
                normed.wait(pe, b, u)
                if u >= 2:
                    turn_read.wait(pe, b, u - 2)
                for c in range(lo, hi, P):
                    mm = pe.transpose(turn_banks[u % 2][:, c:c + P], probs[:, u % NPROB, c:c + P], identity[:])
                mm.then_inc(turned, 1)

            def heads(b, layer, n, step):
                g, t = divmod(n, NT)
                kts = range(t + 1) if layer == 0 else range(max(t - 1, 0), NT)
                step -= NT - len(kts) if layer == 0 else 0
                if not 0 <= step < len(kts):
                    return
                if step == 0:
                    heads_waits(b, layer, n)
                kt = kts[step]
                for j in range(HG):
                    c = g * VD0 if layer == 0 else (g * HG + j) * 32
                    v = (v0 if layer == 0 else v1)[:, kt, c:c + 32]
                    mm = pe.matmul(out_bank[32 * j:32 * j + 32, t * P:(t + 1) * P], v, probsT[:, t % 2, j, kt, :],
                                   start=(kt == kts[0]), stop=(kt == kts[-1]))
                if kt == kts[-1]:
                    mm.then_inc(heads_out, 1)

            def heads_waits(b, layer, n):
                g, t = divmod(n, NT)
                turn_read.wait_up_to(pe, b, layer * UNITS + HG * (n + 1) - 1)
                if t == 0 and (layer or g):
                    pe.wait_ge(attn_ready, b * 2 * G0 + layer * G0 + g)
                if n == 0:
                    dense.wait_read(pe, b, *(("v0",) if layer == 0 else ("v1", NT - 1)))

            def attention(b, layer):
                for name in (("qn", 0, HG - 1), ("qr", 0, 1)) if layer == 0 else (("v1", NT - 1),):
                    dense.wait_read(pe, b, *name)
                for s in range(UNITS + PVLAG + HG):
                    if s < UNITS:
                        scores(b, layer, s)
                    if 0 <= s - LAG < UNITS:
                        turn(b, layer, s - LAG)
                    g, r = divmod(s, 16)
                    n, r4 = divmod(s - PVLAG, HG)
                    if n >= 1:
                        heads(b, layer, n - 1, r4)
                    if layer == 0 and g + 1 < G0 and r in (5, 7, 9, 11, 13, 15):
                        q_unit(b, q_group_units(g + 1)[(r - 5) // 2])

            def earlier_choices(b):
                pe.wait_ge(mask_ready, b + 1)
                dense.wait_free(pe, b, "pos")
                bank = dense.bank("pos")
                pe.matmul(bank[:, 0:NT * E], tri_sb[:], mask_b[:].rearrange("p t e -> p (t e)"), start=True, stop=False)
                for t in range(NT - 1):
                    rest = NT - 1 - t
                    mm = pe.matmul(bank[:, (t + 1) * E:NT * E].rearrange("p (t e) -> p t e", e=E), ones_b[:],
                                   mask_b[:, t:t + 1, :].to_broadcast([P, rest, E]), start=False, stop=(rest == 1))
                mm.then_inc(dense_filled, 1)
                product(b, ("count",), lambda k: k[:, 0:E], [(ones_b[:], mask_b[:, t, :]) for t in range(NT)])

            def slot_table(b):
                pe.wait_ge(hots_ready, b + 1)
                pe.wait_ge(low_values_ready, b + 1)
                for n in range(2):
                    dense.wait_free(pe, b, "table", n)
                    for g in (2 * n, 2 * n + 1):
                        for v in range(2):
                            c = (g % 2 * 2 + v) * P
                            for t in range(NT):
                                mm = pe.matmul(dense.bank("table", n)[:, c:c + P], onehot_a[:, t, g * P:(g + 1) * P],
                                               val_b[:, v, t, g * P:(g + 1) * P], start=(t == 0), stop=(t == NT - 1))
                    mm.then_inc(dense_filled, 1)

            with pe.Fori(0, B) as b:
                for t in range(NT):
                    turn_tile(b, 1, t)
                for t in range(NT):
                    product(b, ("proj", t), lambda k: k[:, 0:2 * CQ],
                            [(xnT[:, k, t * P:(t + 1) * P], wproj_sb[:, k, :]) for k in range(KD)], fresh=t == 0 and 1)
                pe.wait_ge(attn_w_in, NATTN_W * 16)
                pe.wait_ge(consts_made, 2)
                for r in range(2):
                    product(b, ("kr", r), lambda k: k[:, :], [(wkr_sb[:, r, k, :], xnT[:, k, 0:S]) for k in range(KD)])
                pe.wait_ge(xn_ready, b * 5 * NT + 2 * NT)
                for c in range(2):
                    dense.wait_free(pe, b, "cT", c)
                    for t in range(NT):
                        mm = pe.transpose(dense.bank("cT", c)[:, t * P:(t + 1) * P], cn[:, t, c * P:(c + 1) * P], identity[:])
                    mm.then_inc(dense_filled, 1)
                dense.wait_read(pe, b, "cT", 0)
                for r in range(2):
                    q_unit(b, ("qr", 0, r))
                dense.wait_read(pe, b, "cT", 1)
                dense.wait_free(pe, b, "v0")
                for t in range(NT):
                    mm = pe.matmul(dense.bank("v0")[:, t * P:(t + 1) * P], cT[:, 1, t * P:(t + 1) * P], wuv_sb[:],
                                   start=True, stop=True)
                mm.then_inc(dense_filled, 1)
                for g in range(G0):
                    product(b, ("kn", g), lambda k: k[0:KN, :], [(wuk_sb[:, g, :], cT[:, 1, :])])
                for j in range(HG):
                    q_unit(b, ("qn", 0, j))
                attention(b, 0)
                pe.wait_ge(attn_ready, b * 2 * G0 + G0)
                pe.wait_ge(weights_in, NWEIGHTS * 16)
                product_and_turn(b, "o0", 2, lambda t: [(attnT[:, g, t * P:(t + 1) * P], wo0_sb[:, g, :]) for g in range(G0)])
                for hf in range(HALVES):
                    for i in range(PLANES):
                        c = i * 256 + hf * P
                        for name, w in (("gate", wgate_sb), ("up", wup_sb)):
                            product(b, (name, i, hf), lambda k: k[:, :],
                                    [(w[:, k, c:c + P], xnT[:, k, 0:S]) for k in range(KD)],
                                    fresh=(name, i, hf) == ("gate", 0, 0) and 2)
                for t in range(NT):
                    dense.wait_free(pe, b, "down", t)

                def down(t, hf, i):
                    m = 2 * i + hf
                    return pe.matmul(dense.bank("down", t)[:, 0:D], hT[:, m, t * P:(t + 1) * P], wdown_sb[:, m, :],
                                     start=(m == 0), stop=(m == 2 * PLANES - 1))

                for hf, planes in ((0, range(PLANES)), (1, range(1))):
                    for i in planes:
                        pe.wait_ge(hT_ready, b * 8 + (hf * PLANES + i + 1))
                        for t in range(NT):
                            down(t, hf, i)
                for t in range(NT):
                    for i in range(1, PLANES):
                        if t == 0:
                            pe.wait_ge(hT_ready, b * 8 + (PLANES + i + 1))
                        mm = down(t, 1, i)
                    mm.then_inc(dense_filled, 1)
                    if t >= 2:
                        turn_tile(b, 3, t - 2)
                for t in (NT - 2, NT - 1):
                    turn_tile(b, 3, t)
                for c in QK_ORDER:
                    product(b, ("qk", c), lambda k: k[:, :],
                            [(wqk1_sb[:, c // 2, k, (c % 2) * P:(c % 2 + 1) * P],
                              xnT[:, k, 0:S] if c < 2 else xnT[:, k, SINKS:]) for k in range(KD)], fresh=c == 0 and 3)
                for t in range(NT):
                    product(b, ("v1", t), lambda k: k[:, :],
                            [(xnT[:, k, SINKS + t * P:SINKS + (t + 1) * P], wv1_sb[:, k, :]) for k in range(KD)])
                attention(b, 1)
                pe.wait_ge(attn_ready, b * 2 * G0 + 2 * G0)
                product_and_turn(b, "o1", 4, lambda t: [(attnT[:, g, t * P:(t + 1) * P], wo1_sb[:, g, :]) for g in range(4)])
                for k in range(KD):
                    dense.wait_read(pe, b, "xT", 4, k)
                dense.wait_free(pe, b, "logit")
                for t in range(NT):
                    for k in range(KD):
                        mm = pe.matmul(dense.bank("logit")[:, t * E:(t + 1) * E], xnT[:, k, t * P:(t + 1) * P],
                                       gatew_sb[:, k, :], start=(k == 0), stop=(k == KD - 1))
                mm.then_inc(dense_filled, 1)
                for c in range(NSI):
                    for m, name in enumerate(("sg", "su")):
                        product(b, (name, c), lambda k: k[0:IC, :],
                                [(sw13_sb[:, m, k, c * IC:(c + 1) * IC], xnT[:, k, 0:S]) for k in range(KD)])
                earlier_choices(b)
                dense.wait_read(pe, b, "su", NSI - 1)
                for t in range(NT):
                    product(b, ("sdown", t), lambda k: k[:, 0:D],
                            [(shT[:, c, t * P:(t + 1) * P], sw2_sb[:, c, :]) for c in range(NSI)])
                slot_table(b)

            def turn_rows(ep, i):
                e, i, ep = ep * NBUF + i, i % NBUF, ep + i // NBUF
                pe.wait_ge(e_rows[i], (ep + 1) * 32)
                pe.wait_ge(e_x_lo, e + 1)
                for hf in range(2):
                    for k in range(KD):
                        mm = pe.transpose(row_banks[i % 2][:, k * CAP + hf * P:k * CAP + hf * P + P],
                                          xg[:, i, hf, k * P:(k + 1) * P], identity[:])
                mm.then_inc(e_turned, 1)

            def gate_up(ep, i):
                e, i, ep = ep * NBUF + i, i % NBUF, ep + i // NBUF
                pe.wait_ge(e_x_lo, e + 3)
                pe.wait_ge(e_w_lo, e + 1)
                pe.wait_ge(e_h, e + 1)
                w_hi, w_lo = (w13_part[:, i % 2, part] for part in range(2))
                x_hi, x_lo = (xgT_part[:, i % 2, part] for part in range(2))
                terms = [(w, x, k) for w, x in ((w_hi, x_hi), (w_lo, x_hi), (w_hi, x_lo)) for k in range(KD)]
                for m, bank in enumerate((gate_banks[i % 2], up_banks[i % 2])):
                    for c in range(NI):
                        for n, (w, x, k) in enumerate(terms):
                            mm = pe.matmul(bank[0:IC, c * CAP:(c + 1) * CAP], w[:, m, k, c * IC:(c + 1) * IC], x[:, k, :],
                                           start=(n == 0), stop=(n == len(terms) - 1))
                mm.then_inc(e_up, 1)

            def expert_out(ep, i):
                e = ep * NBUF + i
                pe.wait_ge(ew_in[i], (ep + 1) * 48)
                pe.wait_ge(e_h, e + 3)
                pe.wait_ge(e_y, e + 1)
                for hf in range(2):
                    for c in range(NI):
                        mm = pe.matmul(y_banks[i % 2][:, hf * D:(hf + 1) * D], eh[:, i % 2, c, hf * P:(hf + 1) * P],
                                       w2_sb[:, i, c, :], start=(c == 0), stop=(c == NI - 1))
                mm.then_inc(e_down, 1)

            dense.wait_read(pe, B - 1, "table", 1)
            pe.wait_ge(spread_ready, 2)
            for k in range(2):
                for g in range(4):
                    c = k * 64 + g * 16
                    mm = pe.matmul(banks[0][:, c:c + 16], spread[:, k, g].rearrange("p h l -> p (h l)"), small_sb[:, 96:112],
                                   start=True, stop=True)
            mm.then_inc(slots_turned, 1)
            turn_rows(0, 0)
            gate_up(0, 0)
            turn_rows(0, 1)
            with pe.Fori(0, E // NBUF - 1) as ep:
                for i in range(NBUF):
                    gate_up(ep, i + 1)
                    turn_rows(ep, i + 2)
                    expert_out(ep, i)
            last = E // NBUF - 1
            for i in range(NBUF):
                if i + 1 < NBUF:
                    gate_up(last, i + 1)
                if i + 2 < NBUF:
                    turn_rows(last, i + 2)
                expert_out(last, i)

        @block.scalar
        def _(act):
            act.wait_ge(proj_w_in, NPROJ_W * 16)
            act.sem_inc(freed_act, dense.reads["A"])

            def xT_copy(b, layer):
                copy_xT(act, b, layer, 0)

            def qn_copy(b, g, j):
                dense.wait_filled(act, b, "qn", g, j)
                if g >= 2 and j == 0:
                    act.wait_ge(scores_ready, b * 2 * UNITS + 16 * (g - 1))
                act.activation(qT[0:QN, g % 2, j, :], dense.bank("qn", g, j)[0:QN, :], ACT.Copy,
                               scale=float(QN + QR) ** -0.5).then_inc(freed_act, 1)

            def attention(b, layer):
                for s in range(UNITS + PVLAG + HG + 1):
                    copy_turned(act, "A", b, layer, s - LAG - 1)
                    if s < UNITS:
                        h, t, lo, hi = unit_of(layer, s)
                        u = layer * UNITS + s
                        act.wait_ge(max_ready, b * 2 * UNITS + u + 1)
                        if u >= NPROB:
                            act.wait_ge(turned, b * 2 * UNITS + u - NPROB + 1)
                        act.activation(probs[:, u % NPROB, lo:hi], score_banks[u % 3][:, lo:hi], ACT.Exp,
                                       bias=nmax[:, u % 4:u % 4 + 1], accum_out=den[:, u % NPROB:u % NPROB + 1])\
                            .then_inc(probs_ready, 1)
                    g, r = divmod(s, 16)
                    if r == PVLAG + (4, 2)[layer] and g >= 1:
                        act.wait_ge(heads_out, b * 2 * TILES + layer * TILES + NT * g)
                        if g == 1 and layer == 1:
                            dense.wait_filled(act, b, "o0", NT - 1)
                        act.activation(attnT[:, g - 1, :], out_bank[:], ACT.Copy).then_inc(attn_ready, 1)
                    if layer == 0 and g + 1 < G0 and r in (9, 11, 13, 15):
                        qn_copy(b, g + 1, (r - 9) // 2)

            with act.Fori(0, B) as b:
                xT_copy(b, 1)
                for c in range(2):
                    dense.wait_filled(act, b, "cT", c)
                    act.activation(cT[:, c, :], dense.bank("cT", c)[:], ACT.Copy, scale=gam_sb[:, c:c + 1]).then_inc(freed_act, 1)
                dense.wait_filled(act, b, "v0")
                act.activation(v0[:].rearrange("p t n -> p (t n)"), dense.bank("v0")[:], ACT.Copy).then_inc(freed_act, 1)
                for g in range(G0):
                    dense.wait_filled(act, b, "kn", g)
                    act.activation(kT[0:KN, g, :], dense.bank("kn", g)[0:KN, :], ACT.Copy).then_inc(freed_act, 1)
                for j in range(HG):
                    qn_copy(b, 0, j)
                attention(b, 0)
                xT_copy(b, 2)
                for hf in range(HALVES):
                    for i in range(PLANES):
                        dense.wait_filled(act, b, "gate", i, hf)
                        n = hf * PLANES + i
                        if n >= 2:
                            dense.wait_read(act, b, "up", (n - 2) % PLANES, (n - 2) // PLANES)
                        act.activation(sg[:, i % 2, :], dense.bank("gate", i, hf)[:], ACT.Silu).then_inc(freed_act, 1)
                        dense.wait_read(act, b, "up", i, hf)
                        act.activation(ha[:, i, :], hp[:, i, :], ACT.Abs).then_inc(abs_ready, 1)
                xT_copy(b, 3)
                for n, c in enumerate(QK_ORDER):
                    dense.wait_read(act, b, "qk", c)
                    act.activation(qk_split[:, c, 0, :], qk32[:, n % 2, :], ACT.Copy).then_inc(qk_hi_ready, 1)
                attention(b, 1)
                xT_copy(b, 4)
                dense.wait_filled(act, b, "logit")
                act.activation(logits[:].rearrange("p t e -> p (t e)"), dense.bank("logit")[:, 0:NT * E], ACT.Copy)\
                    .then_inc(freed_act, 1)
                act.wait_ge(logits_shifted, b + 1)
                act.activation(sc[:], shifted[:], ACT.Exp).then_inc(exp_ready, 1)
                for c in range(NSI):
                    dense.wait_filled(act, b, "sg", c)
                    if c >= 2:
                        dense.wait_read(act, b, "su", c - 2)
                    act.activation(ssg[:, c % 2, :], dense.bank("sg", c)[0:IC, :], ACT.Silu).then_inc(freed_act, 1)
                act.wait_ge(low_hots_ready, b + 1)
                act.activation(val_b[:, 0], onehot_b[:], ACT.Copy, scale=small_sb[:, 80:81]).then_inc(low_values_ready, 1)

            act.wait_ge(y_out, (B + 1) * 16)
            act.wait_ge(rows_out, (B + 1) * 32)
            act.wait_ge(x_in, (B + 1) * 16)

            def copy_rows(ep, i):
                act.wait_ge(e_turned, ep * NBUF + i + 1)
                act.activation(xgT_part[:, i % 2, 0].rearrange("p k n -> p (k n)"), row_banks[i % 2][:], ACT.Copy)\
                    .then_inc(e_x_hi, 1)

            def round_weights(ep, i):
                ep, i = ep + i // NBUF, i % NBUF
                act.wait_ge(ew_in[i], (ep + 1) * 48)
                act.activation(w13_part[:, i % 2, 0].rearrange("p m k n -> p (m k n)"),
                               w13_sb[:, i].rearrange("p m k n -> p (m k n)"), ACT.Copy).then_inc(e_w_hi, 1)

            def gate(ep, i):
                act.wait_ge(e_up, ep * NBUF + i + 1)
                act.activation(eg[:, i % 2].rearrange("p k n -> p (k n)"), gate_banks[i % 2][0:IC, :], ACT.Silu).then_inc(e_gate, 1)

            round_weights(0, 0)
            round_weights(0, 1)
            copy_rows(0, 0)
            with act.Fori(0, E // NBUF - 1) as ep:
                for i in range(NBUF):
                    gate(ep, i)
                    copy_rows(ep, i + 1)
                    round_weights(ep, i + 2)
            for i in range(NBUF):
                gate(E // NBUF - 1, i)
                if i + 1 < NBUF:
                    copy_rows(E // NBUF - 1, i + 1)
                if i + 2 < NBUF:
                    round_weights(E // NBUF - 1, i + 2)

        @block.vector
        def _(dve):
            dve.sem_inc(freed_dve, dense.reads["V"])

            def scale_rows(b, n, ch, statistics, src, dst, count):
                ch.link(statistics)
                dve.sem_inc(spare, 1)
                for i in range(count):
                    last = dve.bn_aggr(mv[:, i, :], stats[:, i, :])
                ch.link(last)
                dve.tensor_scalar(vare[:, 0:count], mv[:, 0:count, 1], EPS, None, ALU.add).then_inc(var_ready, 1)
                dve.wait_ge(rstd_ready, b * RSTDS + n)
                for i in range(count):
                    ins = dve.tensor_scalar(dst(i), src(i), mv[:, i, 0:1], rstd[:, i:i + 1], ALU.subtract, ALU.mult)
                    if count == NT:
                        ins.then_inc(xn_ready, 1)
                    elif i % 2:
                        ins.then_inc(freed_dve, 1)
                if count > NT:
                    dve.drain().then_inc(xn_ready, NT)

            def norm(b, n, ch, src, dst, count):
                dve.sem_inc(spare, 1)
                for i in range(count):
                    statistics = dve.bn_stats(stats[:, i, :], src(i))
                scale_rows(b, n, ch, statistics, src, dst, count)

            def q_rope(b, g, ch):
                for r in range(2):
                    dense.wait_filled(dve, b, "qr", g, r)
                    if r == 0 and g >= 1:
                        dve.wait_ge(rope_moved, b * H0 * 16 + 64 * g)
                    dve.tensor_tensor(rp[:, 1 + r, :], dense.bank("qr", g, r)[:], rope_q[:, r, :], ALU.mult).then_inc(freed_dve, 1)
                ch.link(dve.drain())
                dve.tensor_tensor(rp[:, 0, :], rp[:, 1, :], rp[:, 2, :], ALU.add).then_inc(rope_ready, 1)

            def attention(b, layer, ch):
                for s in range(UNITS + LAG + 2):
                    if s < UNITS:
                        h, t, lo, hi = unit_of(layer, s)
                        u = layer * UNITS + s
                        dve.wait_ge(scores_ready, b * 2 * UNITS + u + 1)
                        if u >= 4:
                            dve.wait_ge(probs_ready, b * 2 * UNITS + u - 3)
                        dve.tensor_reduce(nmax[:, u % 4:u % 4 + 1], score_banks[u % 3][:, lo:hi], AX.X, ALU.max, negate=True)\
                            .then_inc(max_ready, 1)
                    d = s - DIVLAG
                    u = layer * UNITS + d
                    if 0 <= d < UNITS:
                        dve.wait_ge(probs_ready, b * 2 * UNITS + u + 1)
                        if u >= NPROB:
                            normed.wait(dve, b, u - NPROB)
                        dve.reciprocal(rden[:, u % NPROB:u % NPROB + 1], den[:, u % NPROB:u % NPROB + 1]).then_inc(rden_ready, 1)
                    copy_turned(dve, "V", b, layer, s - LAG - 1)
                    if 0 <= d < UNITS and normed.who[u] == "V":
                        dve.wait_ge(rden_ready, b * 2 * UNITS + u + 1)
                        normalise(dve, b, layer, d)
                    g, r = divmod(s, 16)
                    if layer == 0 and g + 1 < G0 and r == 7:
                        q_rope(b, g + 1, ch)

            def residual_tile(b, name, t):
                dense.wait_filled(dve, b, name, t)
                dve.tensor_tensor(xb[:, t, :], xb[:, t, :], dense.bank(name, t)[:, 0:D], ALU.add).then_inc(freed_dve, 1)

            def residual_norm(b, n, ch, name):
                def scale_tile(t):
                    dve.wait_ge(rstd_ready, b * RSTDS + (3 + (n - 3) * NT + t))
                    dve.tensor_scalar(xn[:, t, :], xb[:, t, :], mv[:, t, 0:1], rstd[:, t:t + 1], ALU.subtract, ALU.mult)\
                        .then_inc(xn_ready, 1)

                for t in range(NT):
                    residual_tile(b, name, t)
                    dense.wait_read(dve, b, name, t)
                    dve.sem_inc(spare, 1)
                    ch.link(dve.bn_stats(stats[:, t, :], xb[:, t, :]))
                    dve.sem_inc(spare, 1)
                    ch.link(dve.bn_aggr(mv[:, t, :], stats[:, t, :]))
                    dve.tensor_scalar(vare[:, t:t + 1], mv[:, t, 1:2], EPS, None, ALU.add).then_inc(var_ready, 1)
                    if t:
                        scale_tile(t - 1)
                scale_tile(NT - 1)

            def first_norm(b, ch):
                dve.wait_ge(x_in, (b + 1) * 16)
                norm(b, 1, ch, lambda i: x_next[:, i, :], lambda i: xn_next[:, i, :], NT)

            def wide(a):
                return a.unsqueeze(2).to_broadcast([P, NT, E])

            def shift_logits(b, ch):
                dense.wait_read(dve, b, "logit")
                ch.link(dve.tensor_reduce(rmax[:], logits[:], AX.X, ALU.max))
                dve.tensor_tensor(shifted[:], logits[:], wide(rmax[:]), ALU.subtract).then_inc(logits_shifted, 1)

            def choose_experts(b, ch):
                dve.wait_ge(exp_ready, b + 1)
                ch.link(dve.tensor_reduce(rsum[:], sc[:], AX.X, ALU.add))
                ch.link(dve.reciprocal(rrec[:], rsum[:]))
                ch.link(dve.tensor_tensor(sc[:], sc[:], wide(rrec[:]), ALU.mult))
                dve.sem_inc(spare, 1)
                for t in range(NT):
                    last = dve.max(top[:, t, :], sc[:, t, :])
                ch.link(last)
                dve.sem_inc(spare, 1)
                for t in range(NT):
                    last = dve.max_index(topi[:, t, :], top[:, t, :], sc[:, t, :])
                ch.link(last)
                ch.link(dve.tensor_copy(topf[:], topi[:]))
                ch.link(dve.tensor_tensor(hits[:], small_sb[:, 0:E].unsqueeze(1).unsqueeze(1).to_broadcast([P, NT, TOPK, E]),
                                          topf[:, :, 0:TOPK].unsqueeze(3).to_broadcast([P, NT, TOPK, E]), ALU.is_equal))
                ch.link(dve.tensor_reduce(hit[:], hits[:].rearrange("p t k e -> p t e k"), AX.X, ALU.add))
                dve.tensor_copy(mask_b[:], hit[:]).then_inc(mask_ready, 1)
                dve.sem_inc(sc_ready, 1)

            def slot_numbers(b, ch):
                flat = lambda a: a.rearrange("p t e -> p (t e)")
                dense.wait_filled(dve, b, "pos")
                ins = dve.tensor_tensor(posf[:, 2], dense.bank("pos")[:, 0:NT * E].rearrange("p (t e) -> p t e", e=E),
                                        seen[:].unsqueeze(1).to_broadcast([P, NT, E]), ALU.add)
                ins.then_inc(freed_dve, 1)
                ch.link(dve.drain())
                ch.link(dve.tensor_copy(posi[:, 0], posf[:, 2]))
                dense.wait_filled(dve, b, "count")
                dve.tensor_tensor(seen[:], seen[:], dense.bank("count")[:, 0:E], ALU.add).then_inc(freed_dve, 1)
                dve.tensor_single_scalar(flat(posi[:, 1]), flat(posi[:, 0]), 4, ALU.arith_shift_right)
                ch.link(dve.tensor_single_scalar(flat(posi[:, 2]), flat(posi[:, 0]), 15, ALU.bitwise_and))
                dve.tensor_copy(posf[:, 0], posi[:, 1])
                ch.link(dve.tensor_copy(posf[:, 1], posi[:, 2]))
                ch.link(dve.scalar_tensor_tensor(posf[:, 0], hit[:], -1000.0, posf[:, 0], ALU.mult, ALU.add))
                ch.link(dve.tensor_scalar(posf[:, 0], posf[:, 0], 1000.0, None, ALU.add))

            def slot_onehot(half, hot):
                iota16 = small_sb[:, 32:48].unsqueeze(1).to_broadcast([P, NT * E, 16])
                col = posf[:, half].rearrange("p t e -> p (t e)").unsqueeze(2).to_broadcast([P, NT * E, 16])
                return dve.tensor_tensor(hot[:].rearrange("p t (e s) -> p (t e) s", s=16), iota16, col, ALU.is_equal)

            dve.memset(seen[:], 0.0)
            dve.memset(table[:], 0.0)
            dve.memset(ones_b[:], 1.0)
            ch = Chain(dve, dve_chain)
            first_norm(0, ch)
            assert ch.n == FIRST_LINKS
            dve.wait_ge(attn_w_in, NATTN_W * 16)
            for w in (wkr_sb[:].rearrange("p r k n -> p r (k n)"), wqr_sb[:].rearrange("p r g n -> p r (g n)")):
                a, r = (w[:, i, :].rearrange("p (m two) -> p m two", two=2) for i in range(2))
                dve.tensor_scalar(r[:, :, 0], a[:, :, 1], -1.0, None, ALU.mult)
                last = dve.tensor_copy(r[:, :, 1], a[:, :, 0])
            last.then_inc(consts_made, 1)
            dve.tensor_scalar(bqk1_sb[:, 0, :], bqk1_sb[:, 0, :], float(HD1) ** -0.5, None, ALU.mult).then_inc(consts_made, 1)
            dve.wait_ge(consts_made, 2)
            with dve.Fori(0, B) as b:
                ch = Chain(dve, dve_chain, b, DVE_LINKS, FIRST_LINKS)
                dve.wait_ge(rows_out, (b + 1) * 32)
                copy_xT(dve, b, 1, 1)
                for t in range(NT):
                    dense.wait_filled(dve, b, "proj", t)
                    dve.sem_inc(spare, 1)
                    for c in range(2):
                        statistics = dve.bn_stats(stats[:, 2 * t + c, :], dense.bank("proj", t)[:, c * CQ:(c + 1) * CQ])
                scale_rows(b, 2, ch, statistics, lambda i: dense.bank("proj", i // 2)[:, (i % 2) * CQ:(i % 2 + 1) * CQ],
                           lambda i: cn[:, i // 2, (i % 2) * CQ:(i % 2 + 1) * CQ], 2 * NT)
                for r in range(2):
                    dense.wait_filled(dve, b, "kr", r)
                    dve.tensor_tensor(rp[KN:P, 1 + r, :], dense.bank("kr", r)[KN:P, :], rope_k[KN:P, r, :], ALU.mult).then_inc(freed_dve, 1)
                ch.link(dve.drain())
                dve.tensor_tensor(kT[KN:P, 0, :], rp[KN:P, 1, :], rp[KN:P, 2, :], ALU.add).then_inc(kr_ready, 1)
                dve.wait_ge(kr_ready, b + 1)
                q_rope(b, 0, ch)
                attention(b, 0, ch)
                dve.wait_ge(res_in, (b + 1) * 16)
                residual_norm(b, 3, ch, "o0")
                copy_xT(dve, b, 2, 1)
                pairs = ((0, 1), (1, 2), (2, 3), (0, 2), (1, 3), (0, 3))
                w01, w12, w23, w02, w13, w03 = (wins[:, n, :] for n in range(6))

                def compare(hf, i):
                    dve.wait_ge(abs_ready, b * 8 + (hf * PLANES + i + 1))
                    for n, (first, second) in enumerate(pairs):
                        if second == i:
                            last = dve.tensor_tensor(wins[:, n, :], ha[:, first, :], ha[:, second, :], ALU.is_ge)
                    return last

                for hf in range(HALVES):
                    for i in range(PLANES):
                        dense.wait_filled(dve, b, "up", i, hf)
                        dense.wait_read(dve, b, "gate", i, hf)
                        dve.tensor_tensor(hp[:, i, :], dense.bank("up", i, hf)[:], sg[:, i % 2, :], ALU.mult).then_inc(freed_dve, 1)
                        if i >= 2:
                            compare(hf, i - 1)
                    ch.link(compare(hf, PLANES - 1))
                    dve.tensor_tensor(wsum[:, 0, :], w01, w02, ALU.add)
                    dve.tensor_tensor(wsum[:, 1, :], w12, w13, ALU.add)
                    dve.tensor_tensor(wsum[:, 2, :], w23, w02, ALU.subtract)
                    ch.link(dve.tensor_tensor(wsum[:, 3, :], w13, w23, ALU.add))
                    dve.tensor_tensor(wsum[:, 0, :], wsum[:, 0, :], w03, ALU.add)
                    dve.tensor_tensor(wsum[:, 1, :], wsum[:, 1, :], w01, ALU.subtract)
                    dve.tensor_tensor(wsum[:, 2, :], wsum[:, 2, :], w12, ALU.subtract)
                    ch.link(dve.tensor_tensor(wsum[:, 3, :], wsum[:, 3, :], w03, ALU.add))
                    for i, (bound, op) in enumerate(((2.0, ALU.is_ge), (1.0, ALU.is_ge), (0.0, ALU.is_ge), (1.0, ALU.is_le))):
                        ins = dve.scalar_tensor_tensor(hT[:, 2 * i + hf, :], wsum[:, i, :], bound, hp[:, i, :], op, ALU.mult)
                        ins.then_inc(hT_ready, 1)
                    dve.wait_ge(hT_ready, b * 8 + (hf + 1) * PLANES)
                residual_norm(b, 4, ch, "down")
                copy_xT(dve, b, 3, 1)
                for n, c in enumerate(QK_ORDER):
                    dense.wait_filled(dve, b, "qk", c)
                    if n >= 2:
                        dve.wait_ge(qk_hi_ready, b * 4 + (n - 1))
                    dve.tensor_scalar(qk32[:, n % 2, :], dense.bank("qk", c)[:], float(HD1) ** -0.5 if c < 2 else 1.0,
                                      bqk1_sb[:, c // 2, c % 2:c % 2 + 1], ALU.mult, ALU.add).then_inc(freed_dve, 1)
                    dve.wait_ge(qk_hi_ready, b * 4 + (n + 1))
                    dve.tensor_tensor(qk_split[:, c, 1, :], qk32[:, n % 2, :], qk_split[:, c, 0, :].bitcast(F32), ALU.subtract)\
                        .then_inc(qk_lo_ready, 1)
                for t in range(NT):
                    dve.tensor_tensor(xb[:, t, :], xb[:, t, :], bo1_sb[:], ALU.add)
                for t in range(NT):
                    dense.wait_filled(dve, b, "v1", t)
                    dve.tensor_tensor(v1[:, t, :], dense.bank("v1", t)[:], bv1_sb[:], ALU.add).then_inc(freed_dve, 1)
                attention(b, 1, ch)
                residual_norm(b, 5, ch, "o1")
                copy_xT(dve, b, 4, 1)
                for c in range(NSI):
                    if c == 0:
                        shift_logits(b, ch)
                        first_norm(b + 1, ch)
                    elif c == 1:
                        choose_experts(b, ch)
                    dense.wait_filled(dve, b, "su", c)
                    dense.wait_read(dve, b, "sg", c)
                    dve.tensor_tensor(shT[:, c, :], dense.bank("su", c)[0:IC, :], ssg[:, c % 2, :], ALU.mult).then_inc(freed_dve, 1)
                slot_numbers(b, ch)
                slot_onehot(1, onehot_b).then_inc(low_hots_ready, 1)
                residual_tile(b, "sdown", 0)
                slot_onehot(0, onehot_a)
                dve.wait_ge(low_hots_ready, b + 1)
                dve.sem_inc(spare, 1)
                residual_tile(b, "sdown", 1)
                for t in range(NT):
                    last = dve.tensor_scalar(val_b[:, 1, t, :], onehot_b[:, t, :], small_sb[:, bass.ds(b * NT + (t + 1), 1)],
                                             None, ALU.mult)
                last.then_inc(hots_ready, 1)
                residual_tile(b, "sdown", 2)
                residual_tile(b, "sdown", 3)
                dve.drain().then_inc(res_ready, 1)
                for n in range(2):
                    dense.wait_filled(dve, b, "table", n)
                    dve.tensor_tensor(table[:, 2 * n:2 * n + 2].rearrange("p g n -> p (g n)"),
                                      table[:, 2 * n:2 * n + 2].rearrange("p g n -> p (g n)"), dense.bank("table", n)[:], ALU.add)\
                        .then_inc(freed_dve, 1)
                ch.done()

            ch = Chain(dve, table_chain)
            ch.link(dve.drain())
            dve.wait_ge(y_out, (B + 1) * 16)
            dve.wait_ge(rows_out, (B + 1) * 32)
            dve.wait_ge(x_in, (B + 1) * 16)
            for g in range(4):
                last = dve.tensor_tensor(tabm[:, g, :].rearrange("p (v e s) -> p v e s", v=2, s=16),
                                         table[:, g, :].rearrange("p (v e s) -> p v e s", v=2, s=16),
                                         small_sb[:, 64:72].unsqueeze(1).unsqueeze(3).to_broadcast([P, 2, 8, 16]), ALU.mult)
            ch.link(last)
            ch.link(dve.tensor_reduce(tab[:].rearrange("p g v s -> p (g v) s"),
                                      tabm[:].rearrange("p g (v e s) -> p (g v) s e", v=2, s=16), AX.X, ALU.add))
            ch.link(dve.tensor_scalar(tabs[:, :, 0, :], tab[:, :, 1, :], float(P), float(-P), ALU.mult, ALU.add))
            ch.link(dve.tensor_tensor(tabs[:, :, 0, :], tabs[:, :, 0, :], tab[:, :, 0, :], ALU.add))
            ch.link(dve.tensor_scalar(tabs[:, :, 0, :], tabs[:, :, 0, :], 0.0, None, ALU.max))
            ch.link(dve.tensor_scalar(tabs[:, :, 1, :], tab[:, :, 1, :], 0.0, None, ALU.is_equal))
            ch.link(dve.tensor_tensor(tabs[:, :, 2, :], tabs[:, :, 1, :],
                                      small_sb[:, 48:64].unsqueeze(1).to_broadcast([P, 4, 16]), ALU.mult))
            ch.link(dve.tensor_tensor(tabs[:, :, 2, :], tabs[:, :, 2, :], tabs[:, :, 0, :], ALU.add))
            for k, kind in enumerate((0, 2)):
                dve.tensor_tensor(spread[:, k], tabs[:, :, kind, :].unsqueeze(2).to_broadcast([P, 4, 8, 16]),
                                  small_sb[:, 72:80].unsqueeze(1).unsqueeze(3).to_broadcast([P, 4, 8, 16]), ALU.mult)\
                    .then_inc(spread_ready, 1)
            dve.wait_ge(slots_turned, 1)
            for k in range(2):
                dve.tensor_copy(slots[:, k * NBUF:k * NBUF + E, k, :],
                                banks[0][:, k * 64:(k + 1) * 64].rearrange("p (e h) -> p e h", h=2)).then_inc(slots_ready, 1)
            dve.sem_inc(e_y, 2)
            dve.sem_inc(e_h, 2)

            def up_gate(ep, i):
                dve.wait_ge(e_gate, ep * NBUF + i + 1)
                dve.tensor_tensor(eh[:, i % 2].rearrange("p k n -> p (k n)"), up_banks[i % 2][0:IC, :],
                                  eg[:, i % 2].rearrange("p k n -> p (k n)"), ALU.mult).then_inc(e_h, 1)

            def weigh(ep, i):
                e = ep * NBUF + i
                dve.wait_ge(e_down, e + 1)
                dve.wait_ge(e_settled, e + 1)
                dve.sem_inc(spare, 1)
                score = slice(D + e, D + e + 1) if isinstance(e, int) else bass.ds(ep * NBUF + (D + i), 1)
                for hf in range(2):
                    last = dve.tensor_scalar(yo[:, i, hf, :], y_banks[i % 2][:, hf * D:(hf + 1) * D],
                                             xg[:, i, hf, score], None, ALU.mult)
                last.then_inc(e_y, 1)

            def low_weights(ep, i):
                dve.wait_ge(e_w_hi, ep * NBUF + i + 1)
                w_hi, w_lo = (w13_part[:, i % 2, part].rearrange("p m k n -> p (m k n)") for part in range(2))
                dve.tensor_tensor(w_lo, w13_sb[:, i % NBUF].rearrange("p m k n -> p (m k n)"), w_hi.bitcast(F32), ALU.subtract)\
                    .then_inc(e_w_lo, 1)

            def low_rows(ep, i):
                dve.wait_ge(e_x_hi, ep * NBUF + i + 1)
                x_hi, x_lo = (xgT_part[:, i % 2, part].rearrange("p k n -> p (k n)") for part in range(2))
                dve.tensor_tensor(x_lo, row_banks[i % 2][:], x_hi.bitcast(F32), ALU.subtract).then_inc(e_x_lo, 1)

            dve.sem_inc(e_x_lo, 2)
            low_weights(0, 0)
            low_rows(0, 0)
            low_weights(0, 1)
            up_gate(0, 0)
            low_rows(0, 1)
            with dve.Fori(0, E // NBUF - 1) as ep:
                for i in range(NBUF):
                    low_weights(ep, i + 2)
                    up_gate(ep, i + 1)
                    low_rows(ep, i + 2)
                    weigh(ep, i)
            for i in range(NBUF):
                if i + 2 < NBUF:
                    low_weights(E // NBUF - 1, i + 2)
                if i + 1 < NBUF:
                    up_gate(E // NBUF - 1, i + 1)
                if i + 2 < NBUF:
                    low_rows(E // NBUF - 1, i + 2)
                weigh(E // NBUF - 1, i)

        @block.gpsimd
        def _(pool):
            pool.memset(zeros[:], 0.0).then_inc(pool_chain, 1)
            pool.memset(mhalf[:], -0.5).then_inc(pool_chain, 1)
            pool.wait_ge(pool_chain, 2)
            pool.dma_start(out[T:YROWS, :], zeros[:]).then_inc(spare_rows_zeroed, 16)

            def rstd_of(b, n, first, count):
                pool.wait_ge(var_ready, b * RSTDS + n)
                at = slice(first, first + count)
                pool.tensor_tensor(rstd[:, at], vare[:, at], mhalf[:, at], ALU.pow).then_inc(rstd_ready, 1)

            def rstd_tiles(b, n):
                for t in range(NT):
                    rstd_of(b, 3 + (n - 3) * NT + t, t, 1)

            def attention(b, layer):
                for s in range(UNITS):
                    u = layer * UNITS + s
                    if normed.who[u] == "P":
                        pool.wait_ge(rden_ready, b * 2 * UNITS + u + 1)
                        pool.sem_inc(spare, 1)
                        normalise(pool, b, layer, s)

            rstd_of(0, 1, 0, NT)
            with pool.Fori(0, B) as b:
                rstd_of(b, 2, 0, 2 * NT)
                pool.wait_ge(kr_ready, b + 1)
                pool.sem_inc(spare, 1)
                for g in range(1, G0):
                    last = pool.tensor_copy(kT[KN:P, g, :], kT[KN:P, 0, :])
                last.then_inc(kr_copied, 1)
                attention(b, 0)
                rstd_tiles(b, 3)
                rstd_tiles(b, 4)
                dense.wait_filled(pool, b, "down", NT - 1)
                pool.wait_ge(rstd_ready, b * RSTDS + (2 + 2 * NT))
                pool.sem_inc(spare, 1)
                pool.memset(q_st[64:QK_ROWS].rearrange("p a j n -> p (a j n)").bitcast(F32), 0.0).then_inc(pool_chain, 1)
                pool.wait_ge(pool_chain, b + 3)
                pool.sem_inc(spare, 1)
                pool.memset(k_st[64:QK_ROWS].rearrange("p a j n -> p (a j n)").bitcast(F32), 0.0).then_inc(stack_zeroed, 1)
                attention(b, 1)
                rstd_tiles(b, 5)
                rstd_of(b + 1, 1, 0, NT)

            pool.wait_ge(spare_rows_zeroed, 16)
            pool.wait_ge(slots_ready, 2)

            def gather(i):
                for hf in range(2):
                    pool.indirect_dma_start(xg[:, i, hf, :], None, xn_rows,
                                            bass.IndirectOffsetOnAxis(ap=slot_now[:, i, 0, hf:hf + 1], axis=0),
                                            bounds_check=T - 1, oob_is_err=True).then_inc(e_rows[i], 16)

            def add_rows(ep, i, more):
                e = ep * NBUF + i
                pool.wait_ge(e_y, e + 3)
                pool.wait_ge(e_settled, e + NBUF)
                pool.sem_inc(spare, 1)
                at = slice(e + NBUF, e + NBUF + 1) if isinstance(e, int) else bass.ds(ep * NBUF + (NBUF + i), 1)
                kinds = slice(0 if more else 1, 2)
                pool.tensor_copy(slot_now[:, i, kinds], slots[:, at, kinds].rearrange("p o k h -> p (o k) h")).then_inc(idx_ready, 1)
                pool.wait_ge(idx_ready, e + 2)
                pool.sem_inc(spare, 1)
                for hf in range(2):
                    pool.indirect_dma_start(out,
                                            bass.IndirectOffsetOnAxis(ap=slot_now[:, i, 1, hf:hf + 1], axis=0),
                                            yo[:, i, hf, :], None, bounds_check=YROWS - 1, oob_is_err=True,
                                            compute_op=ALU.add).then_inc(e_added[i], 16)
                if more:
                    gather(i)

            pool.sem_inc(e_settled, NBUF)
            pool.tensor_copy(slot_now[:, :, 0, :], slots[:, 0:NBUF, 0, :]).then_inc(idx_ready, 1)
            pool.wait_ge(idx_ready, 1)
            for i in range(NBUF):
                gather(i)
            with pool.Fori(0, E // NBUF - 1) as ep:
                for i in range(NBUF):
                    add_rows(ep, i, True)
            for i in range(NBUF):
                add_rows(E // NBUF - 1, i, False)
            for done in e_added:
                pool.wait_ge(done, 32 * E // NBUF)


def kernel(**inputs):
    import ml_dtypes
    import numpy as np
    from concourse import bacc
    from concourse.bass_utils import run_bass_kernel_spmd

    i = {k: np.asarray(v) for k, v in inputs.items()}
    f = np.float32
    w_dkv = i["L0_attn_w_dkv"]
    w_ukv = i["L0_attn_w_ukv"]

    def planes(w):
        return w.reshape(w.shape[0], FF // 4, 4).transpose(0, 2, 1).reshape(w.shape[0], FF)

    def pad_heads(w):
        o = np.zeros((H1, 32) + w.shape[1:], w.dtype)
        o[:, :HD1] = w.reshape((H1, HD1) + w.shape[1:])
        return o.reshape((H1 * 32,) + w.shape[1:])

    def rope(dim, rows):
        inv = (1.0 / f(10000.0) ** (np.arange(0, dim, 2, dtype=f) / f(dim))).astype(f)
        ang = np.arange(S, dtype=f)[:, None] * inv
        c = np.repeat(np.cos(ang).astype(f).T, 2, axis=0), np.repeat(np.sin(ang).astype(f).T, 2, axis=0)
        return [np.tile(a, (rows // dim, 1)) for a in c]

    cos_q, sin_q = (a * f((QN + QR) ** -0.5) for a in rope(QR, P))
    cos_k, sin_k = rope(KR, P)
    bf = ml_dtypes.bfloat16
    r, c = np.arange(P)[:, None], np.arange(S)[None, :]
    small = np.zeros((P, SMALL), f)
    small[:, 0:32] = np.arange(32)
    small[:, 32:48] = np.arange(16)
    small[:, 48:64] = DUMMY + (r % 8) * 16 + np.arange(16)
    small[:, 64:72] = (r // 16 == np.arange(8))
    small[:, 72:80] = (r % 8 == np.arange(8))
    small[:, 80] = np.arange(P)
    small[:, 96:112] = (r // 8 == np.arange(16))
    arrays = {
        "x": np.concatenate([i["L0_attn_x"], i["L0_attn_x"][:1]]).reshape(T + S, D),
        "w_proj": np.concatenate([i["L0_attn_w_dq"], w_dkv[:, :CQ]], axis=1),
        "w_kr": np.concatenate([np.zeros((D, KN), f), w_dkv[:, CQ:]], axis=1),
        "gamma_q": i["L0_attn_gamma_q"].reshape(CQ, 1), "gamma_kv": i["L0_attn_gamma_kv"].reshape(CQ, 1),
        "w_qn": i["L0_attn_w_uq"][:, :H0 * QN], "w_qr": i["L0_attn_w_uq"][:, H0 * QN:],
        "w_uk": w_ukv[:, :G0 * KN], "w_uv": w_ukv[:, G0 * KN:], "w_o0": i["L0_attn_w_o"],
        "w_gate": planes(i["L0_ffn_w_gate"]), "w_up": planes(i["L0_ffn_w_up"]), "w_down": planes(i["L0_ffn_w_down"].T).T,
        "w_q1": i["L1_attn_Wq"].T, "w_k1": i["L1_attn_Wk"].T,
        "w_v1": pad_heads(i["L1_attn_Wv"]).T, "w_o1": pad_heads(i["L1_attn_Wo"].T),
        "b_q1": i["L1_attn_bq"].reshape(KD, P).T, "b_k1": i["L1_attn_bk"].reshape(KD, P).T,
        "b_v1": pad_heads(i["L1_attn_bv"]).reshape(1, 512), "b_o1": i["L1_attn_bo"].reshape(1, D),
        "gate_w": i["L1_ffn_gate_w"].T, "w1": i["L1_ffn_w1"], "w2": i["L1_ffn_w2"], "w3": i["L1_ffn_w3"],
        "sw1": i["L1_ffn_sw1"], "sw2": i["L1_ffn_sw2"], "sw3": i["L1_ffn_sw3"],
        "cos_q": cos_q, "sin_q": sin_q, "cos_k": cos_k, "sin_k": sin_k,
        "ident": np.eye(P, dtype=f), "identb": np.eye(P, dtype=f).astype(bf),
        "causal": np.where(c[:, :P] > r, f(-1e30), f(0)).astype(bf),
        "window": np.where(c[:, :WCOLS] < r + P - WINDOW - SINKS, f(-1e30), f(0)).astype(bf),
        "tri": (r < c[:, :P]).astype(bf), "small": small,
    }
    nc = bacc.Bacc("TRN2", target_bir_lowering=False, num_devices=1)
    args, ins = {}, {}
    for name, a in arrays.items():
        a = np.ascontiguousarray(a)
        ins[f"in_{name}"] = a
        args[name] = nc.dram_tensor(f"in_{name}", a.shape, mybir.dt.from_np(a.dtype), kind="ExternalInput").ap()
    args["out"] = nc.dram_tensor("out_0", (YROWS, D), F32, kind="ExternalOutput").ap()
    build(nc, **args)
    res = run_bass_kernel_spmd(nc, [ins], core_ids=[0])
    return res.results[0]["out_0"][:T].reshape(B, S, D)
```
